# Optimizing a Trainium2 kernel written in Bass

```python
import numpy as np
import jax
import jax.numpy as jnp

def _softmax(x, axis=-1):
    return jax.nn.softmax(x, axis=axis)

def _gelu(x):
    return jax.nn.gelu(x, approximate=True)

def _silu(x):
    return jax.nn.silu(x)

def _sigmoid(x):
    return jax.nn.sigmoid(x)

def _layernorm(x, axis=-1, eps=1e-05):
    m = jnp.mean(x, axis=axis, keepdims=True)
    v = jnp.var(x, axis=axis, keepdims=True)
    return (x - m) / jnp.sqrt(v + eps)

def _scatter_add(tgt, idx, src, axis=0):
    return tgt.at[idx].add(src)

def _segment_sum(src, seg, n):
    return jax.ops.segment_sum(src, seg, n)
kernel_name = 'mk_adaln_d2_jaxref_r8_c1f089'

def setup_inputs(seed: int=0):
    np.random.seed(seed)
    _w = jnp.asarray

    def _L0_attn_setup():
        import jax, jax.numpy as jnp
        import numpy as np
        import math
        NUM_BUCKETS = 32
        MAX_DISTANCE = 128
        HEADS = 16
        D_MODEL = 128

        def _relative_position_bucket(rel_pos, num_buckets=NUM_BUCKETS, max_distance=MAX_DISTANCE):
            n = jnp.maximum(-rel_pos, 0)
            max_exact = num_buckets // 2
            is_small = n < max_exact
            val_large = max_exact + (jnp.log(jnp.maximum(n, 1).astype(jnp.float32) / max_exact) / math.log(max_distance / max_exact) * (num_buckets - max_exact)).astype(jnp.int32)
            val_large = jnp.minimum(val_large, num_buckets - 1)
            return jnp.where(is_small, n, val_large)
        key = jax.random.key(seed)
        ks = jax.random.split(key, 7)
        d = D_MODEL
        s = 1.0 / math.sqrt(d)
        x = jax.random.normal(ks[0], (2, 256, d), dtype=jnp.float32)
        Wq = jax.random.normal(ks[1], (d, d), dtype=jnp.float32) * s
        Wk = jax.random.normal(ks[2], (d, d), dtype=jnp.float32) * s
        Wv = jax.random.normal(ks[3], (d, d), dtype=jnp.float32) * s
        Wo = jax.random.normal(ks[4], (d, d), dtype=jnp.float32) * s
        bo = jnp.zeros((d,), dtype=jnp.float32)
        rel_emb = jax.random.normal(ks[5], (NUM_BUCKETS, HEADS), dtype=jnp.float32) * 0.02
        return {'x': x, 'Wq': Wq, 'Wk': Wk, 'Wv': Wv, 'Wo': Wo, 'bo': bo, 'rel_emb': rel_emb}
    _L0_attn_in = _L0_attn_setup()

    def _L0_ffn_setup():
        import jax, jax.numpy as jnp
        import numpy as np
        DIM = 128
        HID = 256
        E = 8
        K = 2
        R = 16
        B_, S_ = (2, 128)

        def _lora_in(xf, W, b, A, B):
            base = jnp.einsum('td,ehd->teh', xf, W)
            low = jnp.einsum('ter,ehr->teh', jnp.einsum('td,erd->ter', xf, A), B)
            return base + low + b

        def _lora_out(g, W, b, A, B):
            base = jnp.einsum('teh,edh->ted', g, W)
            low = jnp.einsum('ter,edr->ted', jnp.einsum('teh,erh->ter', g, A), B)
            return base + low + b
        key = jax.random.key(seed)
        ks = jax.random.split(key, 14)
        n = lambda k, shape, scale: jax.random.normal(k, shape, jnp.float32) * scale
        inp = {'x': jax.random.normal(ks[0], (B_, S_, DIM), jnp.float32), 'Wg': n(ks[1], (E, DIM), DIM ** (-0.5)), 'W1': n(ks[2], (E, HID, DIM), DIM ** (-0.5)), 'b1': jnp.zeros((E, HID), jnp.float32), 'A1': n(ks[3], (E, R, DIM), DIM ** (-0.5)), 'B1': n(ks[4], (E, HID, R), 0.01), 'W2': n(ks[5], (E, DIM, HID), HID ** (-0.5)), 'b2': jnp.zeros((E, DIM), jnp.float32), 'A2': n(ks[6], (E, R, HID), HID ** (-0.5)), 'B2': n(ks[7], (E, DIM, R), 0.01), 'W3': n(ks[8], (E, HID, DIM), DIM ** (-0.5)), 'b3': jnp.zeros((E, HID), jnp.float32), 'A3': n(ks[9], (E, R, DIM), DIM ** (-0.5)), 'B3': n(ks[10], (E, HID, R), 0.01)}
        return inp
    _L0_ffn_in = _L0_ffn_setup()
    _L0_c = _w((lambda *s: np.random.randn(*s).astype(np.float32) * 0.05)(4, 128))
    _L0_wmod = _w((lambda *s: np.random.randn(*s).astype(np.float32) * 0.05)(128, 6 * 128) * 128 ** (-0.5))

    def _L1_attn_setup():
        import jax, jax.numpy as jnp
        import numpy as np
        HEADS = 16
        HEAD_DIM = 64
        EMB = 128
        B, S = (4, 256)
        SCALE = 1.0 / 8.0
        MASK_PENALTY = -50.0
        key = jax.random.key(seed)
        ks = jax.random.split(key, 5)
        x = jax.random.normal(ks[0], (B, S, EMB), dtype=jnp.float32)
        Wq = jax.random.normal(ks[1], (EMB, HEADS * HEAD_DIM), dtype=jnp.float32) * 0.02
        Wk = jax.random.normal(ks[2], (EMB, HEADS * HEAD_DIM), dtype=jnp.float32) * 0.02
        Wv = jax.random.normal(ks[3], (EMB, HEADS * HEAD_DIM), dtype=jnp.float32) * 0.02
        Wr = jax.random.normal(ks[4], (HEADS * HEAD_DIM, EMB), dtype=jnp.float32) * 0.02
        return {'x': x, 'Wq': Wq, 'Wk': Wk, 'Wv': Wv, 'Wr': Wr}
    _L1_attn_in = _L1_attn_setup()

    def _L1_ffn_setup():
        import jax, jax.numpy as jnp
        import numpy as np
        DIM = 128
        DEPTH = 2
        HEADS = 8
        DIM_HEAD = 64
        WINDOW = 64
        INNER = HEADS * DIM_HEAD
        HID = int(DIM * 4 * 2 / 3)
        B, N = (2, 1024)
        QK_SCALE = 8.0

        def shift_token(t):
            t1, t2 = jnp.split(t, 2, axis=-1)
            t2 = jnp.pad(t2, ((0, 0), (1, 0), (0, 0)))[:, :-1]
            return jnp.concatenate([t1, t2], axis=-1)

        def l2norm(t):
            return t / jnp.clip(jnp.linalg.norm(t, axis=-1, keepdims=True), 1e-12)

        def rotate_half(x):
            x1, x2 = jnp.split(x, 2, axis=-1)
            return jnp.concatenate([-x2, x1], axis=-1)

        def rotary_xpos(q, k):
            n = q.shape[-2]
            half_idx = jnp.arange(0, DIM_HEAD, 2, dtype=jnp.float32)
            inv_freq = 1.0 / 10000.0 ** (half_idx / DIM_HEAD)
            t = jnp.arange(n, dtype=jnp.float32)
            freqs = t[:, None] * inv_freq[None, :]
            freqs = jnp.concatenate([freqs, freqs], axis=-1)
            base = (half_idx + 0.4 * DIM_HEAD) / (1.4 * DIM_HEAD)
            power = (t - n // 2) / float(WINDOW // 2)
            scale = base[None, :] ** power[:, None]
            scale = jnp.concatenate([scale, scale], axis=-1)
            cos, sin = (jnp.cos(freqs), jnp.sin(freqs))
            q = q * cos * scale + rotate_half(q) * sin * scale
            k = k * cos / scale + rotate_half(k) * sin / scale
            return (q, k)

        def local_attention(q, k, v):
            b, h, n, d = q.shape
            w = n // WINDOW
            bq = q.reshape(b, h, w, WINDOW, d) * QK_SCALE
            bk = k.reshape(b, h, w, WINDOW, d)
            bv = v.reshape(b, h, w, WINDOW, d)

            def look_around(t):
                p = jnp.pad(t, ((0, 0), (0, 0), (1, 0), (0, 0), (0, 0)))
                return jnp.concatenate([p[:, :, :w], p[:, :, 1:]], axis=3)
            bk, bv = (look_around(bk), look_around(bv))
            bt = jnp.arange(n).reshape(w, WINDOW)
            btp = jnp.pad(bt, ((1, 0), (0, 0)), constant_values=-1)
            btk = jnp.concatenate([btp[:w], btp[1:]], axis=1)
            sim = jnp.einsum('bhwid,bhwjd->bhwij', bq, bk)
            i = bt[:, :, None]
            j = btk[:, None, :]
            mask = (i < j) | (i > j + WINDOW) | (j == -1)
            sim = jnp.where(mask, -jnp.finfo(sim.dtype).max, sim)
            attn = jax.nn.softmax(sim, axis=-1)
            out = jnp.einsum('bhwij,bhwjd->bhwid', attn, bv)
            return out.reshape(b, h, n, d)

        def _layer(x, wqkv, qs, ksc, wo, lg, lb, w1, b1, w2, b2):
            b, n, _ = x.shape
            h = shift_token(x)
            qkv = h @ wqkv
            q, k, v = jnp.split(qkv, 3, axis=-1)
            to_heads = lambda t: t.reshape(b, n, HEADS, DIM_HEAD).transpose(0, 2, 1, 3)
            q, k, v = (to_heads(q), to_heads(k), to_heads(v))
            q = l2norm(q) * qs
            k = l2norm(k) * ksc
            q, k = rotary_xpos(q, k)
            o = local_attention(q, k, v)
            o = o.transpose(0, 2, 1, 3).reshape(b, n, INNER)
            x = x + o @ wo
            h = shift_token(x)
            mu = h.mean(-1, keepdims=True)
            var = h.var(-1, keepdims=True)
            h = (h - mu) / jnp.sqrt(var + 1e-05) * lg + lb
            h = h @ w1 + b1
            a, g = jnp.split(h, 2, axis=-1)
            h = a * jax.nn.gelu(g, approximate=False)
            x = x + h @ w2 + b2
            return x
        key = jax.random.key(seed)
        ks = jax.random.split(key, 6)
        return {'x': jax.random.normal(ks[0], (B, N, DIM), jnp.float32), 'wqkv': jax.random.normal(ks[1], (DEPTH, DIM, 3 * INNER), jnp.float32) * 0.02, 'q_scale': jnp.ones((DEPTH, DIM_HEAD), jnp.float32), 'k_scale': jnp.ones((DEPTH, DIM_HEAD), jnp.float32), 'wo': jax.random.normal(ks[2], (DEPTH, INNER, DIM), jnp.float32) * 0.02, 'ln_g': jnp.ones((DEPTH, DIM), jnp.float32), 'ln_b': jnp.zeros((DEPTH, DIM), jnp.float32), 'w1': jax.random.normal(ks[3], (DEPTH, DIM, 2 * HID), jnp.float32) * 0.02, 'b1': jnp.zeros((DEPTH, 2 * HID), jnp.float32), 'w2': jax.random.normal(ks[4], (DEPTH, HID, DIM), jnp.float32) * 0.02, 'b2': jnp.zeros((DEPTH, DIM), jnp.float32)}
    _L1_ffn_in = _L1_ffn_setup()
    _L1_c = _w((lambda *s: np.random.randn(*s).astype(np.float32) * 0.05)(4, 128))
    _L1_wmod = _w((lambda *s: np.random.randn(*s).astype(np.float32) * 0.05)(128, 6 * 128) * 128 ** (-0.5))
    _d = {'L0_attn_x': _L0_attn_in['x'], 'L0_attn_Wq': _L0_attn_in['Wq'], 'L0_attn_Wk': _L0_attn_in['Wk'], 'L0_attn_Wv': _L0_attn_in['Wv'], 'L0_attn_Wo': _L0_attn_in['Wo'], 'L0_attn_bo': _L0_attn_in['bo'], 'L0_attn_rel_emb': _L0_attn_in['rel_emb'], 'L0_ffn_Wg': _L0_ffn_in['Wg'], 'L0_ffn_W1': _L0_ffn_in['W1'], 'L0_ffn_b1': _L0_ffn_in['b1'], 'L0_ffn_A1': _L0_ffn_in['A1'], 'L0_ffn_B1': _L0_ffn_in['B1'], 'L0_ffn_W2': _L0_ffn_in['W2'], 'L0_ffn_b2': _L0_ffn_in['b2'], 'L0_ffn_A2': _L0_ffn_in['A2'], 'L0_ffn_B2': _L0_ffn_in['B2'], 'L0_ffn_W3': _L0_ffn_in['W3'], 'L0_ffn_b3': _L0_ffn_in['b3'], 'L0_ffn_A3': _L0_ffn_in['A3'], 'L0_ffn_B3': _L0_ffn_in['B3'], 'L0_c': _L0_c, 'L0_wmod': _L0_wmod, 'L1_attn_Wq': _L1_attn_in['Wq'], 'L1_attn_Wk': _L1_attn_in['Wk'], 'L1_attn_Wv': _L1_attn_in['Wv'], 'L1_attn_Wr': _L1_attn_in['Wr'], 'L1_ffn_wqkv': _L1_ffn_in['wqkv'], 'L1_ffn_q_scale': _L1_ffn_in['q_scale'], 'L1_ffn_k_scale': _L1_ffn_in['k_scale'], 'L1_ffn_wo': _L1_ffn_in['wo'], 'L1_ffn_ln_g': _L1_ffn_in['ln_g'], 'L1_ffn_ln_b': _L1_ffn_in['ln_b'], 'L1_ffn_w1': _L1_ffn_in['w1'], 'L1_ffn_b1': _L1_ffn_in['b1'], 'L1_ffn_w2': _L1_ffn_in['w2'], 'L1_ffn_b2': _L1_ffn_in['b2'], 'L1_c': _L1_c, 'L1_wmod': _L1_wmod}
    _x0 = _d['L0_attn_x']
    _d['L0_attn_x'] = jax.random.normal(jax.random.fold_in(jax.random.key(seed), 1), (4, 1024, 128), dtype=_x0.dtype)
    del _x0
    return _d

def reference(L0_attn_x, L0_attn_Wq, L0_attn_Wk, L0_attn_Wv, L0_attn_Wo, L0_attn_bo, L0_attn_rel_emb, L0_ffn_Wg, L0_ffn_W1, L0_ffn_b1, L0_ffn_A1, L0_ffn_B1, L0_ffn_W2, L0_ffn_b2, L0_ffn_A2, L0_ffn_B2, L0_ffn_W3, L0_ffn_b3, L0_ffn_A3, L0_ffn_B3, L0_c, L0_wmod, L1_attn_Wq, L1_attn_Wk, L1_attn_Wv, L1_attn_Wr, L1_ffn_wqkv, L1_ffn_q_scale, L1_ffn_k_scale, L1_ffn_wo, L1_ffn_ln_g, L1_ffn_ln_b, L1_ffn_w1, L1_ffn_b1, L1_ffn_w2, L1_ffn_b2, L1_c, L1_wmod):

    def _L0_attn_ref(x, Wq, Wk, Wv, Wo, bo, rel_emb):
        import jax, jax.numpy as jnp
        import numpy as np
        import math
        NUM_BUCKETS = 32
        MAX_DISTANCE = 128
        HEADS = 16
        D_MODEL = 128

        def _relative_position_bucket(rel_pos, num_buckets=NUM_BUCKETS, max_distance=MAX_DISTANCE):
            n = jnp.maximum(-rel_pos, 0)
            max_exact = num_buckets // 2
            is_small = n < max_exact
            val_large = max_exact + (jnp.log(jnp.maximum(n, 1).astype(jnp.float32) / max_exact) / math.log(max_distance / max_exact) * (num_buckets - max_exact)).astype(jnp.int32)
            val_large = jnp.minimum(val_large, num_buckets - 1)
            return jnp.where(is_small, n, val_large)
        b, n, d = x.shape
        h = HEADS
        dh = d // h
        scale = dh ** (-0.5)
        q = (x @ Wq).reshape(b, n, h, dh).transpose(0, 2, 1, 3)
        k = (x @ Wk).reshape(b, n, h, dh).transpose(0, 2, 1, 3)
        v = (x @ Wv).reshape(b, n, h, dh).transpose(0, 2, 1, 3)
        sim = jnp.einsum('bhid,bhjd->bhij', q, k) * scale
        pos = jnp.arange(n, dtype=jnp.int32)
        rel_pos = pos[None, :] - pos[:, None]
        buckets = _relative_position_bucket(rel_pos)
        bias = rel_emb[buckets]
        sim = sim + jnp.transpose(bias, (2, 0, 1))[None]
        mask_value = -jnp.finfo(sim.dtype).max
        causal_mask = jnp.triu(jnp.ones((n, n), dtype=bool), k=1)
        sim = jnp.where(causal_mask[None, None], mask_value, sim)
        attn = jax.nn.softmax(sim, axis=-1)
        out = jnp.einsum('bhij,bhjd->bhid', attn, v)
        out = out.transpose(0, 2, 1, 3).reshape(b, n, d)
        return out @ Wo + bo

    def _L0_ffn_ref(x, Wg, W1, b1, A1, B1, W2, b2, A2, B2, W3, b3, A3, B3):
        import jax, jax.numpy as jnp
        import numpy as np
        DIM = 128
        HID = 256
        E = 8
        K = 2
        R = 16
        B_, S_ = (2, 128)

        def _lora_in(xf, W, b, A, B):
            base = jnp.einsum('td,ehd->teh', xf, W)
            low = jnp.einsum('ter,ehr->teh', jnp.einsum('td,erd->ter', xf, A), B)
            return base + low + b

        def _lora_out(g, W, b, A, B):
            base = jnp.einsum('teh,edh->ted', g, W)
            low = jnp.einsum('ter,edr->ted', jnp.einsum('teh,erh->ter', g, A), B)
            return base + low + b
        orig_shape = x.shape
        xf = x.reshape(-1, x.shape[-1])
        scores = jax.nn.softmax(xf @ Wg.T, axis=-1)
        expert_weights, expert_indices = jax.lax.top_k(scores, K)
        expert_weights = expert_weights / expert_weights.sum(-1, keepdims=True)
        gates = (jax.nn.one_hot(expert_indices, E, dtype=xf.dtype) * expert_weights[..., None]).sum(axis=1)
        h1 = _lora_in(xf, W1, b1, A1, B1)
        h3 = _lora_in(xf, W3, b3, A3, B3)
        g = jax.nn.silu(h1) * h3
        y_e = _lora_out(g, W2, b2, A2, B2)
        y = jnp.einsum('te,ted->td', gates, y_e)
        return y.reshape(orig_shape)

    def _L1_attn_ref(x, Wq, Wk, Wv, Wr):
        import jax, jax.numpy as jnp
        import numpy as np
        HEADS = 16
        HEAD_DIM = 64
        EMB = 128
        B, S = (4, 256)
        SCALE = 1.0 / 8.0
        MASK_PENALTY = -50.0
        b, s, _ = x.shape
        q = (x @ Wq).reshape(b, s, HEADS, HEAD_DIM)
        k = (x @ Wk).reshape(b, s, HEADS, HEAD_DIM)
        v = (x @ Wv).reshape(b, s, HEADS, HEAD_DIM)
        scores = SCALE * jnp.einsum('bqhd,bkhd->bhqk', q, k)
        causal = jnp.triu(jnp.ones((s, s), dtype=x.dtype), k=1)
        scores = scores + MASK_PENALTY * causal
        attn = jax.nn.softmax(scores, axis=-1)
        out = jnp.einsum('bhqk,bkhd->bqhd', attn, v).reshape(b, s, HEADS * HEAD_DIM)
        return out @ Wr

    def _L1_ffn_ref(x, wqkv, q_scale, k_scale, wo, ln_g, ln_b, w1, b1, w2, b2):
        import jax, jax.numpy as jnp
        import numpy as np
        DIM = 128
        DEPTH = 2
        HEADS = 8
        DIM_HEAD = 64
        WINDOW = 64
        INNER = HEADS * DIM_HEAD
        HID = int(DIM * 4 * 2 / 3)
        B, N = (2, 1024)
        QK_SCALE = 8.0

        def shift_token(t):
            t1, t2 = jnp.split(t, 2, axis=-1)
            t2 = jnp.pad(t2, ((0, 0), (1, 0), (0, 0)))[:, :-1]
            return jnp.concatenate([t1, t2], axis=-1)

        def l2norm(t):
            return t / jnp.clip(jnp.linalg.norm(t, axis=-1, keepdims=True), 1e-12)

        def rotate_half(x):
            x1, x2 = jnp.split(x, 2, axis=-1)
            return jnp.concatenate([-x2, x1], axis=-1)

        def rotary_xpos(q, k):
            n = q.shape[-2]
            half_idx = jnp.arange(0, DIM_HEAD, 2, dtype=jnp.float32)
            inv_freq = 1.0 / 10000.0 ** (half_idx / DIM_HEAD)
            t = jnp.arange(n, dtype=jnp.float32)
            freqs = t[:, None] * inv_freq[None, :]
            freqs = jnp.concatenate([freqs, freqs], axis=-1)
            base = (half_idx + 0.4 * DIM_HEAD) / (1.4 * DIM_HEAD)
            power = (t - n // 2) / float(WINDOW // 2)
            scale = base[None, :] ** power[:, None]
            scale = jnp.concatenate([scale, scale], axis=-1)
            cos, sin = (jnp.cos(freqs), jnp.sin(freqs))
            q = q * cos * scale + rotate_half(q) * sin * scale
            k = k * cos / scale + rotate_half(k) * sin / scale
            return (q, k)

        def local_attention(q, k, v):
            b, h, n, d = q.shape
            w = n // WINDOW
            bq = q.reshape(b, h, w, WINDOW, d) * QK_SCALE
            bk = k.reshape(b, h, w, WINDOW, d)
            bv = v.reshape(b, h, w, WINDOW, d)

            def look_around(t):
                p = jnp.pad(t, ((0, 0), (0, 0), (1, 0), (0, 0), (0, 0)))
                return jnp.concatenate([p[:, :, :w], p[:, :, 1:]], axis=3)
            bk, bv = (look_around(bk), look_around(bv))
            bt = jnp.arange(n).reshape(w, WINDOW)
            btp = jnp.pad(bt, ((1, 0), (0, 0)), constant_values=-1)
            btk = jnp.concatenate([btp[:w], btp[1:]], axis=1)
            sim = jnp.einsum('bhwid,bhwjd->bhwij', bq, bk)
            i = bt[:, :, None]
            j = btk[:, None, :]
            mask = (i < j) | (i > j + WINDOW) | (j == -1)
            sim = jnp.where(mask, -jnp.finfo(sim.dtype).max, sim)
            attn = jax.nn.softmax(sim, axis=-1)
            out = jnp.einsum('bhwij,bhwjd->bhwid', attn, bv)
            return out.reshape(b, h, n, d)

        def _layer(x, wqkv, qs, ksc, wo, lg, lb, w1, b1, w2, b2):
            b, n, _ = x.shape
            h = shift_token(x)
            qkv = h @ wqkv
            q, k, v = jnp.split(qkv, 3, axis=-1)
            to_heads = lambda t: t.reshape(b, n, HEADS, DIM_HEAD).transpose(0, 2, 1, 3)
            q, k, v = (to_heads(q), to_heads(k), to_heads(v))
            q = l2norm(q) * qs
            k = l2norm(k) * ksc
            q, k = rotary_xpos(q, k)
            o = local_attention(q, k, v)
            o = o.transpose(0, 2, 1, 3).reshape(b, n, INNER)
            x = x + o @ wo
            h = shift_token(x)
            mu = h.mean(-1, keepdims=True)
            var = h.var(-1, keepdims=True)
            h = (h - mu) / jnp.sqrt(var + 1e-05) * lg + lb
            h = h @ w1 + b1
            a, g = jnp.split(h, 2, axis=-1)
            h = a * jax.nn.gelu(g, approximate=False)
            x = x + h @ w2 + b2
            return x
        for l in range(DEPTH):
            x = _layer(x, wqkv[l], q_scale[l], k_scale[l], wo[l], ln_g[l], ln_b[l], w1[l], b1[l], w2[l], b2[l])
        return x
    x = L0_attn_x
    mod = (_silu(L0_c) @ L0_wmod).reshape(L0_c.shape[0], 6, 1, -1)
    sa, ca, ga, sb, cb, gb = (mod[:, 0], mod[:, 1], mod[:, 2], mod[:, 3], mod[:, 4], mod[:, 5])
    ga = (2 * (ga >= 0) - 1) * jnp.maximum(jnp.abs(ga), 0.25)
    gb = (2 * (gb >= 0) - 1) * jnp.maximum(jnp.abs(gb), 0.25)
    h = _layernorm(x, axis=-1) * (1 + ca) + sa
    x = x + ga * _L0_attn_ref(h, L0_attn_Wq, L0_attn_Wk, L0_attn_Wv, L0_attn_Wo, L0_attn_bo, L0_attn_rel_emb)
    h = _layernorm(x, axis=-1) * (1 + cb) + sb
    x = x + gb * _L0_ffn_ref(h, L0_ffn_Wg, L0_ffn_W1, L0_ffn_b1, L0_ffn_A1, L0_ffn_B1, L0_ffn_W2, L0_ffn_b2, L0_ffn_A2, L0_ffn_B2, L0_ffn_W3, L0_ffn_b3, L0_ffn_A3, L0_ffn_B3)
    mod = (_silu(L1_c) @ L1_wmod).reshape(L1_c.shape[0], 6, 1, -1)
    sa, ca, ga, sb, cb, gb = (mod[:, 0], mod[:, 1], mod[:, 2], mod[:, 3], mod[:, 4], mod[:, 5])
    ga = (2 * (ga >= 0) - 1) * jnp.maximum(jnp.abs(ga), 0.25)
    gb = (2 * (gb >= 0) - 1) * jnp.maximum(jnp.abs(gb), 0.25)
    h = _layernorm(x, axis=-1) * (1 + ca) + sa
    x = x + ga * _L1_attn_ref(h, L1_attn_Wq, L1_attn_Wk, L1_attn_Wv, L1_attn_Wr)
    h = _layernorm(x, axis=-1) * (1 + cb) + sb
    x = x + gb * _L1_ffn_ref(h, L1_ffn_wqkv, L1_ffn_q_scale, L1_ffn_k_scale, L1_ffn_wo, L1_ffn_ln_g, L1_ffn_ln_b, L1_ffn_w1, L1_ffn_b1, L1_ffn_w2, L1_ffn_b2)
    return x

_drawn_inputs = setup_inputs


def setup_inputs(seed=0):
    import zlib

    import numpy as np

    out = dict(_drawn_inputs(seed))
    spreads = {'L0_attn_bo': (0.0, 0.285),
     'L0_ffn_b1': (0.0, 0.693),
     'L0_ffn_b2': (0.0, 0.443),
     'L0_ffn_b3': (0.0, 0.728),
     'L1_ffn_q_scale': (1.0, 0.6),
     'L1_ffn_k_scale': (1.0, 0.6),
     'L1_ffn_ln_g': (1.0, 0.6),
     'L1_ffn_ln_b': (0.0, 0.8),
     'L1_ffn_b1': (0.0, 0.8),
     'L1_ffn_b2': (0.0, 0.8)}
    factors = {'L0_attn_rel_emb': 8.0,
     'L0_ffn_A1': 8.0,
     'L0_ffn_B1': 8.0,
     'L0_ffn_A2': 8.0,
     'L0_ffn_B2': 8.0,
     'L0_ffn_A3': 8.0,
     'L0_ffn_B3': 8.0,
     'L1_attn_Wq': 8.0,
     'L1_attn_Wk': 8.0,
     'L1_attn_Wv': 8.0,
     'L1_attn_Wr': 8.0,
     'L1_ffn_wqkv': 7.898,
     'L1_ffn_wo': 7.926,
     'L1_ffn_w1': 8.0,
     'L1_ffn_w2': 8.0}
    for name, (base, spread) in spreads.items():
        noise = np.random.default_rng([zlib.crc32(name.encode()), seed]).standard_normal(out[name].shape)
        drawn = base * np.exp(spread * noise) if base else spread * noise
        out[name] = jnp.asarray(drawn.astype(out[name].dtype))
    for name, factor in factors.items():
        out[name] = (out[name] * factor).astype(out[name].dtype)
    return out
```

```python
import math
from contextlib import ExitStack

import numpy as np

import concourse.bass as bass
from concourse import mybir

F32 = mybir.dt.float32
F32R = mybir.dt.float32r
BF16 = mybir.dt.bfloat16
U32 = mybir.dt.uint32
ALU = mybir.AluOpType
ACT = mybir.ActivationFunctionType
AX = mybir.AxisListType.X
ds = bass.ds

P = 128
BATCH, SEQ, DIM = 4, 1024, 128
TOKENS = BATCH * SEQ
TILES = TOKENS // P
TB = SEQ // P
BANK = 512
HEADS = 16
PAIRS = BATCH * HEADS // 2
HI_BITS = 0xFFFFF000
BIG = 1e30
BUCKETS, MAX_DISTANCE = 32, 128
EXPERTS, HIDDEN, RANK = 8, 256, 16
LDEPTH, LHEADS, LDH, LWIN = 2, 8, 64, 64
INNER = LHEADS * LDH
LHID = int(DIM * 4 * 2 / 3)
EPS = 1e-5



def bias_selector():
    n = 255 - np.arange(384)
    exact = BUCKETS // 2
    pos = np.maximum(n, 1).astype(np.float32)
    large = exact + (np.log(pos / exact) / np.float32(math.log(MAX_DISTANCE / exact)) * (BUCKETS - exact)).astype(np.int32)
    bucket = np.where(n < exact, np.maximum(n, 0), np.minimum(large, BUCKETS - 1))
    sel = np.zeros((BUCKETS + 1, 384), np.float32)
    sel[bucket, np.arange(384)] = -1.0
    sel[BUCKETS - 1] += 1.0
    sel[:, n < 0] = 0.0
    sel[BUCKETS, n < 0] = BIG
    return sel


def rotary_tables():
    half = np.arange(0, LDH, 2, dtype=np.float32)
    inv = (1.0 / 10000.0 ** (half / LDH)).astype(np.float32)
    t = np.arange(SEQ, dtype=np.float32)
    f = (t[:, None] * inv[None, :]).astype(np.float32)
    f = np.concatenate([f, f], -1)
    base = ((half + 0.4 * LDH) / (1.4 * LDH)).astype(np.float32)
    power = ((t - SEQ // 2) / float(LWIN // 2)).astype(np.float32)
    s = (base[None, :] ** power[:, None]).astype(np.float32)
    s = np.concatenate([s, s], -1)
    sign = np.where(np.arange(LDH) < LDH // 2, -1.0, 1.0).astype(np.float32)
    c, n = np.cos(f), np.sin(f) * sign
    return np.stack([c * s, n * s, c / s, n / s]).astype(np.float32)


def band_mask():
    d = np.arange(P)[:, None] + P - np.arange(2 * P)[None, :]
    return np.where((d >= 0) & (d <= LWIN), 0.0, BIG).astype(np.float32)


class Chip:
    pass


def allocate(nc, ctx, g):
    def sb(name, shape, dt=F32):
        return ctx.enter_context(nc.sbuf_tensor(name, shape, dt))

    g.x = sb("x", [P, TILES, DIM])
    g.hT = sb("hT", [P, TOKENS])
    g.ident = sb("ident", [P, P])
    g.mod_cols = sb("mod_cols", [P, 2, 6, BATCH])
    g.gate_rows = sb("gate_rows", [P, 2, 2, BATCH, DIM])
    g.ps = ctx.enter_context(nc.psum_tensor("ps", [P, 8, BANK], F32))


def kept(nc, stage_sems, name):
    stage_sems.append(nc.alloc_semaphore(name))
    return stage_sems[-1]


def give_back(nc, stage_sems):
    nc.clear_and_free_semaphores(stage_sems)
    nc.all_engine_barrier()


def setup(nc, g):
    stage_sems = []
    with ExitStack() as ctx:
        ctx.callback(give_back, nc, stage_sems)

        def sb(name, shape, dt=F32):
            return ctx.enter_context(nc.sbuf_tensor(name, shape, dt))

        def sem(name):
            return kept(nc, stage_sems, name)

        cT = sb("cT", [P, 2, BATCH])
        silu_c = sb("silu_c", [P, 2, BATCH])
        silu_wide = sb("silu_wide", [P, 2, BATCH, P])
        wmod = sb("wmod", [P, 2, 6 * DIM])
        gabs = sb("gabs", [P, 2 * BATCH * DIM])
        gsgn = sb("gsgn", [P, 2 * BATCH * DIM])
        raw = sb("raw", [P, 2 * BATCH * DIM])
        rel = sb("rel", [BUCKETS + 1, HEADS])
        sel = sb("sel", [BUCKETS + 1, 384])
        bias_sb = sb("bias_sb", [HEADS, 384])
        bo_row = sb("bo_row", [P, DIM])
        mirrored = sb("mirrored", [P, HEADS, 2 * P])
        mirrored_in, flip_mm, flip_out = sem("set_mirrored_in"), sem("set_flip_mm"), sem("set_flip_out")
        flip = sb("flip", [P, P])
        FLIPS = HEADS * 2 * P // BANK
        loaded, bias_loaded, rel_one, silu_done, wide, mod_mm, mod_out, bias_out, stored, step = map(sem, (
            "set_loaded", "set_bias_loaded", "set_rel_one", "set_silu", "set_wide", "set_mod_mm",
            "set_mod_out", "set_bias_out", "set_stored", "set_step"))
        with nc.Block() as block:
            @block.sync
            def _(sp):
                sp.dma_start(cT[:], g.cT).then_inc(loaded, 16)
                sp.dma_start(wmod[:], g.wmod).then_inc(loaded, 16)
                sp.dma_start(g.ident[:], g.ident_in).then_inc(loaded, 16)
                sp.dma_start(flip[:], g.flip_in).then_inc(loaded, 16)
                sp.dma_start(bo_row[:], g.bo.partition_broadcast(P)).then_inc(loaded, 16)
                sp.dma_start(rel[0:BUCKETS, :], g.rel_emb).then_inc(bias_loaded, 16)
                sp.dma_start(sel[:], g.bias_sel).then_inc(bias_loaded, 16)
                for b in range(BATCH):
                    sp.dma_start(g.x[:, b * TB:(b + 1) * TB, :], g.x_in[b]).then_inc(loaded, 16)
                sp.wait_ge(bias_out, 1)
                sp.dma_start(g.bias_dram, bias_sb[:]).then_inc(stored, 16)
                sp.wait_ge(stored, 16)
                sp.dma_start(mirrored[:], g.toeplitz_src).then_inc(mirrored_in, 16)
                sp.wait_ge(loaded, 16 * 9)

            @block.gpsimd
            def _(pool):
                pool.memset(rel[BUCKETS:BUCKETS + 1, :], 1.0).then_inc(rel_one, 1)

            @block.scalar
            def _(act):
                act.wait_ge(loaded, 144)
                act.activation(silu_c[:], cT[:], ACT.Silu).then_inc(silu_done, 1)
                for n in range(FLIPS):
                    act.wait_ge(flip_mm, n + 1)
                    act.activation(g.toeplitz_all[:, 2 * n:2 * n + 2, :].rearrange("p h j -> p (h j)"), g.ps[:, 5 + n % 2, :],
                                   ACT.Copy).then_inc(flip_out, 1)

            @block.tensor
            def _(pe):
                pe.wait_ge(bias_loaded, 32)
                pe.wait_ge(rel_one, 1)
                pe.matmul(g.ps[0:HEADS, 7, 0:384], rel[:], sel[:], start=True, stop=True).then_inc(mod_mm, 1)
                pe.wait_ge(silu_done, 1)
                for l in range(2):
                    for j in range(6):
                        col = (l * 6 + j) * BATCH
                        mm = pe.matmul(g.ps[:, 0, col:col + BATCH], wmod[:, l, j * DIM:(j + 1) * DIM],
                                       silu_c[:, l, :], start=True, stop=True)
                mm.then_inc(mod_mm, 1)
                pe.wait_ge(wide, 1)
                for l in range(2):
                    for n, j in enumerate((2, 5)):
                        for b in range(BATCH):
                            mm = pe.matmul(g.ps[:, 1 + l * 2 + n, b * DIM:(b + 1) * DIM], silu_wide[:, l, b, :],
                                           wmod[:, l, j * DIM:(j + 1) * DIM], start=True, stop=True)
                mm.then_inc(mod_mm, 1)
                pe.wait_ge(mirrored_in, 16)
                for n in range(FLIPS):
                    if n >= 2:
                        pe.wait_ge(flip_out, n - 1)
                    pe.matmul(g.ps[:, 5 + n % 2, :], flip[:], mirrored[:, 2 * n:2 * n + 2, :].rearrange("p h j -> p (h j)"),
                              start=True, stop=True).then_inc(flip_mm, 1)

            @block.vector
            def _(dve):
                dve.wait_ge(silu_done, 1)
                dve.tensor_copy(silu_wide[:], silu_c[:].unsqueeze(3).to_broadcast([P, 2, BATCH, P])).then_inc(wide, 1)
                dve.wait_ge(mod_mm, 1)
                dve.tensor_copy(bias_sb[:], g.ps[0:HEADS, 7, 0:384]).then_inc(bias_out, 1)
                dve.wait_ge(mod_mm, 2)
                dve.tensor_copy(g.mod_cols[:].rearrange("p l j b -> p (l j b)"), g.ps[:, 0, 0:48]).then_inc(step, 1)
                dve.wait_ge(step, 1)
                for l in range(2):
                    for j in (1, 4):
                        last = dve.tensor_scalar(g.mod_cols[:, l, j, :], g.mod_cols[:, l, j, :], 1.0, None, ALU.add)
                last.then_inc(step, 1)
                dve.wait_ge(mod_mm, 3)
                for l in range(2):
                    gate = g.ps[:, 1 + l * 2:3 + l * 2, :].rearrange("p n c -> p (n c)")
                    dve.tensor_copy(raw[:], gate).then_inc(step, 1)
                    dve.wait_ge(step, 3 + 4 * l)
                    dve.scalar_tensor_tensor(gabs[:], raw[:], -1.0, raw[:], ALU.mult, ALU.max)
                    dve.tensor_scalar(gsgn[:], raw[:], 0.0, 2.0, ALU.is_ge, ALU.mult).then_inc(step, 1)
                    dve.wait_ge(step, 4 + 4 * l)
                    dve.tensor_scalar(gabs[:], gabs[:], 0.25, None, ALU.max).then_inc(step, 1)
                    dve.wait_ge(step, 5 + 4 * l)
                    dve.scalar_tensor_tensor(g.gate_rows[:, l].rearrange("p n b d -> p (n b d)"), gsgn[:], -1.0,
                                             gabs[:], ALU.add, ALU.mult).then_inc(step, 1)
                    dve.wait_ge(step, 6 + 4 * l)
                dve.wait_ge(loaded, 144)
                dve.tensor_tensor(g.ga_bo[:], g.gate_rows[:, 0, 0], bo_row[:].unsqueeze(1).to_broadcast([P, BATCH, DIM]),
                                  ALU.mult).then_inc(step, 1)


def norm_modulate(nc, g, layer, which, add_ga_bo=False, shift=False):
    tag = f"n{layer}{which}_"
    stage_sems = []
    with ExitStack() as ctx:
        ctx.callback(give_back, nc, stage_sems)

        def sem(name):
            return kept(nc, stage_sems, tag + name)

        stats = ctx.enter_context(nc.sbuf_tensor(tag + "stats", [P, TB, 6], F32))
        mv = ctx.enter_context(nc.sbuf_tensor(tag + "mv", [P, TB, 2], F32))
        std = ctx.enter_context(nc.sbuf_tensor(tag + "std", [P, TB], F32))
        rstd = ctx.enter_context(nc.sbuf_tensor(tag + "rstd", [P, TB], F32))
        xn = ctx.enter_context(nc.sbuf_tensor(tag + "xn", [P, TB, DIM], F32))
        stats_done, var_done, std_done, rstd_done, xn_done, turned, evacuated = map(sem, (
            "stats", "var", "std", "rstd", "xn", "turned", "evacuated"))
        held = sem("held")
        s_cols, c_cols = g.mod_cols[:, layer, 3 * which, :], g.mod_cols[:, layer, 3 * which + 1, :]
        with nc.Block() as block:
            @block.vector
            def _(dve):
                with dve.Fori(0, BATCH) as b:
                    for t in range(TB):
                        last = dve.bn_stats(stats[:, t, :], g.x[:, ds(b * TB + t, 1), :].rearrange("p a d -> p (a d)"))
                    last.then_inc(stats_done, 1)
                    dve.wait_ge(stats_done, b + 1)
                    settle(dve, held)
                    for t in range(TB):
                        last = dve.bn_aggr(mv[:, t, :], stats[:, t, :])
                    last.then_inc(var_done, 1)
                    dve.wait_ge(var_done, 2 * b + 1)
                    dve.tensor_scalar(std[:], mv[:, :, 1], EPS, None, ALU.add).then_inc(var_done, 1)
                    dve.wait_ge(std_done, b + 1)
                    dve.reciprocal(rstd[:], std[:]).then_inc(rstd_done, 1)
                    dve.wait_ge(rstd_done, b + 1)
                    dve.wait_ge(turned, b + 1)
                    for t in range(TB):
                        last = dve.tensor_scalar(xn[:, t, :], g.x[:, ds(b * TB + t, 1), :].rearrange("p a d -> p (a d)"),
                                                 mv[:, t, 0:1], rstd[:, t:t + 1], ALU.subtract, ALU.mult)
                    last.then_inc(xn_done, 1)
                    if add_ga_bo:
                        dve.wait_ge(xn_done, b + 1)
                        dve.tensor_tensor(g.x[:, ds(b * TB, TB), :], g.x[:, ds(b * TB, TB), :],
                                          g.ga_bo[:, ds(b, 1), :].to_broadcast([P, TB, DIM]), ALU.add)

            @block.scalar
            def _(act):
                with act.Fori(0, BATCH) as b:
                    act.wait_ge(var_done, 2 * b + 2)
                    act.activation(std[:], std[:], ACT.Sqrt).then_inc(std_done, 1)
                    act.wait_ge(turned, b + 2)
                    for half in range(2):
                        for rows in (TOP, LOW) if shift else (slice(0, P),):
                            dst = shifted(g.zA, rows, b, half * BANK, BANK) if shift else \
                                g.hT[:, ds(b * SEQ + half * BANK, BANK)]
                            last = act.activation(dst, g.ps[rows, half, :], ACT.Identity, bias=s_cols[rows, ds(b, 1)],
                                                  scale=c_cols[rows, ds(b, 1)])
                    last.then_inc(evacuated, 1)

            @block.tensor
            def _(pe):
                pe.sem_inc(turned, 1)
                pe.sem_inc(evacuated, 1)
                with pe.Fori(0, BATCH) as b:
                    pe.wait_ge(xn_done, b + 1)
                    pe.wait_ge(evacuated, b + 1)
                    for t in range(TB):
                        last = pe.transpose(g.ps[:, t // 4, t % 4 * P:(t % 4 + 1) * P], xn[:, t, :], g.ident[:])
                    last.then_inc(turned, 1)


def split_project(nc, g):
    stage_sems = []
    with ExitStack() as ctx:
        ctx.callback(give_back, nc, stage_sems)

        def sb(name, shape, dt=F32):
            return ctx.enter_context(nc.sbuf_tensor(name, shape, dt))

        def sem(name):
            return kept(nc, stage_sems, name)

        w = sb("pj_w", [P, 3, DIM])
        parts = [sb(f"pj_part{n}", [P, 2, 2, BANK], BF16) for n in range(3)]
        rest = sb("pj_rest", [P, 2, BANK])
        w_in, scaled, q_mm, part_done, v_mm, v_out = map(sem, (
            "pj_w_in", "pj_scaled", "pj_q_mm", "pj_part_done", "pj_v_mm", "pj_v_out"))
        rest_done, mid_done = sem("pj_rest_done"), sem("pj_mid_done")
        written = [sem(f"pj_written{n}") for n in range(2)]
        CHUNKS = TOKENS // BANK
        with nc.Block() as block:
            @block.sync
            def _(sp):
                sp.dma_start(w[:], g.w0_qkv).then_inc(w_in, 16)
                for c in range(CHUNKS):
                    sp.wait_ge(part_done, c + 1)
                    for part in range(3):
                        sp.dma_start(g.qk_dram[part, :, :, c * BANK:(c + 1) * BANK].rearrange("a p n -> p a n"),
                                     parts[part][:, c % 2]).then_inc(written[c % 2], 16)
                for n in range(2):
                    sp.wait_ge(written[n], 48 * CHUNKS // 2)

            @block.tensor
            def _(pe):
                pe.wait_ge(w_in, 16)
                pe.wait_ge(scaled, 1)
                for c in range(CHUNKS):
                    if c >= 2:
                        pe.wait_ge(part_done, c - 1)
                    for a in range(2):
                        mm = pe.matmul(g.ps[:, 2 * (c % 2) + a, :], w[:, a, :], g.hT[:, c * BANK:(c + 1) * BANK],
                                       start=True, stop=True)
                    mm.then_inc(q_mm, 1)
                    if c >= 2:
                        pe.wait_ge(v_out, c - 1)
                    for t in range(4):
                        tok = c * BANK + t * P
                        mm = pe.matmul(g.ps[:, 4 + c % 2, t * P:(t + 1) * P], g.hT[:, tok:tok + P], w[:, 2, :],
                                       start=True, stop=True)
                    mm.then_inc(v_mm, 1)

            @block.vector
            def _(dve):
                dve.wait_ge(w_in, 16)
                dve.tensor_scalar(w[:, 0, :], w[:, 0, :], -float(np.float32(8 ** -0.5)), None, ALU.mult).then_inc(scaled, 1)
                for c in range(CHUNKS):
                    dve.wait_ge(q_mm, c + 1)
                    both = g.ps[:, 2 * (c % 2):2 * (c % 2) + 2, :]
                    if c >= 2:
                        dve.wait_ge(written[c % 2], 48 * (c // 2))
                    dve.tensor_copy(parts[0][:, c % 2], both).then_inc(mid_done, 1)
                    dve.wait_ge(mid_done, 2 * c + 1)
                    dve.tensor_tensor(rest[:], both, parts[0][:, c % 2], ALU.subtract).then_inc(rest_done, 1)
                    dve.wait_ge(rest_done, c + 1)
                    dve.tensor_copy(parts[1][:, c % 2], rest[:]).then_inc(mid_done, 1)
                    dve.wait_ge(mid_done, 2 * c + 2)
                    dve.tensor_tensor(parts[2][:, c % 2], rest[:], parts[1][:, c % 2], ALU.subtract).then_inc(part_done, 1)

            @block.scalar
            def _(act):
                for c in range(CHUNKS):
                    act.wait_ge(v_mm, c + 1)
                    act.activation(g.v_all[:, 4 * c:4 * c + 4, :], g.ps[:, 4 + c % 2, :].rearrange("p (t d) -> p t d", t=4),
                                   ACT.Copy).then_inc(v_out, 1)


class Plan:

    JOBS = 2 * PAIRS

    def __init__(self, layer):
        self.layer = layer
        self.causal = layer == 0
        self.rows = 32 if layer == 0 else 64
        self.prep = 0 if layer == 0 else 10
        self.total = 0
        self.index = {}
        for n in range(self.prep):
            self.index["prep", 0, n] = self.total
            self.total += 1
        for J in range(self.JOBS + 2):
            for s in range(8):
                for kind, job, n in self.items(J, s):
                    self.index[kind, job, n] = self.total
                    self.total += 1

    def steps(self, J):
        return 4 * (J % 2 + 1) if self.causal else 8

    def step(self, J):
        return J // 2 * (self.steps(0) + self.steps(1)) + (J % 2) * self.steps(0)

    def width(self, J, i):
        return (4 * (J % 2) + i + 1) * P if self.causal else SEQ

    def plain(self, J, i):
        return max(0, 4 * (J % 2) + i - 1) * P if self.causal else (4 * (J % 2) + i) * P

    def plains(self, J, u=0):
        if J < 0:
            return 0
        per = [sum(self.plain(j, s // 2) > 0 for s in range(8)) for j in range(2)]
        return J // 2 * sum(per) + (J % 2) * per[0] + sum(self.plain(J, s // 2) > 0 for s in range(u))

    def first(self, J, kt):
        return max(0, kt - 4 * (J % 2)) * P if self.causal else 0

    def product(self, J, s):
        if s and s - 1 < self.steps(J - 1):
            return J - 1, s - 1
        if s == 0 and self.steps(J - 2) == 8:
            return J - 2, 7
        return None, None

    def items(self, J, s):
        out = []
        if s == 1 and self.steps(J - 2) == 8 and 0 <= J - 2 < self.JOBS:
            out.append(("y", J - 2, 0))
        if s == 5 and self.steps(J - 1) == 4 and 0 <= J - 1 < self.JOBS:
            out.append(("y", J - 1, 0))
        if s == 2 and 0 <= J - 1 < self.JOBS:
            out.append(("r", J - 1, 0))
        if self.prep and s >= 3 and J < self.JOBS - 2:
            out.append(("prep", J // 2 + 1, 5 * (J % 2) + s - 3))
        return out


def at(it, jj, f):
    if isinstance(it, int):
        return f(4 * it + jj)
    per = f(4 * 3 + jj) - f(4 * 2 + jj)
    return it * per + (f(4 * 2 + jj) - 2 * per)


def wait(eng, sem, it, jj, f):
    v = at(it, jj, f)
    if not isinstance(v, int) or v > 0:
        eng.wait_ge(sem, v)


def settle(eng, sem):
    eng.sem_inc(sem, 1)


def turns(eng, plan, turn):
    last = plan.JOBS // 4 - 1
    for jj in range(4):
        turn(0, jj, jj)
    with eng.Fori(1, last) as it:
        for jj in range(4):
            turn(it, jj, 8 + jj)
    for jj in range(6):
        turn(last, jj, 4 * last + jj)


def batch_of(it, jj):
    return (4 * it + jj) // 16 if isinstance(it, int) else (it * 4 + jj) // 16


def attention(nc, g, layer):
    plan = Plan(layer)
    tag = f"a{layer}_"
    rows = plan.rows
    SLOTS = 8
    LOADS = 16 * (2 * SLOTS + 2)
    JOBS = plan.JOBS
    stage_sems = []
    with ExitStack() as ctx:
        ctx.callback(give_back, nc, stage_sems)

        def sb(name, shape, dt=F32):
            return ctx.enter_context(nc.sbuf_tensor(tag + name, shape, dt))

        def sem(name):
            return kept(nc, stage_sems, tag + name)

        if layer == 0:
            q_stack = [[sb(f"q_stack{n}", [P, 2, SEQ], BF16)] for n in range(2)]
            toeplitz = [sb(f"toeplitz{n}", [P, 2, 2 * P]) for n in range(2)]
        else:
            q_stack = [[sb(f"q_hi{n}", [P, 2, SEQ], F32R), sb(f"q_lo{n}", [P, 2, SEQ], F32R)] for n in range(2)]
            causal_rows = sb("causal_rows", [P, SEQ])
            h_pair = sb("h_pair", [P, SEQ])
            w_qk = sb("w_qk", [P, 2, 2, 2, 64])
            w_q = sb("w_q", [P, 2, 2, 64])
            w_v = sb("w_v", [P, 2 * 64])
        k_stack = [sb(f"k_stack{n}", [P, 2, SEQ], F32R if layer else BF16) for n in range(2)]
        v = [sb(f"v{n}", [P, TB, 2, rows]) for n in range(2)]
        w_out_raw = [sb(f"w_out_raw{n}", [P, DIM]) for n in range(2)]
        w_out = [sb(f"w_out{n}", [P, DIM]) for n in range(2)]
        probs = [sb(f"probs{n}", [P, 2, 4, SEQ]) for n in range(2)]
        turned = [[sb(f"turned{h}{n}", [P, BANK]) for n in range(2)] for h in range(2)]
        plain_min = sb("plain_min", [P, 16])
        row_min = sb("row_min", [P, 16])
        row_sum = sb("row_sum", [P, 2, 8])
        inv_sum = sb("inv_sum", [P, 8])
        inv_wide = sb("inv_wide", [P, 4, 2, 64])
        inv_rows = sb("inv_rows", [P, BANK])
        out_T = sb("out_T", [P, BANK])

        scores_bank = lambda s: g.ps[:, 2 * (s % 2):2 * (s % 2) + 2, :].rearrange("p a n -> p (a n)")
        turn_bank = [g.ps[:, 4, :], g.ps[:, 5, :]]
        out_bank = g.ps[:, 6, :]
        shared = g.ps[:, 7, :]

        scores_done = sem("scores_done")
        plain_done = sem("plain_done")
        min_done = sem("min_done")
        probs_done = sem("probs_done")
        turn_done = [sem(f"turn_done{h}") for h in range(2)]
        turned_out = [sem(f"turned_out{h}") for h in range(2)]
        product_done = sem("product_done")
        inv_done = sem("inv_done")
        wide_done = sem("wide_done")
        out_done = sem("out_done")
        item_done = sem("item_done")
        item_out = sem("item_out")
        w_out_done = sem("w_out_done")
        if layer == 0:
            stack_in = [sem(f"stack_in{n}") for n in range(2)]
            v_done = sem("v_done")
            table_done = sem("table_done")
        else:
            weights_in = sem("weights_in")
            w_q_done = sem("w_q_done")
            hi_done = sem("hi_done")
            lo_done = sem("lo_done")
            v_done = sem("v_done")
        cleared = sem("cleared")
        held = {e: sem("held_" + e) for e in ("dve", "pool", "sp")}

        def unit(u):
            return u // 2, u % 2

        with nc.Block() as block:
            @block.sync
            def _(sp):
                if layer == 0:
                    sp.wait_ge(cleared, 1)

                    def pair(it, n):
                        wait(sp, scores_done, it, 2 * n, lambda J: 8 * (J - 2))
                        settle(sp, held["sp"])
                        wait(sp, w_out_done, it, 2 * n, lambda J: J // 2 - 1)
                        settle(sp, held["sp"])
                        tok = (it // 4) * SEQ
                        head = (it % 4) * 4 + 2 * n
                        for slot in range(SLOTS):
                            for a, part, dst in ((0, slot // 3, q_stack[n][0]), (1, slot % 3, k_stack[n])):
                                src = g.qk_dram[part, a, ds(head * 8, 16), ds(tok, SEQ)]
                                sp.dma_start(dst[8 * slot:8 * slot + 8], src.rearrange("(h d) t -> d h t", d=8))\
                                    .then_inc(stack_in[n], 16)
                        for h in range(2):
                            sp.dma_start(w_out_raw[n][32 * h:32 * h + 8, :],
                                         g.w0_out[ds((head + h) * 8, 8), :]).then_inc(stack_in[n], 16)

                    for n in range(2):
                        pair(0, n)
                    with sp.Fori(1, PAIRS // 2) as it:
                        for n in range(2):
                            pair(it, n)
                else:
                    def pair(it, n):
                        if not (isinstance(it, int) and 2 * it + n == 0):
                            wait(sp, item_done, it, 2 * n, lambda J: plan.index["prep", J // 2 - 1, 9] + 1)
                            settle(sp, held["sp"])
                            wait(sp, w_out_done, it, 2 * n, lambda J: J // 2)
                        settle(sp, held["sp"])
                        col = (it % 4) * 256 + 128 * n
                        sp.dma_start(h_pair[:], g.hT[:, ds((it // 4) * SEQ, SEQ)]).then_inc(weights_in, 16)
                        for a in range(2):
                            for copy in range(2):
                                sp.dma_start(w_qk[:, a, :, copy, :], g.w1_qk[a, :, ds(col, 128)].rearrange(
                                    "p (h d) -> p h d", h=2)).then_inc(weights_in, 16)
                        sp.dma_start(w_v[:], g.w1_v[:, ds(col, 128)]).then_inc(weights_in, 16)
                        sp.dma_start(w_out_raw[0][:], g.w1_out[ds(col, 128), :]).then_inc(weights_in, 16)

                    pair(0, 0)
                    pair(0, 1)
                    with sp.Fori(1, PAIRS // 2) as it:
                        for n in range(2):
                            pair(it, n)

            @block.gpsimd
            def _(pool):
                if layer == 0:
                    zeroed = [q_stack[0][0], q_stack[1][0], k_stack[0], k_stack[1]]
                    for t in zeroed:
                        pool.memset(t[:], 0.0)
                    for t in w_out_raw:
                        pool.memset(t[:], 0.0)
                    for t in v:
                        last = pool.memset(t[:], 0.0)
                    last.then_inc(cleared, 1)
                    pool.wait_ge(cleared, 1)
                else:
                    pool.memset(causal_rows[:], 50.0).then_inc(cleared, 1)
                    pool.wait_ge(cleared, 1)
                    pool.affine_select(out=causal_rows[:], in_=causal_rows[:], compare_op=ALU.is_gt, fill=0.0,
                                       base=0, pattern=[[1, SEQ]], channel_multiplier=-1).then_inc(cleared, 1)

                def pair(it, n):
                    b = it // 4
                    if layer == 0:
                        head = (it % 4) * 4 + 2 * n
                        wait(pool, product_done, it, 2 * n, lambda J: plan.step(J - 2))
                        pool.tensor_copy(v[n][:, :, :, 0:8], g.v_all[:, ds(b * TB, TB), ds(head * 8, 16)].rearrange(
                            "p t (h d) -> p t h d", h=2)).then_inc(v_done, 1)
                        wait(pool, min_done, it, 2 * n, lambda J: 8 * (J - 2))
                        pool.tensor_copy(toeplitz[n][:], g.toeplitz_all[:, ds(head, 2), :]).then_inc(table_done, 1)
                        pool.wait_ge(stack_in[n], it * LOADS + LOADS)
                        raw = w_out_raw[n]
                    else:
                        pool.wait_ge(weights_in, (it * 2 + n) * 112 + 112)
                        if not (isinstance(it, int) and 2 * it + n == 0):
                            wait(pool, item_done, it, 2 * n, lambda J: plan.index["prep", J // 2 - 1, 3] + 1)
                        settle(pool, held["pool"])
                        pool.tensor_scalar(w_q[:], w_qk[:, 0], -0.125, None, ALU.mult).then_inc(w_q_done, 1)
                        raw = w_out_raw[0]
                    if not (isinstance(it, int) and it == 0):
                        wait(pool, item_done, it, 2 * n, lambda J: plan.index["y", J - 3, 0] + 1)
                    settle(pool, held["pool"])
                    pool.tensor_tensor(w_out[n][:], raw[:],
                                       g.gate_rows[:, layer, 0, ds(b, 1), :].rearrange("p a d -> p (a d)"),
                                       ALU.mult).then_inc(w_out_done, 1)

                for n in range(2):
                    pair(0, n)
                with pool.Fori(1, PAIRS // 2) as it:
                    for n in range(2):
                        pair(it, n)

            @block.tensor
            def _(pe):
                def prep(it, jj, J, key):
                    _, p, n = key
                    if n == 0:
                        wait(pe, weights_in, it, jj, lambda J: 112 * (J // 2 + 2)) if J is not None else pe.wait_ge(weights_in, 112)
                        wait(pe, w_q_done, it, jj, lambda J: J // 2 + 2) if J is not None else pe.wait_ge(w_q_done, 1)
                    if n < 8:
                        a, h, half = n // 4, n // 2 % 2, n % 2
                        w = w_q[:, h] if a == 0 else w_qk[:, 1, h]
                        return pe.matmul(shared, w.rearrange("p c d -> p (c d)"), h_pair[:, half * BANK:(half + 1) * BANK],
                                         start=True, stop=True)
                    for t in range(4):
                        tok = (4 * (n - 8) + t) * P
                        mm = pe.matmul(shared[:, t * P:(t + 1) * P], h_pair[:, tok:tok + P], w_v[:], start=True, stop=True)
                    return mm

                def item(it, jj, J, key):
                    index = lambda J2: plan.index[key[0], J2 + key[1] - J, key[2]]
                    if key[0] == "prep":
                        index = lambda J2: plan.index["prep", J2 // 2 + 1, key[2]]
                    wait(pe, item_out, it, jj, index)
                    if key[0] == "prep":
                        mm = prep(it, jj, J, key)
                    elif key[0] == "r":
                        wait(pe, wide_done, it, jj, lambda J2: J2)
                        for i in range(4):
                            mm = pe.transpose(shared[:, i * P:(i + 1) * P], inv_wide[:, i].rearrange("p h r -> p (h r)"),
                                              g.ident[:])
                    else:
                        lag = J - key[1]
                        wait(pe, out_done, it, jj, lambda J2: J2 - lag + 1)
                        wait(pe, w_out_done, it, jj, lambda J2: (J2 - lag) // 2 + 1)
                        for i in range(4):
                            mm = pe.matmul(shared[:, i * P:(i + 1) * P], out_T[0:2 * rows, i * P:(i + 1) * P],
                                           w_out[key[1] // 2 % 2][0:2 * rows, :], start=True, stop=True)
                    mm.then_inc(item_done, 1)

                def turn(it, jj, J):
                    n = J // 2 % 2
                    for s in range(8):
                        i, h = unit(s)
                        if J < JOBS:
                            if s == 0 and layer == 0:
                                pe.wait_ge(stack_in[n], it * LOADS + LOADS)
                            if s == 0 and layer == 1:
                                wait(pe, lo_done, it, jj, lambda J2: 8 * (J2 // 2 + 1))
                            wait(pe, probs_done, it, jj, lambda J2: 8 * J2 + s - 1)
                            q0 = (4 * (J % 2) + i) * P
                            width = plan.width(J, i)
                            for k0 in range(0, width, BANK):
                                k1 = min(width, k0 + BANK)
                                for m, q in enumerate(q_stack[n]):
                                    mm = pe.matmul(scores_bank(s)[:, k0:k1], q[:, h, q0:q0 + P], k_stack[n][:, h, k0:k1],
                                                   start=(m == 0), stop=(m == len(q_stack[n]) - 1))
                            mm.then_inc(scores_done, 1)
                        if 0 <= J - 1 < JOBS and s < plan.steps(J - 1):
                            if s == 0:
                                wait(pe, probs_done, it, jj, lambda J2: 8 * J2)
                            for h in range(2):
                                wait(pe, turned_out[h], it, jj, lambda J2: plan.step(J2 - 1) + s)
                                for i in range(plan.first(J - 1, s) // P, 4):
                                    mm = pe.transpose(turn_bank[h][:, i * P:(i + 1) * P],
                                                      probs[(J - 1) % 2][:, h, i, s * P:(s + 1) * P], g.ident[:])
                                mm.then_inc(turn_done[h], 1)
                        for key in plan.items(J, s):
                            item(it, jj, J, key)
                        job, kt = plan.product(J, s)
                        if job is not None and 0 <= job < JOBS:
                            lag = J - job
                            if kt == 0:
                                wait(pe, out_done, it, jj, lambda J2: J2 - lag)
                                wait(pe, v_done, it, jj, lambda J2: ((J2 - lag) // 2 + 1) * (1 if layer == 0 else 2))
                            off = plan.first(job, kt)
                            for h in range(2):
                                wait(pe, turned_out[h], it, jj, lambda J2: plan.step(J2 - lag) + kt + 1)
                                mm = pe.matmul(out_bank[rows * h:rows * (h + 1), off:], v[job // 2 % 2][:, kt, h, :],
                                               turned[h][kt % 2][:, off:], start=(kt == 0),
                                               stop=(kt == plan.steps(job) - 1), tile_position=(0, rows * h))
                            mm.then_inc(product_done, 1)

                for n in range(plan.prep):
                    if n:
                        pe.wait_ge(item_out, n)
                    prep(0, 0, None, ("prep", 0, n)).then_inc(item_done, 1)
                turns(pe, plan, turn)

            @block.vector
            def _(dve):
                def split(it, jj, J, key):
                    _, p, n = key
                    a, h, half = n // 4, n // 2 % 2, n % 2
                    cols = slice(half * BANK, (half + 1) * BANK)
                    hi = (q_stack[p % 2][0] if a == 0 else k_stack[p % 2])[:, h, cols]
                    dve.tensor_copy(hi, shared).then_inc(hi_done, 1)
                    count = lambda J2: 8 * (J2 // 2 + 1) + n + 1
                    if J is None:
                        dve.wait_ge(hi_done, n + 1)
                    else:
                        wait(dve, hi_done, it, jj, count)
                    if a == 0:
                        done = dve.tensor_tensor(q_stack[p % 2][1][:, h, cols], shared, hi.bitcast(F32), ALU.subtract)
                    else:
                        low = hi[64:128].bitcast(F32)
                        done = dve.tensor_tensor(k_stack[p % 2][64:128, h, cols], shared[64:128], low, ALU.subtract)
                    done.then_inc(lo_done, 1)
                    if J is None:
                        dve.wait_ge(lo_done, n + 1)
                    else:
                        wait(dve, lo_done, it, jj, count)
                    dve.sem_inc(item_out, 1)

                def turn(it, jj, J):
                    for s in range(8):
                        i, h = unit(s)
                        if J < JOBS:
                            n = J // 2 % 2
                            wait(dve, scores_done, it, jj, lambda J2: 8 * J2 + s + 1)
                            width, plain = plan.width(J, i), plan.plain(J, i)
                            sc = scores_bank(s)
                            slot = 8 * (J % 2) + s
                            floor = 3e38
                            if plain:
                                dve.tensor_reduce(plain_min[:, slot:slot + 1], sc[:, 0:plain], AX, ALU.min)\
                                   .then_inc(plain_done, 1)
                                wait(dve, plain_done, it, jj, lambda J2: plan.plains(J2, s + 1))
                                floor = plain_min[:, slot:slot + 1]
                            rest = width - plain
                            if layer == 0:
                                if s == 0:
                                    wait(dve, table_done, it, jj, lambda J2: J2 // 2 + 1)
                                add = toeplitz[n][:, h, 2 * P - rest:]
                            else:
                                if s == 0 and J == 0:
                                    dve.wait_ge(cleared, 2)
                                add = causal_rows[:, 0:rest]
                            settle(dve, held["dve"])
                            dve.tensor_tensor_reduce(out=sc[:, plain:width], in0=sc[:, plain:width], in1=add, scale=1.0,
                                                     scalar=floor, op0=ALU.add, op1=ALU.min,
                                                     accum_out=row_min[:, slot:slot + 1]).then_inc(min_done, 1)
                        if 0 <= J - 1 < JOBS and s < plan.steps(J - 1):
                            wait(dve, turn_done[0], it, jj, lambda J2: plan.step(J2 - 1) + s + 1)
                            wait(dve, product_done, it, jj, lambda J2: plan.step(J2 - 1) + s - 1)
                            off = plan.first(J - 1, s)
                            dve.tensor_copy(turned[0][s % 2][:, off:], turn_bank[0][:, off:]).then_inc(turned_out[0], 1)
                        if s == 1 and 0 <= J - 1 < JOBS:
                            wait(dve, probs_done, it, jj, lambda J2: 8 * J2)
                            dve.reciprocal(inv_sum[:], row_sum[:, (J - 1) % 2]).then_inc(inv_done, 1)
                            wait(dve, inv_done, it, jj, lambda J2: J2)
                            if not (isinstance(it, int) and J - 2 < 0):
                                wait(dve, item_done, it, jj, lambda J2: plan.index["r", J2 - 2, 0] + 1)
                            dve.tensor_copy(inv_wide[:].rearrange("p i h r -> p i (h r)")[:, :, 0:2 * rows].rearrange(
                                "p i (h r) -> p i h r", h=2),
                                inv_sum[:].rearrange("p (i h) -> p i h", h=2).unsqueeze(3).to_broadcast([P, 4, 2, rows]))\
                               .then_inc(wide_done, 1)
                        for key in plan.items(J, s):
                            if key[0] == "prep" and key[2] < 8:
                                wait(dve, item_done, it, jj, lambda J2: plan.index["prep", J2 // 2 + 1, key[2]] + 1)
                                split(it, jj, J, key)
                            if key[0] == "y":
                                lag = J - key[1]
                                wait(dve, item_done, it, jj, lambda J2: plan.index["y", J2 - lag, 0] + 1)
                                if isinstance(it, int):
                                    tile = 4 * (key[1] % 2) + key[1] // 16 * TB
                                else:
                                    tile = (it * 4 + (jj - lag)) // 16 * TB + 4 * (key[1] % 2)
                                rowsx = g.x[:, ds(tile, 4), :]
                                dve.tensor_tensor(rowsx, rowsx, shared.rearrange("p (t d) -> p t d", t=4), ALU.add)\
                                   .then_inc(item_out, 1)
                        job, kt = plan.product(J, s)
                        if job is not None and 0 <= job < JOBS and kt == plan.steps(job) - 1:
                            lag = J - job
                            wait(dve, product_done, it, jj, lambda J2: plan.step(J2 - lag) + kt + 1)
                            wait(dve, item_out, it, jj, lambda J2: plan.index["r", J2 - lag, 0] + 1)
                            if job > 0:
                                wait(dve, item_done, it, jj, lambda J2: plan.index["y", J2 - lag - 1, 0] + 1)
                            dve.tensor_tensor(out_T[0:2 * rows, :], out_bank[0:2 * rows, :], inv_rows[0:2 * rows, :],
                                              ALU.mult).then_inc(out_done, 1)

                if layer == 0:
                    dve.memset(inv_wide[:], 0.0).then_inc(inv_done, 0 + 1) if False else dve.memset(inv_wide[:], 0.0)
                for n in range(min(8, plan.prep)):
                    dve.wait_ge(item_done, n + 1)
                    split(0, 0, None, ("prep", 0, n))
                turns(dve, plan, turn)

            @block.scalar
            def _(act):
                def copy_v(it, jj, J, key):
                    _, p, n = key
                    t0 = 4 * (n - 8)
                    act.activation(v[p % 2][:, t0:t0 + 4].rearrange("p t h d -> p t (h d)"),
                                   shared.rearrange("p (t c) -> p t c", t=4), ACT.Copy).then_inc(v_done, 1)
                    if J is None:
                        act.wait_ge(v_done, n - 7)
                    else:
                        wait(act, v_done, it, jj, lambda J2: 2 * (J2 // 2 + 1) + n - 7)
                    act.sem_inc(item_out, 1)

                def turn(it, jj, J):
                    for s in range(8):
                        i, h = unit(s)
                        if 0 <= J - 1 < JOBS and s < plan.steps(J - 1):
                            wait(act, turn_done[1], it, jj, lambda J2: plan.step(J2 - 1) + s + 1)
                            wait(act, product_done, it, jj, lambda J2: plan.step(J2 - 1) + s - 1)
                            off = plan.first(J - 1, s)
                            act.activation(turned[1][s % 2][:, off:], turn_bank[1][:, off:], ACT.Copy)\
                               .then_inc(turned_out[1], 1)
                        if J < JOBS:
                            wait(act, min_done, it, jj, lambda J2: 8 * J2 + s + 1)
                            if s == 0:
                                wait(act, turn_done[1], it, jj, lambda J2: plan.step(J2 - 1))
                                wait(act, inv_done, it, jj, lambda J2: J2 - 1)
                            slot = 8 * (J % 2) + s
                            width = plan.width(J, i)
                            act.activation(probs[J % 2][:, h, i, 0:width], scores_bank(s)[:, 0:width], ACT.Exp,
                                           bias=row_min[:, slot:slot + 1], scale=-1.0,
                                           accum_out=row_sum[:, J % 2, s:s + 1]).then_inc(probs_done, 1)
                        for key in plan.items(J, s):
                            if key[0] == "prep" and key[2] >= 8:
                                wait(act, item_done, it, jj, lambda J2: plan.index["prep", J2 // 2 + 1, key[2]] + 1)
                                copy_v(it, jj, J, key)
                            if key[0] == "r":
                                wait(act, item_done, it, jj, lambda J2: plan.index["r", J2 - 1, 0] + 1)
                                wait(act, out_done, it, jj, lambda J2: J2 - 1)
                                act.activation(inv_rows[:], shared, ACT.Copy).then_inc(item_out, 1)

                for n in range(8, plan.prep):
                    act.wait_ge(item_done, n + 1)
                    copy_v(0, 0, None, ("prep", 0, n))
                turns(act, plan, turn)


def experts(nc, g):
    EM = EXPERTS * 2
    CHUNKS = TOKENS // BANK
    stage_sems = []
    with ExitStack() as ctx:
        ctx.callback(give_back, nc, stage_sems)

        def sb(name, shape, dt=F32):
            return ctx.enter_context(nc.sbuf_tensor("e_" + name, shape, dt))

        def sem(name):
            return kept(nc, stage_sems, "e_" + name)

        w1 = sb("w1", [P, EXPERTS, HIDDEN])
        w3 = sb("w3", [P, EXPERTS, HIDDEN])
        w2 = sb("w2", [P, EXPERTS, 2, DIM])
        lora_a = sb("lora_a", [RANK, 2, EXPERTS, DIM])
        lora_b = sb("lora_b", [RANK, 2, EXPERTS, HIDDEN])
        lora_a2 = sb("lora_a2", [RANK, EXPERTS, HIDDEN])
        lora_b2 = sb("lora_b2", [RANK, EXPERTS, DIM])
        b13 = sb("b13", [P, 2, EXPERTS, 2])
        b2 = sb("b2", [EXPERTS, DIM])
        w_gate = sb("w_gate", [P, EXPERTS])
        iota = sb("iota", [P, EXPERTS])
        logits_T = sb("logits_T", [EXPERTS, TOKENS])
        logits = sb("logits", [P, TILES, EXPERTS])
        best = sb("best", [P, TILES, 8])
        best_at = sb("best_at", [P, TILES, 8], U32)
        index = sb("index", [P, TILES, 2])
        weight = sb("weight", [P, TILES, 2])
        gap = sb("gap", [P, TILES])
        total = sb("total", [P, TILES])
        second = sb("second", [P, TILES, EXPERTS])
        gates = sb("gates", [P, TILES, EXPERTS])
        gates_T = sb("gates_T", [EXPERTS, TOKENS])
        gates_chunk = sb("gates_chunk", [EXPERTS, BANK])
        silu = [sb(f"silu{n}", [P, BANK]) for n in range(2)]
        hidden = [[sb(f"hidden{n}{m}", [P, BANK]) for m in range(2)] for n in range(2)]
        acc = sb("acc", [P, 4, DIM])
        gated = sb("gated", [P, 4, DIM])
        loaded, low_done, merged = sem("loaded"), sem("low_done"), sem("merged")
        logit_mm, logit_out, turn_done, route, exp_done, gate_turned, gate_out = map(sem, (
            "logit_mm", "logit_out", "turn_done", "route", "exp_done", "gate_turned", "gate_out"))
        merges = [("13", a, e) for a in range(2) for e in range(0, EXPERTS, 2)] + [("2", 0, e) for e in range(0, EXPERTS, 2)]
        with nc.Block() as block:
            @block.sync
            def _(sp):
                loads = ((lora_a, g.lora_a), (lora_b, g.lora_b), (w1, g.w1), (w3, g.w3), (lora_a2, g.lora_a2),
                         (lora_b2, g.lora_b2), (w2, g.w2), (w_gate, g.w_gate), (iota, g.iota), (b13, g.b13), (b2, g.b2))
                for dst, src in loads:
                    sp.dma_start(dst[:], src).then_inc(loaded, 16)

            @block.tensor
            def _(pe):
                pe.wait_ge(loaded, 176)
                for c in range(CHUNKS):
                    if c >= 2:
                        pe.wait_ge(logit_out, c - 1)
                    pe.matmul(g.ps[0:EXPERTS, 6 + c % 2, :], w_gate[:], g.hT[:, c * BANK:(c + 1) * BANK], start=True,
                              stop=True).then_inc(logit_mm, 1)
                pe.wait_ge(logit_out, CHUNKS)
                for t in range(TILES):
                    mm = pe.transpose(g.ps[:, 6, t * EXPERTS:(t + 1) * EXPERTS], logits_T[:, t * P:(t + 1) * P],
                                      g.ident[0:EXPERTS, 0:EXPERTS])
                mm.then_inc(turn_done, 1)
                for n, (kind, a, e) in enumerate(merges):
                    if n >= 4:
                        pe.wait_ge(merged, n - 3)
                    for j in range(2):
                        if kind == "13":
                            mm = pe.matmul(g.ps[:, n % 4, j * HIDDEN:(j + 1) * HIDDEN], lora_a[:, a, e + j],
                                           lora_b[:, a, e + j], start=True, stop=True)
                        else:
                            for m in range(2):
                                col = (2 * j + m) * DIM
                                mm = pe.matmul(g.ps[:, n % 4, col:col + DIM], lora_a2[:, e + j, m * P:(m + 1) * P],
                                               lora_b2[:, e + j], start=True, stop=True)
                    mm.then_inc(low_done, 1)
                pe.wait_ge(route, 7)
                for c in range(CHUNKS):
                    if c >= 2:
                        pe.wait_ge(gate_out, c - 1)
                    for t in range(4):
                        mm = pe.transpose(g.ps[0:EXPERTS, 4 + c % 2, t * P:(t + 1) * P], gates[:, 4 * c + t, :], g.ident[:])
                    mm.then_inc(gate_turned, 1)

            @block.scalar
            def _(act):
                for c in range(CHUNKS):
                    act.wait_ge(logit_mm, c + 1)
                    act.activation(logits_T[:, c * BANK:(c + 1) * BANK], g.ps[0:EXPERTS, 6 + c % 2, :], ACT.Copy)\
                       .then_inc(logit_out, 1)
                act.wait_ge(route, 3)
                act.activation(weight[:, :, 1], gap[:], ACT.Exp).then_inc(exp_done, 1)
                for c in range(CHUNKS):
                    act.wait_ge(gate_turned, c + 1)
                    act.activation(gates_T[:, c * BANK:(c + 1) * BANK], g.ps[0:EXPERTS, 4 + c % 2, :], ACT.Copy)\
                       .then_inc(gate_out, 1)

            @block.vector
            def _(dve):
                dve.wait_ge(turn_done, 1)
                dve.tensor_copy(logits[:].rearrange("p t e -> p (t e)"), g.ps[:, 6, 0:TILES * EXPERTS]).then_inc(route, 1)
                dve.wait_ge(route, 1)
                for t in range(TILES):
                    last = dve.max(best[:, t, :], logits[:, t, :])
                last.then_inc(route, 1)
                dve.wait_ge(route, 2)
                dve.tensor_tensor(gap[:], best[:, :, 1], best[:, :, 0], ALU.subtract).then_inc(route, 1)
                for t in range(TILES):
                    last = dve.max_index(best_at[:, t, :], best[:, t, :], logits[:, t, :])
                last.then_inc(route, 1)
                dve.wait_ge(exp_done, 1)
                dve.tensor_scalar(total[:], weight[:, :, 1], 1.0, None, ALU.add).then_inc(route, 1)
                dve.wait_ge(route, 5)
                dve.reciprocal(weight[:, :, 0], total[:])
                dve.tensor_copy(index[:], best_at[:, :, 0:2]).then_inc(route, 1)
                dve.wait_ge(route, 6)
                dve.tensor_tensor(weight[:, :, 1], weight[:, :, 1], weight[:, :, 0], ALU.mult)
                wide = [P, TILES, EXPERTS]
                for n, dst in ((0, gates), (1, second)):
                    last = dve.tensor_tensor(dst[:], iota[:].unsqueeze(1).to_broadcast(wide),
                                             index[:, :, n:n + 1].to_broadcast(wide), ALU.is_equal)
                last.then_inc(exp_done, 1)
                dve.wait_ge(exp_done, 2)
                for n, dst in ((0, gates), (1, second)):
                    last = dve.tensor_tensor(dst[:], dst[:], weight[:, :, n:n + 1].to_broadcast(wide), ALU.mult)
                last.then_inc(exp_done, 1)
                dve.wait_ge(exp_done, 3)
                dve.tensor_tensor(gates[:], gates[:], second[:], ALU.add).then_inc(route, 1)
                for n, (kind, a, e) in enumerate(merges):
                    dve.wait_ge(low_done, n + 1)
                    w = (w1, w3)[a][:, e:e + 2].rearrange("p e n -> p (e n)") if kind == "13" else \
                        w2[:, e:e + 2].rearrange("p e m d -> p (e m d)")
                    dve.tensor_tensor(w, w, g.ps[:, n % 4, :], ALU.add).then_inc(merged, 1)

        up_done, silu_done, hidden_done, down_done, acc_done, bias_in, bias_mm, bias_out, gated_done, x_done = map(sem, (
            "up_done", "silu_done", "hidden_done", "down_done", "acc_done", "bias_in", "bias_mm", "bias_out",
            "gated_done", "x_done"))
        with nc.Block() as block:
            @block.gpsimd
            def _(pool):
                with pool.Fori(0, CHUNKS) as c:
                    pool.wait_ge(bias_mm, c + 1)
                    pool.tensor_copy(gates_chunk[:], gates_T[:, ds(c * BANK, BANK)]).then_inc(bias_in, 1)

            @block.tensor
            def _(pe):
                pe.sem_inc(bias_mm, 1)
                pe.sem_inc(down_done, 2)

                def down(c, e):
                    pe.wait_ge(hidden_done, c * EM + 2 * e + 4)
                    pe.wait_ge(acc_done, c * EXPERTS + e + 1)
                    for t in range(4):
                        for m in range(2):
                            mm = pe.matmul(g.ps[:, 4 + e % 2, t * DIM:(t + 1) * DIM], hidden[e % 2][m][:, t * P:(t + 1) * P],
                                           w2[:, e, m, :], start=(m == 0), stop=(m == 1))
                    mm.then_inc(down_done, 1)

                with pe.Fori(0, CHUNKS) as c:
                    for e in range(EXPERTS):
                        for m in range(2):
                            i = 2 * e + m
                            pe.wait_ge(hidden_done, c * EM + i + 1)
                            for n, w in enumerate((w1, w3)):
                                mm = pe.matmul(g.ps[:, 2 * n + i % 2, :], w[:, e, m * P:(m + 1) * P],
                                               g.hT[:, ds(c * BANK, BANK)], start=True, stop=True)
                            mm.then_inc(up_done, 1)
                        if e == 0:
                            pe.wait_ge(bias_in, c + 1)
                            pe.wait_ge(bias_out, c + 1)
                            for t in range(4):
                                mm = pe.matmul(g.ps[:, 6, t * DIM:(t + 1) * DIM], gates_chunk[:, t * P:(t + 1) * P], b2[:],
                                               start=True, stop=True)
                            mm.then_inc(bias_mm, 1)
                        else:
                            down(c, e - 1)
                    down(c, EXPERTS - 1)

            @block.scalar
            def _(act):
                act.sem_inc(bias_out, 1)
                with act.Fori(0, CHUNKS) as c:
                    for i in range(EM):
                        act.wait_ge(up_done, c * EM + i + 1)
                        act.activation(silu[i % 2][:], g.ps[:, i % 2, :], ACT.Silu, bias=b13[:, 0, i // 2, i % 2:i % 2 + 1])\
                           .then_inc(silu_done, 1)
                        if i == 1:
                            act.wait_ge(bias_mm, c + 2)
                            act.wait_ge(gated_done, c + 1)
                            act.activation(acc[:].rearrange("p t d -> p (t d)"), g.ps[:, 6, :], ACT.Copy).then_inc(bias_out, 1)

            @block.vector
            def _(dve):
                dve.sem_inc(hidden_done, 2)
                dve.sem_inc(acc_done, 2)
                dve.sem_inc(gated_done, 1)

                def accumulate(c, e):
                    dve.wait_ge(down_done, c * EXPERTS + e + 3)
                    if e == 0:
                        dve.wait_ge(bias_out, c + 2)
                    else:
                        dve.wait_ge(acc_done, c * EXPERTS + e + 2)
                    for t in range(4):
                        last = dve.scalar_tensor_tensor(
                            acc[:, t, :], g.ps[:, 4 + e % 2, t * DIM:(t + 1) * DIM],
                            gates[:, ds(c * 4 + t, 1), e:e + 1].rearrange("p a e -> p (a e)"), acc[:, t, :], ALU.mult, ALU.add)
                    last.then_inc(acc_done, 1)

                with dve.Fori(0, CHUNKS) as c:
                    for e in range(EXPERTS):
                        for m in range(2):
                            i = 2 * e + m
                            dve.wait_ge(silu_done, c * EM + i + 1)
                            dve.wait_ge(down_done, c * EXPERTS + e + 1)
                            dve.scalar_tensor_tensor(hidden[e % 2][m][:], g.ps[:, 2 + i % 2, :], b13[:, 1, e, m:m + 1],
                                                     silu[i % 2][:], ALU.add, ALU.mult).then_inc(hidden_done, 1)
                        if e:
                            accumulate(c, e - 1)
                    accumulate(c, EXPERTS - 1)
                    dve.wait_ge(acc_done, c * EXPERTS + EXPERTS + 2)
                    dve.tensor_tensor(gated[:], acc[:], g.gate_rows[:, 0, 1, ds(c // 2, 1), :].to_broadcast([P, 4, DIM]),
                                      ALU.mult).then_inc(gated_done, 1)
                    dve.wait_ge(gated_done, c + 2)
                    rowsx = g.x[:, ds(c * 4, 4), :]
                    dve.tensor_tensor(rowsx, rowsx, gated[:], ALU.add).then_inc(x_done, 1)


def shifted(z, rows, b, t0, n):
    lo = t0 + (1 if rows.start else 0)
    return z[rows, ds(b, 1), ds(lo, n)].rearrange("p a t -> p (a t)")


TOP, LOW = slice(0, 64), slice(64, 128)


def local_attention(nc, g, layer):
    stage_sems = []
    with ExitStack() as ctx:
        ctx.callback(give_back, nc, stage_sems)

        def sb(name, shape, dt=F32):
            return ctx.enter_context(nc.sbuf_tensor(f"t{layer}_{name}", shape, dt))

        def sem(name):
            return kept(nc, stage_sems, f"t{layer}_{name}")

        G = 4
        w = sb("w", [P, 3 * INNER])
        wo = sb("wo", [P, 4, DIM])
        scale_rows = sb("scale_rows", [P, 2, LDH])
        rot = sb("rot", [P, TB, 2, 2, LDH])
        mask = sb("mask", [P, 2, 192])
        half = sb("half", [P, 16])
        h_tile = [sb(f"h_tile{n}", [P, P]) for n in range(2)]
        squares = sb("squares", [P, 2 * INNER])
        norm = sb("norm", [P, 16])
        inv_norm = sb("inv_norm", [P, 16])
        by_cos = sb("by_cos", [P, 16, LDH])
        by_sin = sb("by_sin", [P, 16, LDH])
        rotated = sb("rotated", [P, 16, LDH])
        q_T = [sb(f"q_T{n}", [P, 4, P]) for n in range(2)]
        k_T = [sb(f"k_T{n}", [P, 4, P]) for n in range(4)]
        v = [sb(f"v{n}", [P, INNER]) for n in range(4)]
        row_min = sb("row_min", [P, 2, G])
        row_sum = sb("row_sum", [P, 2, 2 * G])
        inv_sum = sb("inv_sum", [P, 2 * G])
        probs = [sb(f"probs{n}", [P, G, 2 * P]) for n in range(2)]
        probs_T = [sb(f"probs_T{n}", [P, 2, BANK]) for n in range(2)]
        out = sb("out", [P, INNER])
        out_T = sb("out_T", [P, 4, P])

        loaded, ready, tables = sem("loaded"), sem("ready"), sem("tables")
        h_done, qkv_done, square_done, v_done, sum_done, rotate_done = map(sem, (
            "h_done", "qkv_done", "square_done", "v_done", "sum_done", "rotate_done"))
        root_done, inv_done, pool_step, rotated_done = map(sem, ("root_done", "inv_done", "pool_step", "rotated_done"))
        scores_done, min_done, probs_done = map(sem, ("scores_done", "min_done", "probs_done"))
        turn_done, out5, out6 = map(sem, ("turn_done", "out5", "out6"))
        product_done, norm_out, proj_done, sum_inv, inv_sum_done, held = map(sem, (
            "product_done", "norm_out", "proj_done", "sum_inv", "inv_sum_done", "held"))
        qk_banks = g.ps[:, 0:2, :].rearrange("p a n -> p (a n)")
        heads_of = lambda ap: ap.rearrange("p (h d) -> p h d", d=LDH)
        G0, BACK, G1, FRONT = range(4)
        USES = 4 * TB

        def use(t, k):
            return 4 * t - 1 + k if t else (0, None, 1, 2)[k]

        with nc.Block() as block:
            @block.sync
            def _(sp):
                for dst, src in ((w[:], g.wqkv[layer]), (wo[:], g.wo[layer]), (rot[:], g.rotary), (mask[:], g.band)):
                    sp.dma_start(dst, src).then_inc(loaded, 16)
                for n, src in enumerate((g.q_scale, g.k_scale)):
                    sp.dma_start(scale_rows[:, n, :], src[layer].partition_broadcast(P)).then_inc(loaded, 16)

            @block.gpsimd
            def _(pool):
                pool.memset(half[:], 0.5)
                for t in probs + [k_T[3], v[3]]:
                    last = pool.memset(t[:], 0.0)
                last.then_inc(ready, 1)

                def take(b, t):
                    pool.tensor_copy(h_tile[t % 2][:], g.zA[:, ds(b, 1), ds(t * P, P)].rearrange("p a t -> p (a t)"))\
                        .then_inc(h_done, 1)

                def front(n, nxt, turns_before):
                    pool.wait_ge(sum_done, n + 1)
                    settle(pool, held)
                    pool.tensor_tensor(norm[:], norm[:], half[:], ALU.pow).then_inc(root_done, 1)
                    if nxt is not None:
                        pool.wait_ge(qkv_done, n + 1)
                        take(*nxt)
                    pool.wait_ge(rotate_done, n + 2)
                    settle(pool, held)
                    if turns_before is not None:
                        pool.wait_ge(turn_done, turns_before)
                        settle(pool, held)
                    pool.tensor_tensor(rotated[:], by_cos[:], by_sin[:], ALU.add).then_inc(pool_step, 1)
                    pool.wait_ge(pool_step, n + 1)
                    pool.wait_ge(inv_done, n + 1)
                    settle(pool, held)
                    pool.tensor_tensor(rotated[:], rotated[:], inv_norm[:].unsqueeze(2).to_broadcast([P, 16, LDH]),
                                       ALU.mult).then_inc(rotated_done, 1)

                take(0, 0)
                take(0, 1)
                front(0, (0, 2), None)
                with pool.Fori(0, BATCH) as b:
                    for t in range(TB):
                        b2 = b if t + 3 < TB else (b + 1) % BATCH
                        front(b * TB + t + 1, (b2, (t + 3) % TB), b * USES + use(t, G0) + 1)

            @block.tensor
            def _(pe):
                pe.wait_ge(loaded, 96)
                pe.wait_ge(ready, 1)
                pe.sem_inc(product_done, 2)

                def qkv(n, t):
                    pe.wait_ge(h_done, n + 1)
                    pe.wait_ge(rotate_done, n + 1)
                    pe.wait_ge(v_done, n + 1)
                    pe.wait_ge(square_done, n + 1)
                    for a in range(3):
                        mm = pe.matmul(g.ps[:, a, :], h_tile[t % 2][:], w[:, a * INNER:(a + 1) * INNER], start=True, stop=True)
                    mm.then_inc(qkv_done, 1)

                def scores(b, t, s):
                    pe.wait_ge(probs_done, b * 2 * TB + 2 * t + s + 1)
                    pe.wait_ge(out5, b * USES + use(t, G0) + 1)
                    pe.wait_ge(out6, b * USES + use(t, G0) + 1)
                    for j in range(G):
                        h = s * G + j
                        r = slice(64 * (h % 2), 64 * (h % 2) + 64)
                        for prev in range(2):
                            keys = k_T[(t - 1 + prev) % 4]
                            col = j // 2 * 2 * P + prev * P
                            mm = pe.matmul(g.ps[:, 3 + j % 2, col:col + P], q_T[t % 2][r, h // 2, :],
                                           keys[r, h // 2, :], start=True, stop=True)
                    mm.then_inc(scores_done, 1)

                def banks_free(b, t, k):
                    n = b * USES + use(t, k) + 1
                    pe.wait_ge(out5, n)
                    pe.wait_ge(out6, n)

                def turn(b, t, s):
                    banks_free(b, t, G0 if s == 0 else G1)
                    pe.wait_ge(probs_done, b * 2 * TB + 2 * t + s + 2)
                    for j in range(G):
                        for prev in range(2):
                            col = j * 2 * P + prev * P
                            mm = pe.transpose(g.ps[:, 5 + col // BANK, col % BANK:col % BANK + P],
                                              probs[s][:, j, prev * P:(prev + 1) * P], g.ident[:])
                    mm.then_inc(turn_done, 1)

                def product(b, t, s):
                    n = b * USES + use(t, (G0, G1)[s]) + 2
                    pe.wait_ge(out5, n)
                    pe.wait_ge(out6, n)
                    pe.wait_ge(v_done, b * TB + t + 2)
                    if s == 0:
                        pe.wait_ge(norm_out, b * TB + t + 1)
                    for j in range(G):
                        h = s * G + j
                        for prev in range(2):
                            col = j * 2 * P + prev * P
                            mm = pe.matmul(g.ps[:, 7, h * LDH:(h + 1) * LDH],
                                           probs_T[s][:, col // BANK, col % BANK:col % BANK + P],
                                           v[(t - 1 + prev) % 4][:, h * LDH:(h + 1) * LDH], start=(prev == 0), stop=(prev == 1))
                    mm.then_inc(product_done, 1)

                def back(b, t, at_use):
                    pe.wait_ge(out5, b * USES + at_use + 1)
                    pe.wait_ge(out6, b * USES + at_use + 1)
                    pe.wait_ge(norm_out, b * TB + t + 2)
                    for j in range(4):
                        mm = pe.transpose(g.ps[:, 5, j * P:(j + 1) * P], out[:, j * P:(j + 1) * P], g.ident[:])
                    mm.then_inc(turn_done, 1)
                    pe.wait_ge(out5, b * USES + at_use + 2)
                    for j in range(4):
                        mm = pe.matmul(g.ps[:, 6, 0:P], wo[:, j, :], out_T[:, j, :], start=(j == 0), stop=(j == 3))
                    mm.then_inc(proj_done, 1)

                def front_turn(n, free):
                    pe.wait_ge(rotated_done, n + 1)
                    if free is not None:
                        banks_free(*free)
                    for a in range(2):
                        for j in range(4):
                            mm = pe.transpose(g.ps[:, 5 + a, j * P:(j + 1) * P],
                                              rotated[:, 8 * a + 2 * j:8 * a + 2 * j + 2, :].rearrange("p h d -> p (h d)"),
                                              g.ident[:])
                    mm.then_inc(turn_done, 1)

                qkv(0, 0)
                front_turn(0, None)
                with pe.Fori(0, BATCH) as b:
                    for t in range(TB):
                        n = b * TB + t + 1
                        scores(b, t, 0)
                        qkv(n, t + 1)
                        turn(b, t, 0)
                        scores(b, t, 1)
                        product(b, t, 0)
                        if t:
                            back(b, t - 1, use(t, BACK))
                        turn(b, t, 1)
                        front_turn(n, (b, t, FRONT))
                        product(b, t, 1)
                    back(b, TB - 1, USES - 1)

            @block.scalar
            def _(act):
                act.sem_inc(square_done, 1)
                act.sem_inc(v_done, 1)
                act.sem_inc(probs_done, 1)

                def front(n, t):
                    act.wait_ge(qkv_done, n + 1)
                    if not isinstance(n, int):
                        act.wait_ge(sum_done, n)
                    act.activation(squares[:], qk_banks, ACT.Square).then_inc(square_done, 1)
                    if not isinstance(n, int):
                        act.wait_ge(product_done, n * 2 - 2)
                    act.activation(v[t % 4][:], g.ps[:, 2, :], ACT.Copy).then_inc(v_done, 1)

                def exps(b, t, s):
                    i = b * 2 * TB + 2 * t + s
                    act.wait_ge(min_done, i + 1)
                    act.wait_ge(turn_done, b * USES + use(t, G0) + 1)
                    for j in range(G):
                        mm = act.activation(probs[s][:, j, 64:], g.ps[:, 3 + j % 2, j // 2 * 256 + 64:j // 2 * 256 + 256], ACT.Exp,
                                            bias=row_min[:, s, j:j + 1], scale=-1.0,
                                            accum_out=row_sum[:, t % 2, s * G + j:s * G + j + 1])
                    mm.then_inc(probs_done, 1)

                def evacuate(b, at_use, dst):
                    act.wait_ge(turn_done, b * USES + at_use + 2)
                    act.activation(dst, g.ps[:, 6, :], ACT.Copy).then_inc(out6, 1)

                def group_out(b, t, s):
                    act.wait_ge(product_done, b * 2 * TB + 2 * t + s + 1)
                    evacuate(b, use(t, (G0, G1)[s]), probs_T[s][:, 1, :])

                flat = lambda t4: t4[:].rearrange("p j t -> p (j t)")
                front(0, 0)
                act.wait_ge(turn_done, 1)
                act.activation(flat(k_T[0]), g.ps[:, 6, :], ACT.Copy).then_inc(out6, 1)
                with act.Fori(0, BATCH) as b:
                    for t in range(TB):
                        exps(b, t, 0)
                        front(b * TB + t + 1, t + 1)
                        group_out(b, t, 0)
                        exps(b, t, 1)
                        group_out(b, t, 1)
                        evacuate(b, use(t, FRONT), flat(k_T[(t + 1) % 4]))

            @block.vector
            def _(dve):
                dve.wait_ge(loaded, 96)
                for a in range(2):
                    sc = scale_rows[:, a, :]
                    for h in range(2):
                        d, o = slice(32 * h, 32 * h + 32), slice(32 - 32 * h, 64 - 32 * h)
                        last = dve.tensor_tensor(rot[:, :, a, 1, d], rot[:, :, a, 1, d], sc[:, o].unsqueeze(1).to_broadcast([P, TB, 32]), ALU.mult)
                    last = dve.tensor_tensor(rot[:, :, a, 0, :], rot[:, :, a, 0, :], sc.unsqueeze(1).to_broadcast([P, TB, LDH]), ALU.mult)
                last.then_inc(tables, 1)
                dve.wait_ge(tables, 1)
                dve.tensor_scalar(rot[:, :, 0], rot[:, :, 0], -8.0, None, ALU.mult).then_inc(tables, 1)
                dve.wait_ge(tables, 2)
                dve.sem_inc(rotate_done, 1)
                dve.sem_inc(norm_out, 1)

                def front_sum(n, t):
                    dve.wait_ge(square_done, n + 2)
                    dve.tensor_reduce(norm[:], heads_of(squares[:]), AX, ALU.add).then_inc(sum_done, 1)
                    if not isinstance(n, int):
                        dve.wait_ge(pool_step, n)
                    wide = [P, 8, LDH]
                    for a in range(2):
                        qk = heads_of(g.ps[:, a, :])
                        dve.tensor_tensor(by_cos[:, 8 * a:8 * a + 8, :], qk, rot[:, t % TB, a, 0, :].unsqueeze(1).to_broadcast(wide), ALU.mult)
                        for h in range(2):
                            d, o = slice(32 * h, 32 * h + 32), slice(32 - 32 * h, 64 - 32 * h)
                            last = dve.tensor_tensor(by_sin[:, 8 * a:8 * a + 8, d], qk[:, :, o],
                                                     rot[:, t % TB, a, 1, d].unsqueeze(1).to_broadcast([P, 8, 32]), ALU.mult)
                    last.then_inc(rotate_done, 1)

                def front_inv(n):
                    dve.wait_ge(root_done, n + 1)
                    if not isinstance(n, int):
                        dve.wait_ge(rotated_done, n)
                    dve.tensor_scalar(inv_norm[:], norm[:], 1e-12, None, ALU.max).then_inc(sum_inv, 1)
                    dve.wait_ge(sum_inv, n + 1)
                    dve.reciprocal(inv_norm[:], inv_norm[:]).then_inc(inv_done, 1)

                def mins(b, t, s):
                    dve.wait_ge(scores_done, b * 2 * TB + 2 * t + s + 1)
                    settle(dve, held)
                    for j in range(G):
                        sc = g.ps[:, 3 + j % 2, j // 2 * 256 + 64:j // 2 * 256 + 256]
                        last = dve.tensor_tensor_reduce(out=sc, in0=sc, in1=mask[:, min(t, 1), :], scale=1.0, scalar=3e38,
                                                        op0=ALU.add, op1=ALU.min, accum_out=row_min[:, s, j:j + 1])
                    last.then_inc(min_done, 1)

                def evacuate(b, at_use, dst):
                    dve.wait_ge(turn_done, b * USES + at_use + 2)
                    dve.tensor_copy(dst, g.ps[:, 5, :]).then_inc(out5, 1)

                def group_out(b, t, s):
                    dve.wait_ge(product_done, b * 2 * TB + 2 * t + s + 1)
                    evacuate(b, use(t, (G0, G1)[s]), probs_T[s][:, 0, :])

                def normalise(b, t):
                    dve.wait_ge(probs_done, b * 2 * TB + 2 * t + 3)
                    dve.reciprocal(inv_sum[:], row_sum[:, t % 2, :]).then_inc(inv_sum_done, 1)
                    dve.wait_ge(product_done, b * 2 * TB + 2 * t + 4)
                    dve.wait_ge(inv_sum_done, b * TB + t + 1)
                    dve.tensor_tensor(heads_of(out[:]), heads_of(g.ps[:, 7, :]), inv_sum[:].unsqueeze(2).to_broadcast([P, 8, LDH]),
                                      ALU.mult).then_inc(norm_out, 1)

                def back(b, t, at_use):
                    evacuate(b, at_use, out_T[:].rearrange("p j t -> p (j t)"))
                    dve.wait_ge(proj_done, b * TB + t + 1)
                    for rows in (TOP, LOW):
                        last = dve.tensor_tensor(shifted(g.zB, rows, b, t * P, P), shifted(g.zA, rows, b, t * P, P),
                                                 g.ps[rows, 6, 0:P], ALU.add)
                    last.then_inc(out6, 1)

                flat = lambda t4: t4[:].rearrange("p j t -> p (j t)")
                front_sum(0, 0)
                front_inv(0)
                dve.wait_ge(turn_done, 1)
                dve.tensor_copy(flat(q_T[0]), g.ps[:, 5, :]).then_inc(out5, 1)
                with dve.Fori(0, BATCH) as b:
                    for t in range(TB):
                        n = b * TB + t + 1
                        mins(b, t, 0)
                        front_sum(n, t + 1)
                        group_out(b, t, 0)
                        mins(b, t, 1)
                        if t:
                            back(b, t - 1, use(t, BACK))
                        front_inv(n)
                        group_out(b, t, 1)
                        evacuate(b, use(t, FRONT), flat(q_T[(t + 1) % 2]))
                        normalise(b, t)
                    back(b, TB - 1, USES - 1)


def mlp(nc, g, layer):
    stage_sems = []
    with ExitStack() as ctx:
        ctx.callback(give_back, nc, stage_sems)

        def sb(name, shape, dt=F32):
            return ctx.enter_context(nc.sbuf_tensor(f"m{layer}_{name}", shape, dt))

        def sem(name):
            return kept(nc, stage_sems, f"m{layer}_{name}")

        CHUNKS = TOKENS // BANK
        SIZES = (P, P, LHID - 2 * P)
        w1 = sb("w1", [P, 2 * LHID])
        w1_scaled = sb("w1_scaled", [P, 2 * LHID])
        w2 = sb("w2", [P, 3, DIM])
        b1 = sb("b1", [P, 2, 3])
        cols = sb("cols", [P, 3])
        mean_of = sb("mean_of", [P, P])
        centred = sb("centred", [P, BANK])
        squares = sb("squares", [P, BANK])
        variance = sb("variance", [P, BANK])
        std = sb("std", [P, BANK])
        rstd = sb("rstd", [P, BANK])
        normed = [sb(f"normed{n}", [P, BANK]) for n in range(2)]
        gelu = [sb(f"gelu{n}", [P, BANK]) for n in range(2)]
        hidden = [sb(f"hidden{n}", [P, BANK]) for n in range(3)]
        loaded, ready, shift_mm, folded = sem("loaded"), sem("ready"), sem("shift_mm"), sem("folded")
        mean_done, centred_done, square_done, var_done, eps_done, std_done, rstd_done, normed_done = map(sem, (
            "mean_done", "centred_done", "square_done", "var_done", "eps_done", "std_done", "rstd_done", "normed_done"))
        up_done, gelu_done, hidden_done, down_done, z_done, held = map(sem, (
            "up_done", "gelu_done", "hidden_done", "down_done", "z_done", "held"))

        def unit_cols(k, j):
            start = k * LHID + j * P
            return slice(start, start + SIZES[j])

        def z_shifted(z, c):
            return z[:, ds(c // 2, 1), ds((c % 2) * BANK, BANK)].rearrange("p a t -> p (a t)")

        with nc.Block() as block:
            @block.sync
            def _(sp):
                for dst, src in ((w1[:], g.mw1[layer]), (w2[:], g.mw2[layer]), (b1[:], g.mb1[layer]), (cols[:], g.mcols[layer])):
                    sp.dma_start(dst, src).then_inc(loaded, 16)

            @block.gpsimd
            def _(pool):
                pool.memset(mean_of[:], 1.0 / DIM).then_inc(ready, 1)

            @block.tensor
            def _(pe):
                def mean(n, c):
                    pe.wait_ge(centred_done, n + 1)
                    pe.matmul(g.ps[:, 0, :], mean_of[:], z_shifted(g.zB, c), start=True, stop=True).then_inc(mean_done, 1)

                def var(n):
                    pe.wait_ge(square_done, n + 1)
                    pe.wait_ge(eps_done, n + 1)
                    pe.matmul(g.ps[:, 1, :], mean_of[:], squares[:], start=True, stop=True).then_inc(var_done, 1)

                def up(c, u, j):
                    i = 3 * u + j
                    pe.wait_ge(normed_done, c + 1)
                    pe.wait_ge(hidden_done, c * 3 + j + 1)
                    for k in range(2):
                        mm = pe.matmul(g.ps[0:SIZES[j], 2 + 2 * k + i % 2, :], w1_scaled[:, unit_cols(k, j)], normed[u][:],
                                       start=True, stop=True)
                    mm.then_inc(up_done, 1)

                def down(c, u, j):
                    pe.wait_ge(hidden_done, c * 3 + j + 3)
                    if j == 0:
                        pe.wait_ge(z_done, c + 1)
                    pe.matmul(g.ps[:, 6 + u, :], w2[0:SIZES[j], j, :], hidden[j][0:SIZES[j], :], start=(j == 0),
                              stop=(j == 2)).then_inc(down_done, 1)

                pe.sem_inc(down_done, 3)
                pe.wait_ge(loaded, 64)
                pe.wait_ge(ready, 1)
                for k in range(2):
                    for j in range(3):
                        mm = pe.matmul(g.ps[0:SIZES[j], 7, 3 * k + j:3 * k + j + 1], w1[:, unit_cols(k, j)], cols[:, 1:2],
                                       start=True, stop=True)
                mm.then_inc(shift_mm, 1)
                pe.wait_ge(folded, 1)
                mean(0, 0)
                var(0)
                with pe.Fori(0, CHUNKS // 2) as cc:
                    for u in range(2):
                        c = cc * 2 + u
                        up(c, u, 0)
                        mean(c + 1, (c + 1) % CHUNKS)
                        up(c, u, 1)
                        down(c, u, 0)
                        up(c, u, 2)
                        down(c, u, 1)
                        var(c + 1)
                        down(c, u, 2)

            @block.scalar
            def _(act):
                def square(n):
                    act.wait_ge(centred_done, n + 2)
                    if not isinstance(n, int):
                        act.wait_ge(var_done, n)
                    act.activation(squares[:], centred[:], ACT.Square).then_inc(square_done, 1)

                def root(n):
                    act.wait_ge(eps_done, n + 2)
                    act.activation(std[:], variance[:], ACT.Sqrt).then_inc(std_done, 1)

                def gate(c, u, j):
                    i = 3 * u + j
                    act.wait_ge(up_done, c * 3 + j + 1)
                    rows = slice(0, SIZES[j])
                    act.activation(gelu[i % 2][rows, :], g.ps[rows, 4 + i % 2, :], ACT.Gelu, bias=b1[rows, 1, j:j + 1])\
                       .then_inc(gelu_done, 1)

                square(0)
                root(0)
                with act.Fori(0, CHUNKS // 2) as cc:
                    for u in range(2):
                        c = cc * 2 + u
                        gate(c, u, 0)
                        square(c + 1)
                        gate(c, u, 1)
                        gate(c, u, 2)
                        root(c + 1)

            @block.vector
            def _(dve):
                dve.sem_inc(eps_done, 1)
                dve.sem_inc(hidden_done, 2)
                dve.sem_inc(z_done, 2)
                dve.wait_ge(loaded, 64)
                dve.tensor_scalar(w1_scaled[:], w1[:], cols[:, 0:1], None, ALU.mult)
                dve.wait_ge(shift_mm, 1)
                shifts = g.ps[:, 7, 0:6].rearrange("p (k j) -> p k j", k=2)
                last_rows = slice(0, SIZES[2])
                dve.tensor_tensor(b1[:, :, 0:2], b1[:, :, 0:2], shifts[:, :, 0:2], ALU.add)
                dve.tensor_tensor(b1[last_rows, :, 2:3], b1[last_rows, :, 2:3], shifts[last_rows, :, 2:3], ALU.add)\
                   .then_inc(folded, 1)
                dve.wait_ge(folded, 1)
                dve.sem_inc(centred_done, 1)

                def centre(n, c):
                    dve.wait_ge(mean_done, n + 1)
                    dve.tensor_tensor(centred[:], z_shifted(g.zB, c), g.ps[:, 0, :], ALU.subtract).then_inc(centred_done, 1)

                def norm(n, u):
                    dve.wait_ge(var_done, n + 1)
                    dve.tensor_scalar(variance[:], g.ps[:, 1, :], EPS, None, ALU.add).then_inc(eps_done, 1)
                    dve.wait_ge(std_done, n + 1)
                    dve.reciprocal(rstd[:], std[:]).then_inc(rstd_done, 1)
                    dve.wait_ge(rstd_done, n + 1)
                    dve.tensor_tensor(normed[u][:], centred[:], rstd[:], ALU.mult).then_inc(normed_done, 1)

                def multiply(c, u, j):
                    i = 3 * u + j
                    rows = slice(0, SIZES[j])
                    dve.wait_ge(gelu_done, c * 3 + j + 1)
                    dve.wait_ge(down_done, c * 3 + j + 1)
                    dve.scalar_tensor_tensor(hidden[j][rows, :], g.ps[rows, 2 + i % 2, :], b1[rows, 0, j:j + 1],
                                             gelu[i % 2][rows, :], ALU.add, ALU.mult).then_inc(hidden_done, 1)

                def add(c, u):
                    dve.wait_ge(down_done, c * 3 + 6)
                    for rows in (TOP, LOW):
                        t0 = (c % 2) * BANK
                        last = dve.scalar_tensor_tensor(shifted(g.zA, rows, c // 2, t0, BANK), g.ps[rows, 6 + u, :], cols[rows, 2:3],
                                                        shifted(g.zB, rows, c // 2, t0, BANK), ALU.add, ALU.add)
                    last.then_inc(z_done, 1)

                centre(0, 0)
                norm(0, 0)
                with dve.Fori(0, CHUNKS // 2) as cc:
                    for u in range(2):
                        c = cc * 2 + u
                        centre(c + 1, (c + 1) % CHUNKS)
                        multiply(c, u, 0)
                        multiply(c, u, 1)
                        multiply(c, u, 2)
                        norm(c + 1, 1 - u)
                        add(c, u)


def clear_first_token(nc, g):
    with nc.Block() as block:
        @block.gpsimd
        def _(pool):
            for z in (g.zA, g.zB):
                pool.memset(z[LOW, :, 0:1], 0.0)


def finish(nc, g):
    stage_sems = []
    with ExitStack() as ctx:
        ctx.callback(give_back, nc, stage_sems)

        def sem(name):
            return kept(nc, stage_sems, "f_" + name)

        gated = [ctx.enter_context(nc.sbuf_tensor(f"f_gated{n}", [P, 4, DIM], F32)) for n in range(2)]
        turned, scaled, added, stored = map(sem, ("turned", "scaled", "added", "stored"))
        CHUNKS = TOKENS // BANK
        with nc.Block() as block:
            @block.tensor
            def _(pe):
                for c in range(CHUNKS):
                    if c >= 4:
                        pe.wait_ge(scaled, c - 3)
                    for t in range(4):
                        b, t0 = c // 2, (c % 2) * BANK + t * P
                        for n, (rows, lag) in enumerate(((TOP, 0), (LOW, 1))):
                            mm = pe.transpose(g.ps[:, 2 * (c % 4) + n, t * 64:t * 64 + 64],
                                              g.zA[rows, b, t0 + lag:t0 + lag + P], g.ident[rows, rows])
                    mm.then_inc(turned, 1)

            @block.vector
            def _(dve):
                for c in range(CHUNKS):
                    dve.wait_ge(turned, c + 1)
                    for n, feats in enumerate((TOP, LOW)):
                        last = dve.tensor_tensor(gated[c % 2][:, :, feats], g.ps[:, 2 * (c % 4) + n, 0:256].rearrange("p (t d) -> p t d", t=4),
                                                 g.gate_rows[:, 1, 1, c // 2:c // 2 + 1, feats].to_broadcast([P, 4, 64]), ALU.mult)
                    last.then_inc(scaled, 1)
                    dve.wait_ge(scaled, c + 1)
                    rowsx = g.x[:, 4 * c:4 * c + 4, :]
                    dve.tensor_tensor(rowsx, rowsx, gated[c % 2][:], ALU.add).then_inc(added, 1)

            @block.sync
            def _(sp):
                for c in range(CHUNKS):
                    sp.wait_ge(added, c + 1)
                    sp.dma_start(g.out[c // 2, :, 4 * (c % 2):4 * (c % 2) + 4, :], g.x[:, 4 * c:4 * c + 4, :]).then_inc(stored, 16)
                sp.wait_ge(stored, 16 * CHUNKS)


def program(nc, g, stages=("l0a", "l0f", "l1a", "l1f")):
    with ExitStack() as ctx:
        allocate(nc, ctx, g)
        g.qk_dram = nc.dram_tensor("qk_dram", [3, 2, P, TOKENS], BF16, kind="Internal").ap()
        g.bias_dram_t = nc.dram_tensor("bias_dram", [HEADS, 384], F32, kind="Internal")
        g.bias_dram = g.bias_dram_t.ap()

        g.toeplitz_src = bass.AP(g.bias_dram_t, 0, [[1, P], [384, HEADS], [1, 2 * P]])
        with ExitStack() as first:
            g.toeplitz_all = first.enter_context(nc.sbuf_tensor("toeplitz_all", [P, HEADS, 2 * P], F32))
            g.ga_bo = first.enter_context(nc.sbuf_tensor("ga_bo", [P, BATCH, DIM], F32))
            g.v_all = first.enter_context(nc.sbuf_tensor("v_all", [P, TILES, DIM], F32))
            setup(nc, g)
            if "l0a" in stages:
                norm_modulate(nc, g, 0, 0, add_ga_bo=True)
                split_project(nc, g)
                attention(nc, g, 0)
        if "l0f" in stages:
            norm_modulate(nc, g, 0, 1)
            experts(nc, g)
        if "l1a" in stages:
            norm_modulate(nc, g, 1, 0)
            attention(nc, g, 1)
        if "l1f" in stages:
            g.zA = ctx.enter_context(nc.sbuf_tensor("zA", [P, BATCH, SEQ + 1], F32))
            g.zB = ctx.enter_context(nc.sbuf_tensor("zB", [P, BATCH, SEQ + 1], F32))
            clear_first_token(nc, g)
            norm_modulate(nc, g, 1, 1, shift=True)
            for layer in range(LDEPTH):
                local_attention(nc, g, layer)
                mlp(nc, g, layer)
            finish(nc, g)
        else:
            store(nc, g)


def store(nc, g):
    stored = nc.alloc_semaphore("stored")
    with nc.Block() as block:
        @block.sync
        def _(sp):
            for b in range(BATCH):
                sp.dma_start(g.out[b], g.x[:, b * TB:(b + 1) * TB, :]).then_inc(stored, 16)
            sp.wait_ge(stored, 16 * BATCH)


def lay_out(inputs):
    f = {k: np.ascontiguousarray(v) for k, v in inputs.items()}
    a = {}
    a["x_in"] = f["L0_attn_x"].reshape(BATCH, TB, P, DIM).transpose(0, 2, 1, 3)
    a["cT"] = np.stack([f["L0_c"].T, f["L1_c"].T], 1)
    a["wmod"] = np.stack([f["L0_wmod"], f["L1_wmod"]], 1)
    a["bo"] = f["L0_attn_bo"]
    a["rel_emb"] = f["L0_attn_rel_emb"]
    a["ident_in"] = np.eye(P, dtype=np.float32)
    a["flip_in"] = np.eye(P, dtype=np.float32)[::-1]
    a["bias_sel"] = bias_selector()
    a["w0_qkv"] = np.stack([f["L0_attn_Wq"], f["L0_attn_Wk"], f["L0_attn_Wv"]], 1)
    a["w0_out"] = f["L0_attn_Wo"]
    a["w1_qk"] = np.stack([f["L1_attn_Wq"], f["L1_attn_Wk"]])
    def hidden_first(w):
        return w.transpose(2, 0, 1)

    a["w1"] = hidden_first(f["L0_ffn_W1"])
    a["w3"] = hidden_first(f["L0_ffn_W3"])
    a["w2"] = f["L0_ffn_W2"].transpose(2, 0, 1).reshape(2, P, EXPERTS, DIM).transpose(1, 2, 0, 3)
    a["lora_a"] = np.stack([f["L0_ffn_A1"], f["L0_ffn_A3"]]).transpose(2, 0, 1, 3)
    a["lora_b"] = np.stack([f["L0_ffn_B1"], f["L0_ffn_B3"]]).transpose(3, 0, 1, 2)
    a["lora_a2"] = f["L0_ffn_A2"].transpose(1, 0, 2)
    a["lora_b2"] = f["L0_ffn_B2"].transpose(2, 0, 1)
    a["w_gate"] = f["L0_ffn_Wg"].T
    a["iota"] = np.tile(np.arange(EXPERTS, dtype=np.float32), (P, 1))
    a["b13"] = np.stack([f["L0_ffn_b1"], f["L0_ffn_b3"]]).reshape(2, EXPERTS, 2, P).transpose(3, 0, 1, 2)
    a["b2"] = f["L0_ffn_b2"]
    a["wqkv"] = f["L1_ffn_wqkv"]
    a["wo"] = f["L1_ffn_wo"].reshape(LDEPTH, 4, P, DIM).transpose(0, 2, 1, 3)
    a["q_scale"], a["k_scale"] = f["L1_ffn_q_scale"], f["L1_ffn_k_scale"]
    a["rotary"] = rotary_tables().reshape(2, 2, TB, P, LDH).transpose(3, 2, 0, 1, 4)
    band = band_mask()[:, 64:]
    no_past = band.copy()
    no_past[:, :64] = BIG
    a["band"] = np.stack([no_past, band], 1)
    a["mw1"] = f["L1_ffn_w1"]
    def hidden_tiles(w):
        out = np.zeros((w.shape[0], 3 * P, w.shape[2]), w.dtype)
        out[:, :LHID] = w
        return out.reshape(w.shape[0], 3, P, w.shape[2]).transpose(0, 2, 1, 3)

    a["mw2"] = hidden_tiles(f["L1_ffn_w2"])
    a["mb1"] = hidden_tiles(f["L1_ffn_b1"].reshape(LDEPTH, 2, LHID).transpose(0, 2, 1)).transpose(0, 1, 3, 2)
    a["mcols"] = np.stack([f["L1_ffn_ln_g"], f["L1_ffn_ln_b"], f["L1_ffn_b2"]], -1)
    a["w1_v"] = f["L1_attn_Wv"]
    a["w1_out"] = f["L1_attn_Wr"]
    return {k: np.ascontiguousarray(v) for k, v in a.items()}


_OUT = (BATCH, P, TB, DIM)


def kernel(**inputs):
    import numpy as _np
    import concourse.bacc as _bacc
    from concourse import mybir as _mybir
    from concourse.bass_utils import run_bass_kernel_spmd as _run

    nc = _bacc.Bacc("TRN2", target_bir_lowering=False, num_devices=1)
    arrays = lay_out(inputs)
    chip = Chip()
    fed = {}
    for name, a in arrays.items():
        fed[f"in_{name}"] = a
        chip.__dict__[name] = nc.dram_tensor(f"in_{name}", a.shape, _mybir.dt.from_np(a.dtype), kind="ExternalInput").ap()
    chip.out = nc.dram_tensor("out_0_dram", _OUT, _mybir.dt.float32, kind="ExternalOutput").ap()
    program(nc, chip)
    r = _run(nc, [fed], core_ids=[0])
    got = r.results[0]["out_0_dram"]
    return _np.ascontiguousarray(got.reshape(_OUT).transpose(0, 2, 1, 3).reshape(BATCH, SEQ, DIM))
```

```python
import math
from contextlib import ExitStack

import numpy as np

import concourse.bass as bass
from concourse import mybir

F32 = mybir.dt.float32
F32R = mybir.dt.float32r
BF16 = mybir.dt.bfloat16
U32 = mybir.dt.uint32
ALU = mybir.AluOpType
ACT = mybir.ActivationFunctionType
AX = mybir.AxisListType.X
ds = bass.ds

P = 128
BATCH, SEQ, DIM = 4, 1024, 128
TOKENS = BATCH * SEQ
TILES = TOKENS // P
TB = SEQ // P
BANK = 512
HEADS = 16
PAIRS = BATCH * HEADS // 2
HI_BITS = 0xFFFFF000
BIG = 1e30
BUCKETS, MAX_DISTANCE = 32, 128
EXPERTS, HIDDEN, RANK = 8, 256, 16
LDEPTH, LHEADS, LDH, LWIN = 2, 8, 64, 64
INNER = LHEADS * LDH
LHID = int(DIM * 4 * 2 / 3)
EPS = 1e-5



def bias_selector():
    n = 255 - np.arange(384)
    exact = BUCKETS // 2
    pos = np.maximum(n, 1).astype(np.float32)
    large = exact + (np.log(pos / exact) / np.float32(math.log(MAX_DISTANCE / exact)) * (BUCKETS - exact)).astype(np.int32)
    bucket = np.where(n < exact, np.maximum(n, 0), np.minimum(large, BUCKETS - 1))
    sel = np.zeros((BUCKETS + 1, 384), np.float32)
    sel[bucket, np.arange(384)] = -1.0
    sel[BUCKETS - 1] += 1.0
    sel[:, n < 0] = 0.0
    sel[BUCKETS, n < 0] = BIG
    return sel


def rotary_tables():
    half = np.arange(0, LDH, 2, dtype=np.float32)
    inv = (1.0 / 10000.0 ** (half / LDH)).astype(np.float32)
    t = np.arange(SEQ, dtype=np.float32)
    f = (t[:, None] * inv[None, :]).astype(np.float32)
    f = np.concatenate([f, f], -1)
    base = ((half + 0.4 * LDH) / (1.4 * LDH)).astype(np.float32)
    power = ((t - SEQ // 2) / float(LWIN // 2)).astype(np.float32)
    s = (base[None, :] ** power[:, None]).astype(np.float32)
    s = np.concatenate([s, s], -1)
    sign = np.where(np.arange(LDH) < LDH // 2, -1.0, 1.0).astype(np.float32)
    c, n = np.cos(f), np.sin(f) * sign
    return np.stack([c * s, n * s, c / s, n / s]).astype(np.float32)


def band_mask():
    d = np.arange(P)[:, None] + P - np.arange(2 * P)[None, :]
    return np.where((d >= 0) & (d <= LWIN), 0.0, BIG).astype(np.float32)


class Chip:
    pass


def allocate(nc, ctx, g):
    def sb(name, shape, dt=F32):
        return ctx.enter_context(nc.sbuf_tensor(name, shape, dt))

    g.x = sb("x", [P, TILES, DIM])
    g.hT = sb("hT", [P, TOKENS])
    g.ident = sb("ident", [P, P])
    g.mod_cols = sb("mod_cols", [P, 2, 6, BATCH])
    g.gate_rows = sb("gate_rows", [P, 2, 2, BATCH, DIM])
    g.ps = ctx.enter_context(nc.psum_tensor("ps", [P, 8, BANK], F32))


def kept(nc, stage_sems, name):
    stage_sems.append(nc.alloc_semaphore(name))
    return stage_sems[-1]


def give_back(nc, stage_sems):
    nc.clear_and_free_semaphores(stage_sems)
    nc.all_engine_barrier()


def setup(nc, g):
    stage_sems = []
    with ExitStack() as ctx:
        ctx.callback(give_back, nc, stage_sems)

        def sb(name, shape, dt=F32):
            return ctx.enter_context(nc.sbuf_tensor(name, shape, dt))

        def sem(name):
            return kept(nc, stage_sems, name)

        cT = sb("cT", [P, 2, BATCH])
        silu_c = sb("silu_c", [P, 2, BATCH])
        silu_wide = sb("silu_wide", [P, 2, BATCH, P])
        wmod = sb("wmod", [P, 2, 6 * DIM])
        gabs = sb("gabs", [P, 2 * BATCH * DIM])
        gsgn = sb("gsgn", [P, 2 * BATCH * DIM])
        raw = sb("raw", [P, 2 * BATCH * DIM])
        rel = sb("rel", [BUCKETS + 1, HEADS])
        sel = sb("sel", [BUCKETS + 1, 384])
        bias_sb = sb("bias_sb", [HEADS, 384])
        bo_row = sb("bo_row", [P, DIM])
        mirrored = sb("mirrored", [P, HEADS, 2 * P])
        mirrored_in, flip_mm, flip_out = sem("set_mirrored_in"), sem("set_flip_mm"), sem("set_flip_out")
        flip = sb("flip", [P, P])
        FLIPS = HEADS * 2 * P // BANK
        loaded, bias_loaded, rel_one, silu_done, wide, mod_mm, mod_out, bias_out, stored, step = map(sem, (
            "set_loaded", "set_bias_loaded", "set_rel_one", "set_silu", "set_wide", "set_mod_mm",
            "set_mod_out", "set_bias_out", "set_stored", "set_step"))
        with nc.Block() as block:
            @block.sync
            def _(sp):
                sp.dma_start(cT[:], g.cT).then_inc(loaded, 16)
                sp.dma_start(wmod[:], g.wmod).then_inc(loaded, 16)
                sp.dma_start(g.ident[:], g.ident_in).then_inc(loaded, 16)
                sp.dma_start(flip[:], g.flip_in).then_inc(loaded, 16)
                sp.dma_start(bo_row[:], g.bo.partition_broadcast(P)).then_inc(loaded, 16)
                sp.dma_start(rel[0:BUCKETS, :], g.rel_emb).then_inc(bias_loaded, 16)
                sp.dma_start(sel[:], g.bias_sel).then_inc(bias_loaded, 16)
                for b in range(BATCH):
                    sp.dma_start(g.x[:, b * TB:(b + 1) * TB, :], g.x_in[b]).then_inc(loaded, 16)
                sp.wait_ge(bias_out, 1)
                sp.dma_start(g.bias_dram, bias_sb[:]).then_inc(stored, 16)
                sp.wait_ge(stored, 16)
                sp.dma_start(mirrored[:], g.toeplitz_src).then_inc(mirrored_in, 16)
                sp.wait_ge(loaded, 16 * 9)

            @block.gpsimd
            def _(pool):
                pool.memset(rel[BUCKETS:BUCKETS + 1, :], 1.0).then_inc(rel_one, 1)

            @block.scalar
            def _(act):
                act.wait_ge(loaded, 144)
                act.activation(silu_c[:], cT[:], ACT.Silu).then_inc(silu_done, 1)
                for n in range(FLIPS):
                    act.wait_ge(flip_mm, n + 1)
                    act.activation(g.toeplitz_all[:, 2 * n:2 * n + 2, :].rearrange("p h j -> p (h j)"), g.ps[:, 5 + n % 2, :],
                                   ACT.Copy).then_inc(flip_out, 1)

            @block.tensor
            def _(pe):
                pe.wait_ge(bias_loaded, 32)
                pe.wait_ge(rel_one, 1)
                pe.matmul(g.ps[0:HEADS, 7, 0:384], rel[:], sel[:], start=True, stop=True).then_inc(mod_mm, 1)
                pe.wait_ge(silu_done, 1)
                for l in range(2):
                    for j in range(6):
                        col = (l * 6 + j) * BATCH
                        mm = pe.matmul(g.ps[:, 0, col:col + BATCH], wmod[:, l, j * DIM:(j + 1) * DIM],
                                       silu_c[:, l, :], start=True, stop=True)
                mm.then_inc(mod_mm, 1)
                pe.wait_ge(wide, 1)
                for l in range(2):
                    for n, j in enumerate((2, 5)):
                        for b in range(BATCH):
                            mm = pe.matmul(g.ps[:, 1 + l * 2 + n, b * DIM:(b + 1) * DIM], silu_wide[:, l, b, :],
                                           wmod[:, l, j * DIM:(j + 1) * DIM], start=True, stop=True)
                mm.then_inc(mod_mm, 1)
                pe.wait_ge(mirrored_in, 16)
                for n in range(FLIPS):
                    if n >= 2:
                        pe.wait_ge(flip_out, n - 1)
                    pe.matmul(g.ps[:, 5 + n % 2, :], flip[:], mirrored[:, 2 * n:2 * n + 2, :].rearrange("p h j -> p (h j)"),
                              start=True, stop=True).then_inc(flip_mm, 1)

            @block.vector
            def _(dve):
                dve.wait_ge(silu_done, 1)
                dve.tensor_copy(silu_wide[:], silu_c[:].unsqueeze(3).to_broadcast([P, 2, BATCH, P])).then_inc(wide, 1)
                dve.wait_ge(mod_mm, 1)
                dve.tensor_copy(bias_sb[:], g.ps[0:HEADS, 7, 0:384]).then_inc(bias_out, 1)
                dve.wait_ge(mod_mm, 2)
                dve.tensor_copy(g.mod_cols[:].rearrange("p l j b -> p (l j b)"), g.ps[:, 0, 0:48]).then_inc(step, 1)
                dve.wait_ge(step, 1)
                for l in range(2):
                    for j in (1, 4):
                        last = dve.tensor_scalar(g.mod_cols[:, l, j, :], g.mod_cols[:, l, j, :], 1.0, None, ALU.add)
                last.then_inc(step, 1)
                dve.wait_ge(mod_mm, 3)
                for l in range(2):
                    gate = g.ps[:, 1 + l * 2:3 + l * 2, :].rearrange("p n c -> p (n c)")
                    dve.tensor_copy(raw[:], gate).then_inc(step, 1)
                    dve.wait_ge(step, 3 + 4 * l)
                    dve.scalar_tensor_tensor(gabs[:], raw[:], -1.0, raw[:], ALU.mult, ALU.max)
                    dve.tensor_scalar(gsgn[:], raw[:], 0.0, 2.0, ALU.is_ge, ALU.mult).then_inc(step, 1)
                    dve.wait_ge(step, 4 + 4 * l)
                    dve.tensor_scalar(gabs[:], gabs[:], 0.25, None, ALU.max).then_inc(step, 1)
                    dve.wait_ge(step, 5 + 4 * l)
                    dve.scalar_tensor_tensor(g.gate_rows[:, l].rearrange("p n b d -> p (n b d)"), gsgn[:], -1.0,
                                             gabs[:], ALU.add, ALU.mult).then_inc(step, 1)
                    dve.wait_ge(step, 6 + 4 * l)
                dve.wait_ge(loaded, 144)
                dve.tensor_tensor(g.ga_bo[:], g.gate_rows[:, 0, 0], bo_row[:].unsqueeze(1).to_broadcast([P, BATCH, DIM]),
                                  ALU.mult).then_inc(step, 1)


def norm_modulate(nc, g, layer, which, add_ga_bo=False, shift=False):
    tag = f"n{layer}{which}_"
    stage_sems = []
    with ExitStack() as ctx:
        ctx.callback(give_back, nc, stage_sems)

        def sem(name):
            return kept(nc, stage_sems, tag + name)

        stats = ctx.enter_context(nc.sbuf_tensor(tag + "stats", [P, TB, 6], F32))
        mv = ctx.enter_context(nc.sbuf_tensor(tag + "mv", [P, TB, 2], F32))
        std = ctx.enter_context(nc.sbuf_tensor(tag + "std", [P, TB], F32))
        rstd = ctx.enter_context(nc.sbuf_tensor(tag + "rstd", [P, TB], F32))
        xn = ctx.enter_context(nc.sbuf_tensor(tag + "xn", [P, TB, DIM], F32))
        stats_done, var_done, std_done, rstd_done, xn_done, turned, evacuated = map(sem, (
            "stats", "var", "std", "rstd", "xn", "turned", "evacuated"))
        held = sem("held")
        s_cols, c_cols = g.mod_cols[:, layer, 3 * which, :], g.mod_cols[:, layer, 3 * which + 1, :]
        with nc.Block() as block:
            @block.vector
            def _(dve):
                with dve.Fori(0, BATCH) as b:
                    for t in range(TB):
                        last = dve.bn_stats(stats[:, t, :], g.x[:, ds(b * TB + t, 1), :].rearrange("p a d -> p (a d)"))
                    last.then_inc(stats_done, 1)
                    dve.wait_ge(stats_done, b + 1)
                    settle(dve, held)
                    for t in range(TB):
                        last = dve.bn_aggr(mv[:, t, :], stats[:, t, :])
                    last.then_inc(var_done, 1)
                    dve.wait_ge(var_done, 2 * b + 1)
                    dve.tensor_scalar(std[:], mv[:, :, 1], EPS, None, ALU.add).then_inc(var_done, 1)
                    dve.wait_ge(std_done, b + 1)
                    dve.reciprocal(rstd[:], std[:]).then_inc(rstd_done, 1)
                    dve.wait_ge(rstd_done, b + 1)
                    dve.wait_ge(turned, b + 1)
                    for t in range(TB):
                        last = dve.tensor_scalar(xn[:, t, :], g.x[:, ds(b * TB + t, 1), :].rearrange("p a d -> p (a d)"),
                                                 mv[:, t, 0:1], rstd[:, t:t + 1], ALU.subtract, ALU.mult)
                    last.then_inc(xn_done, 1)
                    if add_ga_bo:
                        dve.wait_ge(xn_done, b + 1)
                        dve.tensor_tensor(g.x[:, ds(b * TB, TB), :], g.x[:, ds(b * TB, TB), :],
                                          g.ga_bo[:, ds(b, 1), :].to_broadcast([P, TB, DIM]), ALU.add)

            @block.scalar
            def _(act):
                with act.Fori(0, BATCH) as b:
                    act.wait_ge(var_done, 2 * b + 2)
                    act.activation(std[:], std[:], ACT.Sqrt).then_inc(std_done, 1)
                    act.wait_ge(turned, b + 2)
                    for half in range(2):
                        for rows in (TOP, LOW) if shift else (slice(0, P),):
                            dst = shifted(g.zA, rows, b, half * BANK, BANK) if shift else \
                                g.hT[:, ds(b * SEQ + half * BANK, BANK)]
                            last = act.activation(dst, g.ps[rows, half, :], ACT.Identity, bias=s_cols[rows, ds(b, 1)],
                                                  scale=c_cols[rows, ds(b, 1)])
                    last.then_inc(evacuated, 1)

            @block.tensor
            def _(pe):
                pe.sem_inc(turned, 1)
                pe.sem_inc(evacuated, 1)
                with pe.Fori(0, BATCH) as b:
                    pe.wait_ge(xn_done, b + 1)
                    pe.wait_ge(evacuated, b + 1)
                    for t in range(TB):
                        last = pe.transpose(g.ps[:, t // 4, t % 4 * P:(t % 4 + 1) * P], xn[:, t, :], g.ident[:])
                    last.then_inc(turned, 1)


def split_project(nc, g):
    stage_sems = []
    with ExitStack() as ctx:
        ctx.callback(give_back, nc, stage_sems)

        def sb(name, shape, dt=F32):
            return ctx.enter_context(nc.sbuf_tensor(name, shape, dt))

        def sem(name):
            return kept(nc, stage_sems, name)

        w = sb("pj_w", [P, 3, DIM])
        parts = [sb(f"pj_part{n}", [P, 2, 2, BANK], BF16) for n in range(3)]
        rest = sb("pj_rest", [P, 2, BANK])
        w_in, scaled, q_mm, part_done, v_mm, v_out = map(sem, (
            "pj_w_in", "pj_scaled", "pj_q_mm", "pj_part_done", "pj_v_mm", "pj_v_out"))
        rest_done, mid_done = sem("pj_rest_done"), sem("pj_mid_done")
        written = [sem(f"pj_written{n}") for n in range(2)]
        CHUNKS = TOKENS // BANK
        with nc.Block() as block:
            @block.sync
            def _(sp):
                sp.dma_start(w[:], g.w0_qkv).then_inc(w_in, 16)
                for c in range(CHUNKS):
                    sp.wait_ge(part_done, c + 1)
                    for part in range(3):
                        sp.dma_start(g.qk_dram[part, :, :, c * BANK:(c + 1) * BANK].rearrange("a p n -> p a n"),
                                     parts[part][:, c % 2]).then_inc(written[c % 2], 16)
                for n in range(2):
                    sp.wait_ge(written[n], 48 * CHUNKS // 2)

            @block.tensor
            def _(pe):
                pe.wait_ge(w_in, 16)
                pe.wait_ge(scaled, 1)
                for c in range(CHUNKS):
                    if c >= 2:
                        pe.wait_ge(part_done, c - 1)
                    for a in range(2):
                        mm = pe.matmul(g.ps[:, 2 * (c % 2) + a, :], w[:, a, :], g.hT[:, c * BANK:(c + 1) * BANK],
                                       start=True, stop=True)
                    mm.then_inc(q_mm, 1)
                    if c >= 2:
                        pe.wait_ge(v_out, c - 1)
                    for t in range(4):
                        tok = c * BANK + t * P
                        mm = pe.matmul(g.ps[:, 4 + c % 2, t * P:(t + 1) * P], g.hT[:, tok:tok + P], w[:, 2, :],
                                       start=True, stop=True)
                    mm.then_inc(v_mm, 1)

            @block.vector
            def _(dve):
                dve.wait_ge(w_in, 16)
                dve.tensor_scalar(w[:, 0, :], w[:, 0, :], -float(np.float32(8 ** -0.5)), None, ALU.mult).then_inc(scaled, 1)
                for c in range(CHUNKS):
                    dve.wait_ge(q_mm, c + 1)
                    both = g.ps[:, 2 * (c % 2):2 * (c % 2) + 2, :]
                    if c >= 2:
                        dve.wait_ge(written[c % 2], 48 * (c // 2))
                    dve.tensor_copy(parts[0][:, c % 2], both).then_inc(mid_done, 1)
                    dve.wait_ge(mid_done, 2 * c + 1)
                    dve.tensor_tensor(rest[:], both, parts[0][:, c % 2], ALU.subtract).then_inc(rest_done, 1)
                    dve.wait_ge(rest_done, c + 1)
                    dve.tensor_copy(parts[1][:, c % 2], rest[:]).then_inc(mid_done, 1)
                    dve.wait_ge(mid_done, 2 * c + 2)
                    dve.tensor_tensor(parts[2][:, c % 2], rest[:], parts[1][:, c % 2], ALU.subtract).then_inc(part_done, 1)

            @block.scalar
            def _(act):
                for c in range(CHUNKS):
                    act.wait_ge(v_mm, c + 1)
                    act.activation(g.v_all[:, 4 * c:4 * c + 4, :], g.ps[:, 4 + c % 2, :].rearrange("p (t d) -> p t d", t=4),
                                   ACT.Copy).then_inc(v_out, 1)


class Plan:

    JOBS = 2 * PAIRS

    def __init__(self, layer):
        self.layer = layer
        self.causal = layer == 0
        self.rows = 32 if layer == 0 else 64
        self.prep = 0 if layer == 0 else 10
        self.total = 0
        self.index = {}
        for n in range(self.prep):
            self.index["prep", 0, n] = self.total
            self.total += 1
        for J in range(self.JOBS + 2):
            for s in range(8):
                for kind, job, n in self.items(J, s):
                    self.index[kind, job, n] = self.total
                    self.total += 1

    def steps(self, J):
        return 4 * (J % 2 + 1) if self.causal else 8

    def step(self, J):
        return J // 2 * (self.steps(0) + self.steps(1)) + (J % 2) * self.steps(0)

    def width(self, J, i):
        return (4 * (J % 2) + i + 1) * P if self.causal else SEQ

    def plain(self, J, i):
        return max(0, 4 * (J % 2) + i - 1) * P if self.causal else (4 * (J % 2) + i) * P

    def plains(self, J, u=0):
        if J < 0:
            return 0
        per = [sum(self.plain(j, s // 2) > 0 for s in range(8)) for j in range(2)]
        return J // 2 * sum(per) + (J % 2) * per[0] + sum(self.plain(J, s // 2) > 0 for s in range(u))

    def first(self, J, kt):
        return max(0, kt - 4 * (J % 2)) * P if self.causal else 0

    def product(self, J, s):
        if s and s - 1 < self.steps(J - 1):
            return J - 1, s - 1
        if s == 0 and self.steps(J - 2) == 8:
            return J - 2, 7
        return None, None

    def items(self, J, s):
        out = []
        if s == 1 and self.steps(J - 2) == 8 and 0 <= J - 2 < self.JOBS:
            out.append(("y", J - 2, 0))
        if s == 5 and self.steps(J - 1) == 4 and 0 <= J - 1 < self.JOBS:
            out.append(("y", J - 1, 0))
        if s == 2 and 0 <= J - 1 < self.JOBS:
            out.append(("r", J - 1, 0))
        if self.prep and s >= 3 and J < self.JOBS - 2:
            out.append(("prep", J // 2 + 1, 5 * (J % 2) + s - 3))
        return out


def at(it, jj, f):
    if isinstance(it, int):
        return f(4 * it + jj)
    per = f(4 * 3 + jj) - f(4 * 2 + jj)
    return it * per + (f(4 * 2 + jj) - 2 * per)


def wait(eng, sem, it, jj, f):
    v = at(it, jj, f)
    if not isinstance(v, int) or v > 0:
        eng.wait_ge(sem, v)


def settle(eng, sem):
    eng.sem_inc(sem, 1)


def turns(eng, plan, turn):
    last = plan.JOBS // 4 - 1
    for jj in range(4):
        turn(0, jj, jj)
    with eng.Fori(1, last) as it:
        for jj in range(4):
            turn(it, jj, 8 + jj)
    for jj in range(6):
        turn(last, jj, 4 * last + jj)


def batch_of(it, jj):
    return (4 * it + jj) // 16 if isinstance(it, int) else (it * 4 + jj) // 16


def attention(nc, g, layer):
    plan = Plan(layer)
    tag = f"a{layer}_"
    rows = plan.rows
    SLOTS = 8
    LOADS = 16 * (2 * SLOTS + 2)
    JOBS = plan.JOBS
    stage_sems = []
    with ExitStack() as ctx:
        ctx.callback(give_back, nc, stage_sems)

        def sb(name, shape, dt=F32):
            return ctx.enter_context(nc.sbuf_tensor(tag + name, shape, dt))

        def sem(name):
            return kept(nc, stage_sems, tag + name)

        if layer == 0:
            q_stack = [[sb(f"q_stack{n}", [P, 2, SEQ], BF16)] for n in range(2)]
            toeplitz = [sb(f"toeplitz{n}", [P, 2, 2 * P]) for n in range(2)]
        else:
            q_stack = [[sb(f"q_hi{n}", [P, 2, SEQ], F32R), sb(f"q_lo{n}", [P, 2, SEQ], F32R)] for n in range(2)]
            causal_rows = sb("causal_rows", [P, SEQ])
            h_pair = sb("h_pair", [P, SEQ])
            w_qk = sb("w_qk", [P, 2, 2, 2, 64])
            w_q = sb("w_q", [P, 2, 2, 64])
            w_v = sb("w_v", [P, 2 * 64])
        k_stack = [sb(f"k_stack{n}", [P, 2, SEQ], F32R if layer else BF16) for n in range(2)]
        v = [sb(f"v{n}", [P, TB, 2, rows]) for n in range(2)]
        w_out_raw = [sb(f"w_out_raw{n}", [P, DIM]) for n in range(2)]
        w_out = [sb(f"w_out{n}", [P, DIM]) for n in range(2)]
        probs = [sb(f"probs{n}", [P, 2, 4, SEQ]) for n in range(2)]
        turned = [[sb(f"turned{h}{n}", [P, BANK]) for n in range(2)] for h in range(2)]
        plain_min = sb("plain_min", [P, 16])
        row_min = sb("row_min", [P, 16])
        row_sum = sb("row_sum", [P, 2, 8])
        inv_sum = sb("inv_sum", [P, 8])
        inv_wide = sb("inv_wide", [P, 4, 2, 64])
        inv_rows = sb("inv_rows", [P, BANK])
        out_T = sb("out_T", [P, BANK])

        scores_bank = lambda s: g.ps[:, 2 * (s % 2):2 * (s % 2) + 2, :].rearrange("p a n -> p (a n)")
        turn_bank = [g.ps[:, 4, :], g.ps[:, 5, :]]
        out_bank = g.ps[:, 6, :]
        shared = g.ps[:, 7, :]

        scores_done = sem("scores_done")
        plain_done = sem("plain_done")
        min_done = sem("min_done")
        probs_done = sem("probs_done")
        turn_done = [sem(f"turn_done{h}") for h in range(2)]
        turned_out = [sem(f"turned_out{h}") for h in range(2)]
        product_done = sem("product_done")
        inv_done = sem("inv_done")
        wide_done = sem("wide_done")
        out_done = sem("out_done")
        item_done = sem("item_done")
        item_out = sem("item_out")
        w_out_done = sem("w_out_done")
        if layer == 0:
            stack_in = [sem(f"stack_in{n}") for n in range(2)]
            v_done = sem("v_done")
            table_done = sem("table_done")
        else:
            weights_in = sem("weights_in")
            w_q_done = sem("w_q_done")
            hi_done = sem("hi_done")
            lo_done = sem("lo_done")
            v_done = sem("v_done")
        cleared = sem("cleared")
        held = {e: sem("held_" + e) for e in ("dve", "pool", "sp")}

        def unit(u):
            return u // 2, u % 2

        with nc.Block() as block:
            @block.sync
            def _(sp):
                if layer == 0:
                    sp.wait_ge(cleared, 1)

                    def pair(it, n):
                        wait(sp, scores_done, it, 2 * n, lambda J: 8 * (J - 2))
                        settle(sp, held["sp"])
                        wait(sp, w_out_done, it, 2 * n, lambda J: J // 2 - 1)
                        settle(sp, held["sp"])
                        tok = (it // 4) * SEQ
                        head = (it % 4) * 4 + 2 * n
                        for slot in range(SLOTS):
                            for a, part, dst in ((0, slot // 3, q_stack[n][0]), (1, slot % 3, k_stack[n])):
                                src = g.qk_dram[part, a, ds(head * 8, 16), ds(tok, SEQ)]
                                sp.dma_start(dst[8 * slot:8 * slot + 8], src.rearrange("(h d) t -> d h t", d=8))\
                                    .then_inc(stack_in[n], 16)
                        for h in range(2):
                            sp.dma_start(w_out_raw[n][32 * h:32 * h + 8, :],
                                         g.w0_out[ds((head + h) * 8, 8), :]).then_inc(stack_in[n], 16)

                    for n in range(2):
                        pair(0, n)
                    with sp.Fori(1, PAIRS // 2) as it:
                        for n in range(2):
                            pair(it, n)
                else:
                    def pair(it, n):
                        if not (isinstance(it, int) and 2 * it + n == 0):
                            wait(sp, item_done, it, 2 * n, lambda J: plan.index["prep", J // 2 - 1, 9] + 1)
                            settle(sp, held["sp"])
                            wait(sp, w_out_done, it, 2 * n, lambda J: J // 2)
                        settle(sp, held["sp"])
                        col = (it % 4) * 256 + 128 * n
                        sp.dma_start(h_pair[:], g.hT[:, ds((it // 4) * SEQ, SEQ)]).then_inc(weights_in, 16)
                        for a in range(2):
                            for copy in range(2):
                                sp.dma_start(w_qk[:, a, :, copy, :], g.w1_qk[a, :, ds(col, 128)].rearrange(
                                    "p (h d) -> p h d", h=2)).then_inc(weights_in, 16)
                        sp.dma_start(w_v[:], g.w1_v[:, ds(col, 128)]).then_inc(weights_in, 16)
                        sp.dma_start(w_out_raw[0][:], g.w1_out[ds(col, 128), :]).then_inc(weights_in, 16)

                    pair(0, 0)
                    pair(0, 1)
                    with sp.Fori(1, PAIRS // 2) as it:
                        for n in range(2):
                            pair(it, n)

            @block.gpsimd
            def _(pool):
                if layer == 0:
                    zeroed = [q_stack[0][0], q_stack[1][0], k_stack[0], k_stack[1]]
                    for t in zeroed:
                        pool.memset(t[:], 0.0)
                    for t in w_out_raw:
                        pool.memset(t[:], 0.0)
                    for t in v:
                        last = pool.memset(t[:], 0.0)
                    last.then_inc(cleared, 1)
                    pool.wait_ge(cleared, 1)
                else:
                    pool.memset(causal_rows[:], 50.0).then_inc(cleared, 1)
                    pool.wait_ge(cleared, 1)
                    pool.affine_select(out=causal_rows[:], in_=causal_rows[:], compare_op=ALU.is_gt, fill=0.0,
                                       base=0, pattern=[[1, SEQ]], channel_multiplier=-1).then_inc(cleared, 1)

                def pair(it, n):
                    b = it // 4
                    if layer == 0:
                        head = (it % 4) * 4 + 2 * n
                        wait(pool, product_done, it, 2 * n, lambda J: plan.step(J - 2))
                        pool.tensor_copy(v[n][:, :, :, 0:8], g.v_all[:, ds(b * TB, TB), ds(head * 8, 16)].rearrange(
                            "p t (h d) -> p t h d", h=2)).then_inc(v_done, 1)
                        wait(pool, min_done, it, 2 * n, lambda J: 8 * (J - 2))
                        pool.tensor_copy(toeplitz[n][:], g.toeplitz_all[:, ds(head, 2), :]).then_inc(table_done, 1)
                        pool.wait_ge(stack_in[n], it * LOADS + LOADS)
                        raw = w_out_raw[n]
                    else:
                        pool.wait_ge(weights_in, (it * 2 + n) * 112 + 112)
                        if not (isinstance(it, int) and 2 * it + n == 0):
                            wait(pool, item_done, it, 2 * n, lambda J: plan.index["prep", J // 2 - 1, 3] + 1)
                        settle(pool, held["pool"])
                        pool.tensor_scalar(w_q[:], w_qk[:, 0], -0.125, None, ALU.mult).then_inc(w_q_done, 1)
                        raw = w_out_raw[0]
                    if not (isinstance(it, int) and it == 0):
                        wait(pool, item_done, it, 2 * n, lambda J: plan.index["y", J - 3, 0] + 1)
                    settle(pool, held["pool"])
                    pool.tensor_tensor(w_out[n][:], raw[:],
                                       g.gate_rows[:, layer, 0, ds(b, 1), :].rearrange("p a d -> p (a d)"),
                                       ALU.mult).then_inc(w_out_done, 1)

                for n in range(2):
                    pair(0, n)
                with pool.Fori(1, PAIRS // 2) as it:
                    for n in range(2):
                        pair(it, n)

            @block.tensor
            def _(pe):
                def prep(it, jj, J, key):
                    _, p, n = key
                    if n == 0:
                        wait(pe, weights_in, it, jj, lambda J: 112 * (J // 2 + 2)) if J is not None else pe.wait_ge(weights_in, 112)
                        wait(pe, w_q_done, it, jj, lambda J: J // 2 + 2) if J is not None else pe.wait_ge(w_q_done, 1)
                    if n < 8:
                        a, h, half = n // 4, n // 2 % 2, n % 2
                        w = w_q[:, h] if a == 0 else w_qk[:, 1, h]
                        return pe.matmul(shared, w.rearrange("p c d -> p (c d)"), h_pair[:, half * BANK:(half + 1) * BANK],
                                         start=True, stop=True)
                    for t in range(4):
                        tok = (4 * (n - 8) + t) * P
                        mm = pe.matmul(shared[:, t * P:(t + 1) * P], h_pair[:, tok:tok + P], w_v[:], start=True, stop=True)
                    return mm

                def item(it, jj, J, key):
                    index = lambda J2: plan.index[key[0], J2 + key[1] - J, key[2]]
                    if key[0] == "prep":
                        index = lambda J2: plan.index["prep", J2 // 2 + 1, key[2]]
                    wait(pe, item_out, it, jj, index)
                    if key[0] == "prep":
                        mm = prep(it, jj, J, key)
                    elif key[0] == "r":
                        wait(pe, wide_done, it, jj, lambda J2: J2)
                        for i in range(4):
                            mm = pe.transpose(shared[:, i * P:(i + 1) * P], inv_wide[:, i].rearrange("p h r -> p (h r)"),
                                              g.ident[:])
                    else:
                        lag = J - key[1]
                        wait(pe, out_done, it, jj, lambda J2: J2 - lag + 1)
                        wait(pe, w_out_done, it, jj, lambda J2: (J2 - lag) // 2 + 1)
                        for i in range(4):
                            mm = pe.matmul(shared[:, i * P:(i + 1) * P], out_T[0:2 * rows, i * P:(i + 1) * P],
                                           w_out[key[1] // 2 % 2][0:2 * rows, :], start=True, stop=True)
                    mm.then_inc(item_done, 1)

                def turn(it, jj, J):
                    n = J // 2 % 2
                    for s in range(8):
                        i, h = unit(s)
                        if J < JOBS:
                            if s == 0 and layer == 0:
                                pe.wait_ge(stack_in[n], it * LOADS + LOADS)
                            if s == 0 and layer == 1:
                                wait(pe, lo_done, it, jj, lambda J2: 8 * (J2 // 2 + 1))
                            wait(pe, probs_done, it, jj, lambda J2: 8 * J2 + s - 1)
                            q0 = (4 * (J % 2) + i) * P
                            width = plan.width(J, i)
                            for k0 in range(0, width, BANK):
                                k1 = min(width, k0 + BANK)
                                for m, q in enumerate(q_stack[n]):
                                    mm = pe.matmul(scores_bank(s)[:, k0:k1], q[:, h, q0:q0 + P], k_stack[n][:, h, k0:k1],
                                                   start=(m == 0), stop=(m == len(q_stack[n]) - 1))
                            mm.then_inc(scores_done, 1)
                        if 0 <= J - 1 < JOBS and s < plan.steps(J - 1):
                            if s == 0:
                                wait(pe, probs_done, it, jj, lambda J2: 8 * J2)
                            for h in range(2):
                                wait(pe, turned_out[h], it, jj, lambda J2: plan.step(J2 - 1) + s)
                                for i in range(plan.first(J - 1, s) // P, 4):
                                    mm = pe.transpose(turn_bank[h][:, i * P:(i + 1) * P],
                                                      probs[(J - 1) % 2][:, h, i, s * P:(s + 1) * P], g.ident[:])
                                mm.then_inc(turn_done[h], 1)
                        for key in plan.items(J, s):
                            item(it, jj, J, key)
                        job, kt = plan.product(J, s)
                        if job is not None and 0 <= job < JOBS:
                            lag = J - job
                            if kt == 0:
                                wait(pe, out_done, it, jj, lambda J2: J2 - lag)
                                wait(pe, v_done, it, jj, lambda J2: ((J2 - lag) // 2 + 1) * (1 if layer == 0 else 2))
                            off = plan.first(job, kt)
                            for h in range(2):
                                wait(pe, turned_out[h], it, jj, lambda J2: plan.step(J2 - lag) + kt + 1)
                                mm = pe.matmul(out_bank[rows * h:rows * (h + 1), off:], v[job // 2 % 2][:, kt, h, :],
                                               turned[h][kt % 2][:, off:], start=(kt == 0),
                                               stop=(kt == plan.steps(job) - 1), tile_position=(0, rows * h))
                            mm.then_inc(product_done, 1)

                for n in range(plan.prep):
                    if n:
                        pe.wait_ge(item_out, n)
                    prep(0, 0, None, ("prep", 0, n)).then_inc(item_done, 1)
                turns(pe, plan, turn)

            @block.vector
            def _(dve):
                def split(it, jj, J, key):
                    _, p, n = key
                    a, h, half = n // 4, n // 2 % 2, n % 2
                    cols = slice(half * BANK, (half + 1) * BANK)
                    hi = (q_stack[p % 2][0] if a == 0 else k_stack[p % 2])[:, h, cols]
                    dve.tensor_copy(hi, shared).then_inc(hi_done, 1)
                    count = lambda J2: 8 * (J2 // 2 + 1) + n + 1
                    if J is None:
                        dve.wait_ge(hi_done, n + 1)
                    else:
                        wait(dve, hi_done, it, jj, count)
                    if a == 0:
                        done = dve.tensor_tensor(q_stack[p % 2][1][:, h, cols], shared, hi.bitcast(F32), ALU.subtract)
                    else:
                        low = hi[64:128].bitcast(F32)
                        done = dve.tensor_tensor(k_stack[p % 2][64:128, h, cols], shared[64:128], low, ALU.subtract)
                    done.then_inc(lo_done, 1)
                    if J is None:
                        dve.wait_ge(lo_done, n + 1)
                    else:
                        wait(dve, lo_done, it, jj, count)
                    dve.sem_inc(item_out, 1)

                def turn(it, jj, J):
                    for s in range(8):
                        i, h = unit(s)
                        if J < JOBS:
                            n = J // 2 % 2
                            wait(dve, scores_done, it, jj, lambda J2: 8 * J2 + s + 1)
                            width, plain = plan.width(J, i), plan.plain(J, i)
                            sc = scores_bank(s)
                            slot = 8 * (J % 2) + s
                            floor = 3e38
                            if plain:
                                dve.tensor_reduce(plain_min[:, slot:slot + 1], sc[:, 0:plain], AX, ALU.min)\
                                   .then_inc(plain_done, 1)
                                wait(dve, plain_done, it, jj, lambda J2: plan.plains(J2, s + 1))
                                floor = plain_min[:, slot:slot + 1]
                            rest = width - plain
                            if layer == 0:
                                if s == 0:
                                    wait(dve, table_done, it, jj, lambda J2: J2 // 2 + 1)
                                add = toeplitz[n][:, h, 2 * P - rest:]
                            else:
                                if s == 0 and J == 0:
                                    dve.wait_ge(cleared, 2)
                                add = causal_rows[:, 0:rest]
                            settle(dve, held["dve"])
                            dve.tensor_tensor_reduce(out=sc[:, plain:width], in0=sc[:, plain:width], in1=add, scale=1.0,
                                                     scalar=floor, op0=ALU.add, op1=ALU.min,
                                                     accum_out=row_min[:, slot:slot + 1]).then_inc(min_done, 1)
                        if 0 <= J - 1 < JOBS and s < plan.steps(J - 1):
                            wait(dve, turn_done[0], it, jj, lambda J2: plan.step(J2 - 1) + s + 1)
                            wait(dve, product_done, it, jj, lambda J2: plan.step(J2 - 1) + s - 1)
                            off = plan.first(J - 1, s)
                            dve.tensor_copy(turned[0][s % 2][:, off:], turn_bank[0][:, off:]).then_inc(turned_out[0], 1)
                        if s == 1 and 0 <= J - 1 < JOBS:
                            wait(dve, probs_done, it, jj, lambda J2: 8 * J2)
                            dve.reciprocal(inv_sum[:], row_sum[:, (J - 1) % 2]).then_inc(inv_done, 1)
                            wait(dve, inv_done, it, jj, lambda J2: J2)
                            if not (isinstance(it, int) and J - 2 < 0):
                                wait(dve, item_done, it, jj, lambda J2: plan.index["r", J2 - 2, 0] + 1)
                            dve.tensor_copy(inv_wide[:].rearrange("p i h r -> p i (h r)")[:, :, 0:2 * rows].rearrange(
                                "p i (h r) -> p i h r", h=2),
                                inv_sum[:].rearrange("p (i h) -> p i h", h=2).unsqueeze(3).to_broadcast([P, 4, 2, rows]))\
                               .then_inc(wide_done, 1)
                        for key in plan.items(J, s):
                            if key[0] == "prep" and key[2] < 8:
                                wait(dve, item_done, it, jj, lambda J2: plan.index["prep", J2 // 2 + 1, key[2]] + 1)
                                split(it, jj, J, key)
                            if key[0] == "y":
                                lag = J - key[1]
                                wait(dve, item_done, it, jj, lambda J2: plan.index["y", J2 - lag, 0] + 1)
                                if isinstance(it, int):
                                    tile = 4 * (key[1] % 2) + key[1] // 16 * TB
                                else:
                                    tile = (it * 4 + (jj - lag)) // 16 * TB + 4 * (key[1] % 2)
                                rowsx = g.x[:, ds(tile, 4), :]
                                dve.tensor_tensor(rowsx, rowsx, shared.rearrange("p (t d) -> p t d", t=4), ALU.add)\
                                   .then_inc(item_out, 1)
                        job, kt = plan.product(J, s)
                        if job is not None and 0 <= job < JOBS and kt == plan.steps(job) - 1:
                            lag = J - job
                            wait(dve, product_done, it, jj, lambda J2: plan.step(J2 - lag) + kt + 1)
                            wait(dve, item_out, it, jj, lambda J2: plan.index["r", J2 - lag, 0] + 1)
                            if job > 0:
                                wait(dve, item_done, it, jj, lambda J2: plan.index["y", J2 - lag - 1, 0] + 1)
                            dve.tensor_tensor(out_T[0:2 * rows, :], out_bank[0:2 * rows, :], inv_rows[0:2 * rows, :],
                                              ALU.mult).then_inc(out_done, 1)

                if layer == 0:
                    dve.memset(inv_wide[:], 0.0).then_inc(inv_done, 0 + 1) if False else dve.memset(inv_wide[:], 0.0)
                for n in range(min(8, plan.prep)):
                    dve.wait_ge(item_done, n + 1)
                    split(0, 0, None, ("prep", 0, n))
                turns(dve, plan, turn)

            @block.scalar
            def _(act):
                def copy_v(it, jj, J, key):
                    _, p, n = key
                    t0 = 4 * (n - 8)
                    act.activation(v[p % 2][:, t0:t0 + 4].rearrange("p t h d -> p t (h d)"),
                                   shared.rearrange("p (t c) -> p t c", t=4), ACT.Copy).then_inc(v_done, 1)
                    if J is None:
                        act.wait_ge(v_done, n - 7)
                    else:
                        wait(act, v_done, it, jj, lambda J2: 2 * (J2 // 2 + 1) + n - 7)
                    act.sem_inc(item_out, 1)

                def turn(it, jj, J):
                    for s in range(8):
                        i, h = unit(s)
                        if 0 <= J - 1 < JOBS and s < plan.steps(J - 1):
                            wait(act, turn_done[1], it, jj, lambda J2: plan.step(J2 - 1) + s + 1)
                            wait(act, product_done, it, jj, lambda J2: plan.step(J2 - 1) + s - 1)
                            off = plan.first(J - 1, s)
                            act.activation(turned[1][s % 2][:, off:], turn_bank[1][:, off:], ACT.Copy)\
                               .then_inc(turned_out[1], 1)
                        if J < JOBS:
                            wait(act, min_done, it, jj, lambda J2: 8 * J2 + s + 1)
                            if s == 0:
                                wait(act, turn_done[1], it, jj, lambda J2: plan.step(J2 - 1))
                                wait(act, inv_done, it, jj, lambda J2: J2 - 1)
                            slot = 8 * (J % 2) + s
                            width = plan.width(J, i)
                            act.activation(probs[J % 2][:, h, i, 0:width], scores_bank(s)[:, 0:width], ACT.Exp,
                                           bias=row_min[:, slot:slot + 1], scale=-1.0,
                                           accum_out=row_sum[:, J % 2, s:s + 1]).then_inc(probs_done, 1)
                        for key in plan.items(J, s):
                            if key[0] == "prep" and key[2] >= 8:
                                wait(act, item_done, it, jj, lambda J2: plan.index["prep", J2 // 2 + 1, key[2]] + 1)
                                copy_v(it, jj, J, key)
                            if key[0] == "r":
                                wait(act, item_done, it, jj, lambda J2: plan.index["r", J2 - 1, 0] + 1)
                                wait(act, out_done, it, jj, lambda J2: J2 - 1)
                                act.activation(inv_rows[:], shared, ACT.Copy).then_inc(item_out, 1)

                for n in range(8, plan.prep):
                    act.wait_ge(item_done, n + 1)
                    copy_v(0, 0, None, ("prep", 0, n))
                turns(act, plan, turn)


def experts(nc, g):
    EM = EXPERTS * 2
    CHUNKS = TOKENS // BANK
    stage_sems = []
    with ExitStack() as ctx:
        ctx.callback(give_back, nc, stage_sems)

        def sb(name, shape, dt=F32):
            return ctx.enter_context(nc.sbuf_tensor("e_" + name, shape, dt))

        def sem(name):
            return kept(nc, stage_sems, "e_" + name)

        w1 = sb("w1", [P, EXPERTS, HIDDEN])
        w3 = sb("w3", [P, EXPERTS, HIDDEN])
        w2 = sb("w2", [P, EXPERTS, 2, DIM])
        lora_a = sb("lora_a", [RANK, 2, EXPERTS, DIM])
        lora_b = sb("lora_b", [RANK, 2, EXPERTS, HIDDEN])
        lora_a2 = sb("lora_a2", [RANK, EXPERTS, HIDDEN])
        lora_b2 = sb("lora_b2", [RANK, EXPERTS, DIM])
        b13 = sb("b13", [P, 2, EXPERTS, 2])
        b2 = sb("b2", [EXPERTS, DIM])
        w_gate = sb("w_gate", [P, EXPERTS])
        iota = sb("iota", [P, EXPERTS])
        logits_T = sb("logits_T", [EXPERTS, TOKENS])
        logits = sb("logits", [P, TILES, EXPERTS])
        best = sb("best", [P, TILES, 8])
        best_at = sb("best_at", [P, TILES, 8], U32)
        index = sb("index", [P, TILES, 2])
        weight = sb("weight", [P, TILES, 2])
        gap = sb("gap", [P, TILES])
        total = sb("total", [P, TILES])
        second = sb("second", [P, TILES, EXPERTS])
        gates = sb("gates", [P, TILES, EXPERTS])
        gates_T = sb("gates_T", [EXPERTS, TOKENS])
        gates_chunk = sb("gates_chunk", [EXPERTS, BANK])
        silu = [sb(f"silu{n}", [P, BANK]) for n in range(2)]
        hidden = [[sb(f"hidden{n}{m}", [P, BANK]) for m in range(2)] for n in range(2)]
        acc = sb("acc", [P, 4, DIM])
        gated = sb("gated", [P, 4, DIM])
        loaded, low_done, merged = sem("loaded"), sem("low_done"), sem("merged")
        logit_mm, logit_out, turn_done, route, exp_done, gate_turned, gate_out = map(sem, (
            "logit_mm", "logit_out", "turn_done", "route", "exp_done", "gate_turned", "gate_out"))
        merges = [("13", a, e) for a in range(2) for e in range(0, EXPERTS, 2)] + [("2", 0, e) for e in range(0, EXPERTS, 2)]
        with nc.Block() as block:
            @block.sync
            def _(sp):
                loads = ((lora_a, g.lora_a), (lora_b, g.lora_b), (w1, g.w1), (w3, g.w3), (lora_a2, g.lora_a2),
                         (lora_b2, g.lora_b2), (w2, g.w2), (w_gate, g.w_gate), (iota, g.iota), (b13, g.b13), (b2, g.b2))
                for dst, src in loads:
                    sp.dma_start(dst[:], src).then_inc(loaded, 16)

            @block.tensor
            def _(pe):
                pe.wait_ge(loaded, 176)
                for c in range(CHUNKS):
                    if c >= 2:
                        pe.wait_ge(logit_out, c - 1)
                    pe.matmul(g.ps[0:EXPERTS, 6 + c % 2, :], w_gate[:], g.hT[:, c * BANK:(c + 1) * BANK], start=True,
                              stop=True).then_inc(logit_mm, 1)
                pe.wait_ge(logit_out, CHUNKS)
                for t in range(TILES):
                    mm = pe.transpose(g.ps[:, 6, t * EXPERTS:(t + 1) * EXPERTS], logits_T[:, t * P:(t + 1) * P],
                                      g.ident[0:EXPERTS, 0:EXPERTS])
                mm.then_inc(turn_done, 1)
                for n, (kind, a, e) in enumerate(merges):
                    if n >= 4:
                        pe.wait_ge(merged, n - 3)
                    for j in range(2):
                        if kind == "13":
                            mm = pe.matmul(g.ps[:, n % 4, j * HIDDEN:(j + 1) * HIDDEN], lora_a[:, a, e + j],
                                           lora_b[:, a, e + j], start=True, stop=True)
                        else:
                            for m in range(2):
                                col = (2 * j + m) * DIM
                                mm = pe.matmul(g.ps[:, n % 4, col:col + DIM], lora_a2[:, e + j, m * P:(m + 1) * P],
                                               lora_b2[:, e + j], start=True, stop=True)
                    mm.then_inc(low_done, 1)
                pe.wait_ge(route, 7)
                for c in range(CHUNKS):
                    if c >= 2:
                        pe.wait_ge(gate_out, c - 1)
                    for t in range(4):
                        mm = pe.transpose(g.ps[0:EXPERTS, 4 + c % 2, t * P:(t + 1) * P], gates[:, 4 * c + t, :], g.ident[:])
                    mm.then_inc(gate_turned, 1)

            @block.scalar
            def _(act):
                for c in range(CHUNKS):
                    act.wait_ge(logit_mm, c + 1)
                    act.activation(logits_T[:, c * BANK:(c + 1) * BANK], g.ps[0:EXPERTS, 6 + c % 2, :], ACT.Copy)\
                       .then_inc(logit_out, 1)
                act.wait_ge(route, 3)
                act.activation(weight[:, :, 1], gap[:], ACT.Exp).then_inc(exp_done, 1)
                for c in range(CHUNKS):
                    act.wait_ge(gate_turned, c + 1)
                    act.activation(gates_T[:, c * BANK:(c + 1) * BANK], g.ps[0:EXPERTS, 4 + c % 2, :], ACT.Copy)\
                       .then_inc(gate_out, 1)

            @block.vector
            def _(dve):
                dve.wait_ge(turn_done, 1)
                dve.tensor_copy(logits[:].rearrange("p t e -> p (t e)"), g.ps[:, 6, 0:TILES * EXPERTS]).then_inc(route, 1)
                dve.wait_ge(route, 1)
                for t in range(TILES):
                    last = dve.max(best[:, t, :], logits[:, t, :])
                last.then_inc(route, 1)
                dve.wait_ge(route, 2)
                dve.tensor_tensor(gap[:], best[:, :, 1], best[:, :, 0], ALU.subtract).then_inc(route, 1)
                for t in range(TILES):
                    last = dve.max_index(best_at[:, t, :], best[:, t, :], logits[:, t, :])
                last.then_inc(route, 1)
                dve.wait_ge(exp_done, 1)
                dve.tensor_scalar(total[:], weight[:, :, 1], 1.0, None, ALU.add).then_inc(route, 1)
                dve.wait_ge(route, 5)
                dve.reciprocal(weight[:, :, 0], total[:])
                dve.tensor_copy(index[:], best_at[:, :, 0:2]).then_inc(route, 1)
                dve.wait_ge(route, 6)
                dve.tensor_tensor(weight[:, :, 1], weight[:, :, 1], weight[:, :, 0], ALU.mult)
                wide = [P, TILES, EXPERTS]
                for n, dst in ((0, gates), (1, second)):
                    last = dve.tensor_tensor(dst[:], iota[:].unsqueeze(1).to_broadcast(wide),
                                             index[:, :, n:n + 1].to_broadcast(wide), ALU.is_equal)
                last.then_inc(exp_done, 1)
                dve.wait_ge(exp_done, 2)
                for n, dst in ((0, gates), (1, second)):
                    last = dve.tensor_tensor(dst[:], dst[:], weight[:, :, n:n + 1].to_broadcast(wide), ALU.mult)
                last.then_inc(exp_done, 1)
                dve.wait_ge(exp_done, 3)
                dve.tensor_tensor(gates[:], gates[:], second[:], ALU.add).then_inc(route, 1)
                for n, (kind, a, e) in enumerate(merges):
                    dve.wait_ge(low_done, n + 1)
                    w = (w1, w3)[a][:, e:e + 2].rearrange("p e n -> p (e n)") if kind == "13" else \
                        w2[:, e:e + 2].rearrange("p e m d -> p (e m d)")
                    dve.tensor_tensor(w, w, g.ps[:, n % 4, :], ALU.add).then_inc(merged, 1)

        up_done, silu_done, hidden_done, down_done, acc_done, bias_in, bias_mm, bias_out, gated_done, x_done = map(sem, (
            "up_done", "silu_done", "hidden_done", "down_done", "acc_done", "bias_in", "bias_mm", "bias_out",
            "gated_done", "x_done"))
        with nc.Block() as block:
            @block.gpsimd
            def _(pool):
                with pool.Fori(0, CHUNKS) as c:
                    pool.wait_ge(bias_mm, c + 1)
                    pool.tensor_copy(gates_chunk[:], gates_T[:, ds(c * BANK, BANK)]).then_inc(bias_in, 1)

            @block.tensor
            def _(pe):
                pe.sem_inc(bias_mm, 1)
                pe.sem_inc(down_done, 2)

                def down(c, e):
                    pe.wait_ge(hidden_done, c * EM + 2 * e + 4)
                    pe.wait_ge(acc_done, c * EXPERTS + e + 1)
                    for t in range(4):
                        for m in range(2):
                            mm = pe.matmul(g.ps[:, 4 + e % 2, t * DIM:(t + 1) * DIM], hidden[e % 2][m][:, t * P:(t + 1) * P],
                                           w2[:, e, m, :], start=(m == 0), stop=(m == 1))
                    mm.then_inc(down_done, 1)

                with pe.Fori(0, CHUNKS) as c:
                    for e in range(EXPERTS):
                        for m in range(2):
                            i = 2 * e + m
                            pe.wait_ge(hidden_done, c * EM + i + 1)
                            for n, w in enumerate((w1, w3)):
                                mm = pe.matmul(g.ps[:, 2 * n + i % 2, :], w[:, e, m * P:(m + 1) * P],
                                               g.hT[:, ds(c * BANK, BANK)], start=True, stop=True)
                            mm.then_inc(up_done, 1)
                        if e == 0:
                            pe.wait_ge(bias_in, c + 1)
                            pe.wait_ge(bias_out, c + 1)
                            for t in range(4):
                                mm = pe.matmul(g.ps[:, 6, t * DIM:(t + 1) * DIM], gates_chunk[:, t * P:(t + 1) * P], b2[:],
                                               start=True, stop=True)
                            mm.then_inc(bias_mm, 1)
                        else:
                            down(c, e - 1)
                    down(c, EXPERTS - 1)

            @block.scalar
            def _(act):
                act.sem_inc(bias_out, 1)
                with act.Fori(0, CHUNKS) as c:
                    for i in range(EM):
                        act.wait_ge(up_done, c * EM + i + 1)
                        act.activation(silu[i % 2][:], g.ps[:, i % 2, :], ACT.Silu, bias=b13[:, 0, i // 2, i % 2:i % 2 + 1])\
                           .then_inc(silu_done, 1)
                        if i == 1:
                            act.wait_ge(bias_mm, c + 2)
                            act.wait_ge(gated_done, c + 1)
                            act.activation(acc[:].rearrange("p t d -> p (t d)"), g.ps[:, 6, :], ACT.Copy).then_inc(bias_out, 1)

            @block.vector
            def _(dve):
                dve.sem_inc(hidden_done, 2)
                dve.sem_inc(acc_done, 2)
                dve.sem_inc(gated_done, 1)

                def accumulate(c, e):
                    dve.wait_ge(down_done, c * EXPERTS + e + 3)
                    if e == 0:
                        dve.wait_ge(bias_out, c + 2)
                    else:
                        dve.wait_ge(acc_done, c * EXPERTS + e + 2)
                    for t in range(4):
                        last = dve.scalar_tensor_tensor(
                            acc[:, t, :], g.ps[:, 4 + e % 2, t * DIM:(t + 1) * DIM],
                            gates[:, ds(c * 4 + t, 1), e:e + 1].rearrange("p a e -> p (a e)"), acc[:, t, :], ALU.mult, ALU.add)
                    last.then_inc(acc_done, 1)

                with dve.Fori(0, CHUNKS) as c:
                    for e in range(EXPERTS):
                        for m in range(2):
                            i = 2 * e + m
                            dve.wait_ge(silu_done, c * EM + i + 1)
                            dve.wait_ge(down_done, c * EXPERTS + e + 1)
                            dve.scalar_tensor_tensor(hidden[e % 2][m][:], g.ps[:, 2 + i % 2, :], b13[:, 1, e, m:m + 1],
                                                     silu[i % 2][:], ALU.add, ALU.mult).then_inc(hidden_done, 1)
                        if e:
                            accumulate(c, e - 1)
                    accumulate(c, EXPERTS - 1)
                    dve.wait_ge(acc_done, c * EXPERTS + EXPERTS + 2)
                    dve.tensor_tensor(gated[:], acc[:], g.gate_rows[:, 0, 1, ds(c // 2, 1), :].to_broadcast([P, 4, DIM]),
                                      ALU.mult).then_inc(gated_done, 1)
                    dve.wait_ge(gated_done, c + 2)
                    rowsx = g.x[:, ds(c * 4, 4), :]
                    dve.tensor_tensor(rowsx, rowsx, gated[:], ALU.add).then_inc(x_done, 1)


def shifted(z, rows, b, t0, n):
    lo = t0 + (1 if rows.start else 0)
    return z[rows, ds(b, 1), ds(lo, n)].rearrange("p a t -> p (a t)")


TOP, LOW = slice(0, 64), slice(64, 128)


def local_attention(nc, g, layer):
    stage_sems = []
    with ExitStack() as ctx:
        ctx.callback(give_back, nc, stage_sems)

        def sb(name, shape, dt=F32):
            return ctx.enter_context(nc.sbuf_tensor(f"t{layer}_{name}", shape, dt))

        def sem(name):
            return kept(nc, stage_sems, f"t{layer}_{name}")

        G = 4
        KEYS = P + LWIN
        w = sb("w", [P, 3 * INNER])
        wo = sb("wo", [P, 4, DIM])
        scale_rows = sb("scale_rows", [P, 2, LDH])
        rot = sb("rot", [P, TB, 2, 2, LDH])
        mask = sb("mask", [P, 2, KEYS])
        minus_half = sb("minus_half", [P, 16])
        h_tile = [sb(f"h_tile{n}", [P, P]) for n in range(2)]
        squares = sb("squares", [P, 2 * INNER])
        squared_norm = sb("squared_norm", [P, 16])
        inv_norm = sb("inv_norm", [P, 16])
        by_cos = sb("by_cos", [P, 16, LDH])
        by_sin = sb("by_sin", [P, 16, LDH])
        rotated = sb("rotated", [P, 16, LDH])
        q_T = [[sb(f"q_T{n}{odd}", [P, 4, P]) for odd in range(2)] for n in range(2)]
        k_ring = sb("k_ring", [P, 4, (TB + 1) * P])
        v_ring = sb("v_ring", [P, TB + 1, INNER])
        row_min = sb("row_min", [P, 2, G])
        row_sum = sb("row_sum", [P, 2, G])
        inv_sum = sb("inv_sum", [P, 2, G])
        probs = [sb(f"probs{n}", [P, G, 2 * P]) for n in range(2)]
        probs_T = [sb(f"probs_T{n}", [P, 2, BANK]) for n in range(2)]
        out_T = sb("out_T", [P, 4, P])

        h_done = sem("h_done")
        qkv_done = sem("qkv_done")
        square_done, v_done = sem("square_done"), sem("v_done")
        sum_done = sem("sum_done")
        floor_done = sem("floor_done")
        inv_done = sem("inv_done")
        rotate_done = sem("rotate_done")
        pool_step = sem("pool_step")
        rotated_done = sem("rotated_done")
        front_done = sem("front_done")
        q_out, k_out = sem("q_out"), sem("k_out")
        proj_done = sem("proj_done")
        z_done = sem("z_done")
        scores_done = sem("scores_done")
        min_done = sem("min_done")
        probs_done = sem("probs_done")
        inv_sum_done = sem("inv_sum_done")
        scaled_done = sem("scaled_done")
        turn_done = sem("turn_done")
        turned5, turned6 = sem("turned5"), sem("turned6")
        product_done = sem("product_done")
        out_done = sem("out_done")
        loaded, ready, tables, held = sem("loaded"), sem("ready"), sem("tables"), sem("held")
        held_dve = sem("held_dve")
        heads_of = lambda ap: ap.rearrange("p (h d) -> p h d", d=LDH)
        flat = lambda ap: ap.rearrange("p j t -> p (j t)")

        def reach(eng, sem, count):
            if not isinstance(count, int) or count > 0:
                eng.wait_ge(sem, count)

        def batches(eng, turn):
            for t in range(TB):
                turn(0, t)
            with eng.Fori(1, BATCH) as b:
                for t in range(TB):
                    turn(b, t)

        def exists(b, t, n):
            return not isinstance(b, int) or t - n >= 0

        with nc.Block() as block:
            @block.sync
            def _(sp):
                for dst, src in ((w[:], g.wqkv[layer]), (wo[:], g.wo[layer]), (rot[:], g.rotary), (mask[:], g.band)):
                    sp.dma_start(dst, src).then_inc(loaded, 16)
                for n, src in enumerate((g.q_scale, g.k_scale)):
                    sp.dma_start(scale_rows[:, n, :], src[layer].partition_broadcast(P)).then_inc(loaded, 16)

            @block.gpsimd
            def _(pool):
                def take(b, t):
                    pool.tensor_copy(h_tile[t % 2][:], g.zA[:, ds(b, 1), ds(t * P, P)].rearrange("p a t -> p (a t)"))\
                        .then_inc(h_done, 1)

                def add_products(n):
                    reach(pool, rotate_done, n + 1)
                    settle(pool, held)
                    reach(pool, front_done, n)
                    settle(pool, held)
                    pool.tensor_tensor(rotated[:], by_cos[:], by_sin[:], ALU.add).then_inc(pool_step, 1)

                def over_norm(n):
                    reach(pool, floor_done, n + 1)
                    settle(pool, held)
                    reach(pool, rotated_done, n)
                    settle(pool, held)
                    pool.tensor_tensor(inv_norm[:], squared_norm[:], minus_half[:], ALU.pow).then_inc(inv_done, 1)
                    reach(pool, pool_step, n + 1)
                    settle(pool, held)
                    reach(pool, inv_done, n + 1)
                    settle(pool, held)
                    pool.tensor_tensor(rotated[:], rotated[:], inv_norm[:].unsqueeze(2).to_broadcast([P, 16, LDH]),
                                       ALU.mult).then_inc(rotated_done, 1)

                def scale(k, s):
                    reach(pool, inv_sum_done, k + 1)
                    settle(pool, held)
                    pool.tensor_tensor(probs[s][:, :, P - LWIN:], probs[s][:, :, P - LWIN:],
                                       inv_sum[:, s, :].unsqueeze(2).to_broadcast([P, G, KEYS]), ALU.mult)\
                        .then_inc(scaled_done, 1)

                take(0, 0)
                take(0, 1)
                pool.memset(minus_half[:], -0.5)
                for t in probs + [k_ring] + q_T[0] + q_T[1]:
                    pool.memset(t[:], 0.0)
                pool.memset(v_ring[:, 0, :], 0.0).then_inc(ready, 1)
                pool.wait_ge(ready, 1)
                add_products(0)
                over_norm(0)
                pool.wait_ge(qkv_done, 1)
                take(0, 2)
                add_products(1)
                over_norm(1)

                def turn(b, t):
                    T = b * TB + t
                    scale(2 * T, 0)
                    reach(pool, qkv_done, T + 2)
                    ahead = t + 3
                    take(b if ahead < TB else (b + 1) % BATCH, ahead % TB)
                    add_products(T + 2)
                    scale(2 * T + 1, 1)
                    over_norm(T + 2)

                batches(pool, turn)

            @block.tensor
            def _(pe):
                def qkv(n, t):
                    reach(pe, h_done, n + 1)
                    reach(pe, rotate_done, n)
                    reach(pe, square_done, 2 * n)
                    for a in range(3):
                        if a == 2:
                            reach(pe, v_done, n)
                            reach(pe, z_done, n - 4)
                        mm = pe.matmul(g.ps[:, a, :], h_tile[t % 2][:], w[:, a * INNER:(a + 1) * INNER], start=True, stop=True)
                    mm.then_inc(qkv_done, 1)

                def scores(k, t, s):
                    reach(pe, probs_done, k)
                    for j in range(G):
                        h = s * G + j
                        mm = pe.matmul(g.ps[:, 3 + j // 2, j % 2 * KEYS:(j % 2 + 1) * KEYS], q_T[t % 2][h % 2][:, h // 2, :],
                                       k_ring[:, h // 2, t * P + P - LWIN:(t + 2) * P], start=True, stop=True)
                    mm.then_inc(scores_done, 1)

                def turn_probs(k, s, fronts=None):
                    reach(pe, scaled_done, k + 1)
                    if s == 0:
                        reach(pe, q_out, fronts)
                        reach(pe, k_out, fronts)
                    else:
                        reach(pe, turned5, k)
                        reach(pe, turned6, k)
                    for j in range(G):
                        for own in range(2):
                            col = j % 2 * 2 * P + own * P
                            mm = pe.transpose(g.ps[:, 5 + j // 2, col:col + P], probs[s][:, j, own * P:(own + 1) * P], g.ident[:])
                    mm.then_inc(turn_done, 1)

                def product(k, t, s):
                    reach(pe, turned5, k + 1)
                    reach(pe, turned6, k + 1)
                    reach(pe, out_done, k)
                    for pair in range(2):
                        for own in range(2):
                            for odd in range(2):
                                h = s * G + 2 * pair + odd
                                col = odd * 2 * P + own * P
                                mm = pe.matmul(g.ps[64 * odd:64 * odd + 64, 7, h // 2 * P:(h // 2 + 1) * P],
                                               v_ring[:, t + own, h * LDH:(h + 1) * LDH], probs_T[s][:, pair, col:col + P],
                                               start=(own == 0), stop=(own == 1), tile_position=(0, 64 * odd))
                    mm.then_inc(product_done, 1)

                def project(n):
                    reach(pe, out_done, 2 * n + 2)
                    reach(pe, v_done, n + 5 if not isinstance(n, int) else min(n + 5, BATCH * TB + 2))
                    for j in range(4):
                        mm = pe.matmul(g.ps[:, 2, 0:P], wo[:, j, :], out_T[:, j, :], start=(j == 0), stop=(j == 3))
                    mm.then_inc(proj_done, 1)

                def front_turn(n):
                    reach(pe, rotated_done, n + 1)
                    reach(pe, turned5, 2 * n - 2)
                    reach(pe, turned6, 2 * n - 2)
                    for a in range(2):
                        for j in range(4):
                            mm = pe.transpose(g.ps[:, 5 + a, j * P:(j + 1) * P],
                                              rotated[:, 8 * a + 2 * j:8 * a + 2 * j + 2, :].rearrange("p h d -> p (h d)"),
                                              g.ident[:])
                    mm.then_inc(front_done, 1)

                def turn(b, t):
                    T = b * TB + t
                    qkv(T + 2, t + 2)
                    scores_at(b, t, 0)
                    if exists(b, t, 1):
                        turn_probs(2 * T - 1, 1)
                    if exists(b, t, 2):
                        project(T - 2)
                    if exists(b, t, 1):
                        product(2 * T - 2, (t - 1) % TB, 0)
                    scores_at(b, t, 1)
                    front_turn(T + 1)
                    if exists(b, t, 1):
                        product(2 * T - 1, (t - 1) % TB, 1)
                    turn_probs(2 * T, 0, fronts=T + 2)

                def scores_at(b, t, s):
                    T = b * TB + t
                    if s == 0:
                        reach(pe, q_out, T + 1)
                        reach(pe, k_out, T + 1)
                    scores(2 * T + s, t, s)

                pe.wait_ge(loaded, 96)
                pe.wait_ge(ready, 1)
                qkv(0, 0)
                front_turn(0)
                qkv(1, 1)
                batches(pe, turn)
                last = BATCH * TB - 1
                project(last - 1)
                turn_probs(2 * last + 1, 1)
                product(2 * last, TB - 1, 0)
                product(2 * last + 1, TB - 1, 1)
                pe.wait_ge(z_done, last)
                project(last)

            @block.scalar
            def _(act):
                def square(n):
                    reach(act, qkv_done, n + 1)
                    reach(act, sum_done, n)
                    for a in range(2):
                        act.activation(squares[:, a * INNER:(a + 1) * INNER], g.ps[:, a, :], ACT.Square).then_inc(square_done, 1)

                def take_v(n, t):
                    reach(act, qkv_done, n + 1)
                    act.activation(v_ring[:, t % TB + 1, :], g.ps[:, 2, :], ACT.Copy).then_inc(v_done, 1)

                def exps(k, s):
                    reach(act, min_done, k + 1)
                    reach(act, turn_done, k - 1)
                    reach(act, inv_sum_done, k - 1)
                    for j in range(G):
                        done = act.activation(probs[s][:, j, P - LWIN:], g.ps[:, 3 + j // 2, j % 2 * KEYS:(j % 2 + 1) * KEYS],
                                              ACT.Exp, bias=row_min[:, s, j:j + 1], scale=-1.0,
                                              accum_out=row_sum[:, s, j:j + 1])
                    done.then_inc(probs_done, 1)

                def evacuate(k, s):
                    reach(act, turn_done, k + 1)
                    reach(act, product_done, k - 1)
                    act.activation(probs_T[s][:, 1, :], g.ps[:, 6, :], ACT.Copy).then_inc(turned6, 1)

                def take_out(k, s):
                    reach(act, product_done, k + 1)
                    act.activation(flat(out_T[:, 2 * s:2 * s + 2, :]), g.ps[:, 7, 2 * s * P:2 * (s + 1) * P], ACT.Copy)\
                       .then_inc(out_done, 1)

                def take_qk(n, t):
                    reach(act, front_done, n + 1)
                    act.activation(flat(q_T[t % 2][1][LOW]), g.ps[LOW, 5, :], ACT.Copy)
                    t = t % TB + 1
                    act.activation(k_ring[:, :, t * P:(t + 1) * P], g.ps[:, 6, :].rearrange("p (j t) -> p j t", j=4), ACT.Copy)\
                       .then_inc(k_out, 1)

                def turn(b, t):
                    T = b * TB + t
                    square(T + 2)
                    take_v(T + 2, t + 2)
                    exps(2 * T, 0)
                    if exists(b, t, 1):
                        evacuate(2 * T - 1, 1)
                        take_out(2 * T - 2, 0)
                    take_qk(T + 1, t + 1)
                    exps(2 * T + 1, 1)
                    if exists(b, t, 1):
                        take_out(2 * T - 1, 1)
                    evacuate(2 * T, 0)

                act.wait_ge(ready, 1)
                square(0)
                take_v(0, 0)
                take_qk(0, 0)
                square(1)
                take_v(1, 1)
                batches(act, turn)
                last = BATCH * TB - 1
                evacuate(2 * last + 1, 1)
                take_out(2 * last, 0)
                take_out(2 * last + 1, 1)

            @block.vector
            def _(dve):
                def rotate(n, t, a):
                    reach(dve, square_done, 2 * n + 1 + a)
                    if a == 0:
                        reach(dve, pool_step, n)
                    wide = [P, 8, LDH]
                    qk = heads_of(g.ps[:, a, :])
                    dve.tensor_tensor(by_cos[:, 8 * a:8 * a + 8, :], qk, rot[:, t % TB, a, 0, :].unsqueeze(1).to_broadcast(wide), ALU.mult)
                    for h in range(2):
                        d, o = slice(32 * h, 32 * h + 32), slice(32 - 32 * h, 64 - 32 * h)
                        last = dve.tensor_tensor(by_sin[:, 8 * a:8 * a + 8, d], qk[:, :, o],
                                                 rot[:, t % TB, a, 1, d].unsqueeze(1).to_broadcast([P, 8, 32]), ALU.mult)
                    if a == 1:
                        last.then_inc(rotate_done, 1)

                def sum_squares(n):
                    reach(dve, square_done, 2 * n + 2)
                    reach(dve, inv_done, n)
                    dve.tensor_reduce(squared_norm[:], heads_of(squares[:]), AX, ALU.add).then_inc(sum_done, 1)

                def floor_norm(n):
                    reach(dve, sum_done, n + 1)
                    dve.tensor_scalar(squared_norm[:], squared_norm[:], 1e-24, None, ALU.max).then_inc(floor_done, 1)

                def mins(k, t, s):
                    reach(dve, scores_done, k + 1)
                    settle(dve, held_dve)
                    for j in range(G):
                        sc = g.ps[:, 3 + j // 2, j % 2 * KEYS:(j % 2 + 1) * KEYS]
                        last = dve.tensor_tensor_reduce(out=sc, in0=sc, in1=mask[:, min(t, 1), :], scale=1.0, scalar=3e38,
                                                        op0=ALU.add, op1=ALU.min, accum_out=row_min[:, s, j:j + 1])
                    last.then_inc(min_done, 1)

                def invert_sum(k, s):
                    reach(dve, probs_done, k + 1)
                    reach(dve, scaled_done, k - 1)
                    dve.reciprocal(inv_sum[:, s, :], row_sum[:, s, :]).then_inc(inv_sum_done, 1)

                def evacuate(k, s):
                    reach(dve, turn_done, k + 1)
                    reach(dve, product_done, k - 1)
                    dve.tensor_copy(probs_T[s][:, 0, :], g.ps[:, 5, :]).then_inc(turned5, 1)

                def take_q(n, t):
                    reach(dve, front_done, n + 1)
                    dve.tensor_copy(flat(q_T[t % 2][0][TOP]), g.ps[TOP, 5, :]).then_inc(q_out, 1)

                def add(n, b, t):
                    reach(dve, proj_done, n + 1)
                    for rows in (TOP, LOW):
                        last = dve.tensor_tensor(shifted(g.zB, rows, b, t * P, P), shifted(g.zA, rows, b, t * P, P),
                                                 g.ps[rows, 2, 0:P], ALU.add)
                    last.then_inc(z_done, 1)

                def turn(b, t):
                    T = b * TB + t
                    mins(2 * T, t, 0)
                    if exists(b, t, 1):
                        evacuate(2 * T - 1, 1)
                    rotate(T + 2, t + 2, 0)
                    if exists(b, t, 2):
                        add(T - 2, b if t >= 2 else b - 1, (t - 2) % TB)
                    invert_sum(2 * T, 0)
                    rotate(T + 2, t + 2, 1)
                    mins(2 * T + 1, t, 1)
                    take_q(T + 1, t + 1)
                    sum_squares(T + 2)
                    floor_norm(T + 2)
                    invert_sum(2 * T + 1, 1)
                    evacuate(2 * T, 0)

                dve.wait_ge(loaded, 96)
                dve.wait_ge(ready, 1)
                for a in range(2):
                    sc = scale_rows[:, a, :]
                    for h in range(2):
                        d, o = slice(32 * h, 32 * h + 32), slice(32 - 32 * h, 64 - 32 * h)
                        last = dve.tensor_tensor(rot[:, :, a, 1, d], rot[:, :, a, 1, d], sc[:, o].unsqueeze(1).to_broadcast([P, TB, 32]), ALU.mult)
                    last = dve.tensor_tensor(rot[:, :, a, 0, :], rot[:, :, a, 0, :], sc.unsqueeze(1).to_broadcast([P, TB, LDH]), ALU.mult)
                last.then_inc(tables, 1)
                dve.wait_ge(tables, 1)
                dve.tensor_scalar(rot[:, :, 0], rot[:, :, 0], -8.0, None, ALU.mult).then_inc(tables, 1)
                dve.wait_ge(tables, 2)
                rotate(0, 0, 0)
                rotate(0, 0, 1)
                sum_squares(0)
                floor_norm(0)
                take_q(0, 0)
                rotate(1, 1, 0)
                rotate(1, 1, 1)
                sum_squares(1)
                floor_norm(1)
                batches(dve, turn)
                last = BATCH * TB - 1
                add(last - 1, BATCH - 1, TB - 2)
                evacuate(2 * last + 1, 1)
                add(last, BATCH - 1, TB - 1)


def mlp(nc, g, layer):
    stage_sems = []
    with ExitStack() as ctx:
        ctx.callback(give_back, nc, stage_sems)

        def sb(name, shape, dt=F32):
            return ctx.enter_context(nc.sbuf_tensor(f"m{layer}_{name}", shape, dt))

        def sem(name):
            return kept(nc, stage_sems, f"m{layer}_{name}")

        CHUNKS = TOKENS // BANK
        SIZES = (P, P, LHID - 2 * P)
        w1 = sb("w1", [P, 2 * LHID])
        w1_scaled = sb("w1_scaled", [P, 2 * LHID])
        w2 = sb("w2", [P, 3, DIM])
        b1 = sb("b1", [P, 2, 3])
        cols = sb("cols", [P, 3])
        mean_of = sb("mean_of", [P, P])
        centred = sb("centred", [P, BANK])
        squares = sb("squares", [P, BANK])
        variance = sb("variance", [P, BANK])
        std = sb("std", [P, BANK])
        rstd = sb("rstd", [P, BANK])
        normed = [sb(f"normed{n}", [P, BANK]) for n in range(2)]
        gelu = [sb(f"gelu{n}", [P, BANK]) for n in range(2)]
        hidden = [sb(f"hidden{n}", [P, BANK]) for n in range(3)]
        loaded, ready, shift_mm, folded = sem("loaded"), sem("ready"), sem("shift_mm"), sem("folded")
        mean_done, centred_done, square_done, var_done, eps_done, std_done, rstd_done, normed_done = map(sem, (
            "mean_done", "centred_done", "square_done", "var_done", "eps_done", "std_done", "rstd_done", "normed_done"))
        up_done, gelu_done, hidden_done, down_done, z_done, held = map(sem, (
            "up_done", "gelu_done", "hidden_done", "down_done", "z_done", "held"))

        def unit_cols(k, j):
            start = k * LHID + j * P
            return slice(start, start + SIZES[j])

        def z_shifted(z, c):
            return z[:, ds(c // 2, 1), ds((c % 2) * BANK, BANK)].rearrange("p a t -> p (a t)")

        with nc.Block() as block:
            @block.sync
            def _(sp):
                for dst, src in ((w1[:], g.mw1[layer]), (w2[:], g.mw2[layer]), (b1[:], g.mb1[layer]), (cols[:], g.mcols[layer])):
                    sp.dma_start(dst, src).then_inc(loaded, 16)

            @block.gpsimd
            def _(pool):
                pool.memset(mean_of[:], 1.0 / DIM).then_inc(ready, 1)

            @block.tensor
            def _(pe):
                def mean(n, c):
                    pe.wait_ge(centred_done, n + 1)
                    pe.matmul(g.ps[:, 0, :], mean_of[:], z_shifted(g.zB, c), start=True, stop=True).then_inc(mean_done, 1)

                def var(n):
                    pe.wait_ge(square_done, n + 1)
                    pe.wait_ge(eps_done, n + 1)
                    pe.matmul(g.ps[:, 1, :], mean_of[:], squares[:], start=True, stop=True).then_inc(var_done, 1)

                def up(c, u, j):
                    i = 3 * u + j
                    pe.wait_ge(normed_done, c + 1)
                    pe.wait_ge(hidden_done, c * 3 + j + 1)
                    for k in range(2):
                        mm = pe.matmul(g.ps[0:SIZES[j], 2 + 2 * k + i % 2, :], w1_scaled[:, unit_cols(k, j)], normed[u][:],
                                       start=True, stop=True)
                    mm.then_inc(up_done, 1)

                def down(c, u, j):
                    pe.wait_ge(hidden_done, c * 3 + j + 3)
                    if j == 0:
                        pe.wait_ge(z_done, c + 1)
                    pe.matmul(g.ps[:, 6 + u, :], w2[0:SIZES[j], j, :], hidden[j][0:SIZES[j], :], start=(j == 0),
                              stop=(j == 2)).then_inc(down_done, 1)

                pe.sem_inc(down_done, 3)
                pe.wait_ge(loaded, 64)
                pe.wait_ge(ready, 1)
                for k in range(2):
                    for j in range(3):
                        mm = pe.matmul(g.ps[0:SIZES[j], 7, 3 * k + j:3 * k + j + 1], w1[:, unit_cols(k, j)], cols[:, 1:2],
                                       start=True, stop=True)
                mm.then_inc(shift_mm, 1)
                pe.wait_ge(folded, 1)
                mean(0, 0)
                var(0)
                with pe.Fori(0, CHUNKS // 2) as cc:
                    for u in range(2):
                        c = cc * 2 + u
                        up(c, u, 0)
                        mean(c + 1, (c + 1) % CHUNKS)
                        up(c, u, 1)
                        down(c, u, 0)
                        up(c, u, 2)
                        down(c, u, 1)
                        var(c + 1)
                        down(c, u, 2)

            @block.scalar
            def _(act):
                def square(n):
                    act.wait_ge(centred_done, n + 2)
                    if not isinstance(n, int):
                        act.wait_ge(var_done, n)
                    act.activation(squares[:], centred[:], ACT.Square).then_inc(square_done, 1)

                def root(n):
                    act.wait_ge(eps_done, n + 2)
                    act.activation(std[:], variance[:], ACT.Sqrt).then_inc(std_done, 1)

                def gate(c, u, j):
                    i = 3 * u + j
                    act.wait_ge(up_done, c * 3 + j + 1)
                    rows = slice(0, SIZES[j])
                    act.activation(gelu[i % 2][rows, :], g.ps[rows, 4 + i % 2, :], ACT.Gelu, bias=b1[rows, 1, j:j + 1])\
                       .then_inc(gelu_done, 1)

                square(0)
                root(0)
                with act.Fori(0, CHUNKS // 2) as cc:
                    for u in range(2):
                        c = cc * 2 + u
                        gate(c, u, 0)
                        square(c + 1)
                        gate(c, u, 1)
                        gate(c, u, 2)
                        root(c + 1)

            @block.vector
            def _(dve):
                dve.sem_inc(eps_done, 1)
                dve.sem_inc(hidden_done, 2)
                dve.sem_inc(z_done, 2)
                dve.wait_ge(loaded, 64)
                dve.tensor_scalar(w1_scaled[:], w1[:], cols[:, 0:1], None, ALU.mult)
                dve.wait_ge(shift_mm, 1)
                shifts = g.ps[:, 7, 0:6].rearrange("p (k j) -> p k j", k=2)
                last_rows = slice(0, SIZES[2])
                dve.tensor_tensor(b1[:, :, 0:2], b1[:, :, 0:2], shifts[:, :, 0:2], ALU.add)
                dve.tensor_tensor(b1[last_rows, :, 2:3], b1[last_rows, :, 2:3], shifts[last_rows, :, 2:3], ALU.add)\
                   .then_inc(folded, 1)
                dve.wait_ge(folded, 1)
                dve.sem_inc(centred_done, 1)

                def centre(n, c):
                    dve.wait_ge(mean_done, n + 1)
                    dve.tensor_tensor(centred[:], z_shifted(g.zB, c), g.ps[:, 0, :], ALU.subtract).then_inc(centred_done, 1)

                def norm(n, u):
                    dve.wait_ge(var_done, n + 1)
                    dve.tensor_scalar(variance[:], g.ps[:, 1, :], EPS, None, ALU.add).then_inc(eps_done, 1)
                    dve.wait_ge(std_done, n + 1)
                    dve.reciprocal(rstd[:], std[:]).then_inc(rstd_done, 1)
                    dve.wait_ge(rstd_done, n + 1)
                    dve.tensor_tensor(normed[u][:], centred[:], rstd[:], ALU.mult).then_inc(normed_done, 1)

                def multiply(c, u, j):
                    i = 3 * u + j
                    rows = slice(0, SIZES[j])
                    dve.wait_ge(gelu_done, c * 3 + j + 1)
                    dve.wait_ge(down_done, c * 3 + j + 1)
                    dve.scalar_tensor_tensor(hidden[j][rows, :], g.ps[rows, 2 + i % 2, :], b1[rows, 0, j:j + 1],
                                             gelu[i % 2][rows, :], ALU.add, ALU.mult).then_inc(hidden_done, 1)

                def add(c, u):
                    dve.wait_ge(down_done, c * 3 + 6)
                    for rows in (TOP, LOW):
                        t0 = (c % 2) * BANK
                        last = dve.scalar_tensor_tensor(shifted(g.zA, rows, c // 2, t0, BANK), g.ps[rows, 6 + u, :], cols[rows, 2:3],
                                                        shifted(g.zB, rows, c // 2, t0, BANK), ALU.add, ALU.add)
                    last.then_inc(z_done, 1)

                centre(0, 0)
                norm(0, 0)
                with dve.Fori(0, CHUNKS // 2) as cc:
                    for u in range(2):
                        c = cc * 2 + u
                        centre(c + 1, (c + 1) % CHUNKS)
                        multiply(c, u, 0)
                        multiply(c, u, 1)
                        multiply(c, u, 2)
                        norm(c + 1, 1 - u)
                        add(c, u)


def clear_first_token(nc, g):
    with nc.Block() as block:
        @block.gpsimd
        def _(pool):
            for z in (g.zA, g.zB):
                pool.memset(z[LOW, :, 0:1], 0.0)


def finish(nc, g):
    stage_sems = []
    with ExitStack() as ctx:
        ctx.callback(give_back, nc, stage_sems)

        def sem(name):
            return kept(nc, stage_sems, "f_" + name)

        gated = [ctx.enter_context(nc.sbuf_tensor(f"f_gated{n}", [P, 4, DIM], F32)) for n in range(2)]
        turned, scaled, added, stored = map(sem, ("turned", "scaled", "added", "stored"))
        CHUNKS = TOKENS // BANK
        with nc.Block() as block:
            @block.tensor
            def _(pe):
                for c in range(CHUNKS):
                    if c >= 4:
                        pe.wait_ge(scaled, c - 3)
                    for t in range(4):
                        b, t0 = c // 2, (c % 2) * BANK + t * P
                        for n, (rows, lag) in enumerate(((TOP, 0), (LOW, 1))):
                            mm = pe.transpose(g.ps[:, 2 * (c % 4) + n, t * 64:t * 64 + 64],
                                              g.zA[rows, b, t0 + lag:t0 + lag + P], g.ident[rows, rows])
                    mm.then_inc(turned, 1)

            @block.vector
            def _(dve):
                for c in range(CHUNKS):
                    dve.wait_ge(turned, c + 1)
                    for n, feats in enumerate((TOP, LOW)):
                        last = dve.tensor_tensor(gated[c % 2][:, :, feats], g.ps[:, 2 * (c % 4) + n, 0:256].rearrange("p (t d) -> p t d", t=4),
                                                 g.gate_rows[:, 1, 1, c // 2:c // 2 + 1, feats].to_broadcast([P, 4, 64]), ALU.mult)
                    last.then_inc(scaled, 1)
                    dve.wait_ge(scaled, c + 1)
                    rowsx = g.x[:, 4 * c:4 * c + 4, :]
                    dve.tensor_tensor(rowsx, rowsx, gated[c % 2][:], ALU.add).then_inc(added, 1)

            @block.sync
            def _(sp):
                for c in range(CHUNKS):
                    sp.wait_ge(added, c + 1)
                    sp.dma_start(g.out[c // 2, :, 4 * (c % 2):4 * (c % 2) + 4, :], g.x[:, 4 * c:4 * c + 4, :]).then_inc(stored, 16)
                sp.wait_ge(stored, 16 * CHUNKS)


def program(nc, g, stages=("l0a", "l0f", "l1a", "l1f")):
    with ExitStack() as ctx:
        allocate(nc, ctx, g)
        g.qk_dram = nc.dram_tensor("qk_dram", [3, 2, P, TOKENS], BF16, kind="Internal").ap()
        g.bias_dram_t = nc.dram_tensor("bias_dram", [HEADS, 384], F32, kind="Internal")
        g.bias_dram = g.bias_dram_t.ap()

        g.toeplitz_src = bass.AP(g.bias_dram_t, 0, [[1, P], [384, HEADS], [1, 2 * P]])
        with ExitStack() as first:
            g.toeplitz_all = first.enter_context(nc.sbuf_tensor("toeplitz_all", [P, HEADS, 2 * P], F32))
            g.ga_bo = first.enter_context(nc.sbuf_tensor("ga_bo", [P, BATCH, DIM], F32))
            g.v_all = first.enter_context(nc.sbuf_tensor("v_all", [P, TILES, DIM], F32))
            setup(nc, g)
            if "l0a" in stages:
                norm_modulate(nc, g, 0, 0, add_ga_bo=True)
                split_project(nc, g)
                attention(nc, g, 0)
        if "l0f" in stages:
            norm_modulate(nc, g, 0, 1)
            experts(nc, g)
        if "l1a" in stages:
            norm_modulate(nc, g, 1, 0)
            attention(nc, g, 1)
        if "l1f" in stages:
            g.zA = ctx.enter_context(nc.sbuf_tensor("zA", [P, BATCH, SEQ + 1], F32))
            g.zB = ctx.enter_context(nc.sbuf_tensor("zB", [P, BATCH, SEQ + 1], F32))
            clear_first_token(nc, g)
            norm_modulate(nc, g, 1, 1, shift=True)
            for layer in range(LDEPTH):
                local_attention(nc, g, layer)
                mlp(nc, g, layer)
            finish(nc, g)
        else:
            store(nc, g)


def store(nc, g):
    stored = nc.alloc_semaphore("stored")
    with nc.Block() as block:
        @block.sync
        def _(sp):
            for b in range(BATCH):
                sp.dma_start(g.out[b], g.x[:, b * TB:(b + 1) * TB, :]).then_inc(stored, 16)
            sp.wait_ge(stored, 16 * BATCH)


def lay_out(inputs):
    f = {k: np.ascontiguousarray(v) for k, v in inputs.items()}
    a = {}
    a["x_in"] = f["L0_attn_x"].reshape(BATCH, TB, P, DIM).transpose(0, 2, 1, 3)
    a["cT"] = np.stack([f["L0_c"].T, f["L1_c"].T], 1)
    a["wmod"] = np.stack([f["L0_wmod"], f["L1_wmod"]], 1)
    a["bo"] = f["L0_attn_bo"]
    a["rel_emb"] = f["L0_attn_rel_emb"]
    a["ident_in"] = np.eye(P, dtype=np.float32)
    a["flip_in"] = np.eye(P, dtype=np.float32)[::-1]
    a["bias_sel"] = bias_selector()
    a["w0_qkv"] = np.stack([f["L0_attn_Wq"], f["L0_attn_Wk"], f["L0_attn_Wv"]], 1)
    a["w0_out"] = f["L0_attn_Wo"]
    a["w1_qk"] = np.stack([f["L1_attn_Wq"], f["L1_attn_Wk"]])
    def hidden_first(w):
        return w.transpose(2, 0, 1)

    a["w1"] = hidden_first(f["L0_ffn_W1"])
    a["w3"] = hidden_first(f["L0_ffn_W3"])
    a["w2"] = f["L0_ffn_W2"].transpose(2, 0, 1).reshape(2, P, EXPERTS, DIM).transpose(1, 2, 0, 3)
    a["lora_a"] = np.stack([f["L0_ffn_A1"], f["L0_ffn_A3"]]).transpose(2, 0, 1, 3)
    a["lora_b"] = np.stack([f["L0_ffn_B1"], f["L0_ffn_B3"]]).transpose(3, 0, 1, 2)
    a["lora_a2"] = f["L0_ffn_A2"].transpose(1, 0, 2)
    a["lora_b2"] = f["L0_ffn_B2"].transpose(2, 0, 1)
    a["w_gate"] = f["L0_ffn_Wg"].T
    a["iota"] = np.tile(np.arange(EXPERTS, dtype=np.float32), (P, 1))
    a["b13"] = np.stack([f["L0_ffn_b1"], f["L0_ffn_b3"]]).reshape(2, EXPERTS, 2, P).transpose(3, 0, 1, 2)
    a["b2"] = f["L0_ffn_b2"]
    a["wqkv"] = f["L1_ffn_wqkv"]
    a["wo"] = f["L1_ffn_wo"].reshape(LDEPTH, 4, P, DIM).transpose(0, 2, 1, 3)
    a["q_scale"], a["k_scale"] = f["L1_ffn_q_scale"], f["L1_ffn_k_scale"]
    a["rotary"] = rotary_tables().reshape(2, 2, TB, P, LDH).transpose(3, 2, 0, 1, 4)
    band = band_mask()[:, 64:]
    no_past = band.copy()
    no_past[:, :64] = BIG
    a["band"] = np.stack([no_past, band], 1)
    a["mw1"] = f["L1_ffn_w1"]
    def hidden_tiles(w):
        out = np.zeros((w.shape[0], 3 * P, w.shape[2]), w.dtype)
        out[:, :LHID] = w
        return out.reshape(w.shape[0], 3, P, w.shape[2]).transpose(0, 2, 1, 3)

    a["mw2"] = hidden_tiles(f["L1_ffn_w2"])
    a["mb1"] = hidden_tiles(f["L1_ffn_b1"].reshape(LDEPTH, 2, LHID).transpose(0, 2, 1)).transpose(0, 1, 3, 2)
    a["mcols"] = np.stack([f["L1_ffn_ln_g"], f["L1_ffn_ln_b"], f["L1_ffn_b2"]], -1)
    a["w1_v"] = f["L1_attn_Wv"]
    a["w1_out"] = f["L1_attn_Wr"]
    return {k: np.ascontiguousarray(v) for k, v in a.items()}


_OUT = (BATCH, P, TB, DIM)


def kernel(**inputs):
    import numpy as _np
    import concourse.bacc as _bacc
    from concourse import mybir as _mybir
    from concourse.bass_utils import run_bass_kernel_spmd as _run

    nc = _bacc.Bacc("TRN2", target_bir_lowering=False, num_devices=1)
    arrays = lay_out(inputs)
    chip = Chip()
    fed = {}
    for name, a in arrays.items():
        fed[f"in_{name}"] = a
        chip.__dict__[name] = nc.dram_tensor(f"in_{name}", a.shape, _mybir.dt.from_np(a.dtype), kind="ExternalInput").ap()
    chip.out = nc.dram_tensor("out_0_dram", _OUT, _mybir.dt.float32, kind="ExternalOutput").ap()
    program(nc, chip)
    r = _run(nc, [fed], core_ids=[0])
    got = r.results[0]["out_0_dram"]
    return _np.ascontiguousarray(got.reshape(_OUT).transpose(0, 2, 1, 3).reshape(BATCH, SEQ, DIM))
```

```python
import math
from contextlib import ExitStack

import numpy as np

import concourse.bass as bass
from concourse import mybir

F32 = mybir.dt.float32
F32R = mybir.dt.float32r
BF16 = mybir.dt.bfloat16
U32 = mybir.dt.uint32
ALU = mybir.AluOpType
ACT = mybir.ActivationFunctionType
AX = mybir.AxisListType.X
ds = bass.ds

P = 128
BATCH, SEQ, DIM = 4, 1024, 128
TOKENS = BATCH * SEQ
TILES = TOKENS // P
TB = SEQ // P
BANK = 512
HEADS = 16
PAIRS = BATCH * HEADS // 2
BIG = 1e30
BUCKETS, MAX_DISTANCE = 32, 128
EXPERTS, HIDDEN, RANK = 8, 256, 16
LDEPTH, LHEADS, LDH, LWIN = 2, 8, 64, 64
INNER = LHEADS * LDH
LHID = int(DIM * 4 * 2 / 3)
EPS = 1e-5



def bias_selector():
    n = 255 - np.arange(384)
    exact = BUCKETS // 2
    pos = np.maximum(n, 1).astype(np.float32)
    large = exact + (np.log(pos / exact) / np.float32(math.log(MAX_DISTANCE / exact)) * (BUCKETS - exact)).astype(np.int32)
    bucket = np.where(n < exact, np.maximum(n, 0), np.minimum(large, BUCKETS - 1))
    sel = np.zeros((BUCKETS + 1, 384), np.float32)
    sel[bucket, np.arange(384)] = -1.0
    sel[BUCKETS - 1] += 1.0
    sel[:, n < 0] = 0.0
    sel[BUCKETS, n < 0] = BIG
    return sel


def rotary_tables():
    half = np.arange(0, LDH, 2, dtype=np.float32)
    inv = (1.0 / 10000.0 ** (half / LDH)).astype(np.float32)
    t = np.arange(SEQ, dtype=np.float32)
    f = (t[:, None] * inv[None, :]).astype(np.float32)
    f = np.concatenate([f, f], -1)
    base = ((half + 0.4 * LDH) / (1.4 * LDH)).astype(np.float32)
    power = ((t - SEQ // 2) / float(LWIN // 2)).astype(np.float32)
    s = (base[None, :] ** power[:, None]).astype(np.float32)
    s = np.concatenate([s, s], -1)
    sign = np.where(np.arange(LDH) < LDH // 2, -1.0, 1.0).astype(np.float32)
    c, n = np.cos(f), np.sin(f) * sign
    return np.stack([c * s, n * s, c / s, n / s]).astype(np.float32)


def band_mask():
    d = np.arange(P)[:, None] + P - np.arange(2 * P)[None, :]
    return np.where((d >= 0) & (d <= LWIN), 0.0, BIG).astype(np.float32)


class Chip:
    pass


def allocate(nc, ctx, g):
    def sb(name, shape, dt=F32):
        return ctx.enter_context(nc.sbuf_tensor(name, shape, dt))

    g.x = sb("x", [P, TILES, DIM])
    g.hT = sb("hT", [P, TOKENS])
    g.ident = sb("ident", [P, P])
    g.mod_cols = sb("mod_cols", [P, 2, 6, BATCH])
    g.gate_rows = sb("gate_rows", [P, 2, 2, BATCH, DIM])
    g.ps = ctx.enter_context(nc.psum_tensor("ps", [P, 8, BANK], F32))


def kept(nc, stage_sems, name):
    stage_sems.append(nc.alloc_semaphore(name))
    return stage_sems[-1]


def give_back(nc, stage_sems):
    nc.clear_and_free_semaphores(stage_sems)
    nc.all_engine_barrier()


def setup(nc, g):
    stage_sems = []
    with ExitStack() as ctx:
        ctx.callback(give_back, nc, stage_sems)

        def sb(name, shape, dt=F32):
            return ctx.enter_context(nc.sbuf_tensor(name, shape, dt))

        def sem(name):
            return kept(nc, stage_sems, name)

        cT = sb("cT", [P, 2, BATCH])
        silu_c = sb("silu_c", [P, 2, BATCH])
        silu_wide = sb("silu_wide", [P, 2, BATCH, P])
        wmod = sb("wmod", [P, 2, 6 * DIM])
        gabs = sb("gabs", [P, 2 * BATCH * DIM])
        gsgn = sb("gsgn", [P, 2 * BATCH * DIM])
        raw = sb("raw", [P, 2 * BATCH * DIM])
        rel = sb("rel", [BUCKETS + 1, HEADS])
        sel = sb("sel", [BUCKETS + 1, 384])
        bias_sb = sb("bias_sb", [HEADS, 384])
        bo_row = sb("bo_row", [P, DIM])
        mirrored = sb("mirrored", [P, HEADS, 2 * P])
        mirrored_in, flip_mm, flip_out = sem("set_mirrored_in"), sem("set_flip_mm"), sem("set_flip_out")
        flip = sb("flip", [P, P])
        FLIPS = HEADS * 2 * P // BANK
        loaded, bias_loaded, rel_one, silu_done, wide, mod_mm, mod_out, bias_out, stored, step = map(sem, (
            "set_loaded", "set_bias_loaded", "set_rel_one", "set_silu", "set_wide", "set_mod_mm",
            "set_mod_out", "set_bias_out", "set_stored", "set_step"))
        with nc.Block() as block:
            @block.sync
            def _(sp):
                sp.dma_start(cT[:], g.cT).then_inc(loaded, 16)
                sp.dma_start(wmod[:], g.wmod).then_inc(loaded, 16)
                sp.dma_start(g.ident[:], g.ident_in).then_inc(loaded, 16)
                sp.dma_start(flip[:], g.flip_in).then_inc(loaded, 16)
                sp.dma_start(bo_row[:], g.bo.partition_broadcast(P)).then_inc(loaded, 16)
                sp.dma_start(rel[0:BUCKETS, :], g.rel_emb).then_inc(bias_loaded, 16)
                sp.dma_start(sel[:], g.bias_sel).then_inc(bias_loaded, 16)
                for b in range(BATCH):
                    sp.dma_start(g.x[:, b * TB:(b + 1) * TB, :], g.x_in[b]).then_inc(loaded, 16)
                sp.wait_ge(bias_out, 1)
                sp.dma_start(g.bias_dram, bias_sb[:]).then_inc(stored, 16)
                sp.wait_ge(stored, 16)
                sp.dma_start(mirrored[:], g.toeplitz_src).then_inc(mirrored_in, 16)
                sp.wait_ge(loaded, 16 * 9)

            @block.gpsimd
            def _(pool):
                pool.memset(rel[BUCKETS:BUCKETS + 1, :], 1.0).then_inc(rel_one, 1)

            @block.scalar
            def _(act):
                act.wait_ge(loaded, 144)
                act.activation(silu_c[:], cT[:], ACT.Silu).then_inc(silu_done, 1)
                for n in range(FLIPS):
                    act.wait_ge(flip_mm, n + 1)
                    act.activation(g.toeplitz_all[:, 2 * n:2 * n + 2, :].rearrange("p h j -> p (h j)"), g.ps[:, 5 + n % 2, :],
                                   ACT.Copy).then_inc(flip_out, 1)

            @block.tensor
            def _(pe):
                pe.wait_ge(bias_loaded, 32)
                pe.wait_ge(rel_one, 1)
                pe.matmul(g.ps[0:HEADS, 7, 0:384], rel[:], sel[:], start=True, stop=True).then_inc(mod_mm, 1)
                pe.wait_ge(silu_done, 1)
                for l in range(2):
                    for j in range(6):
                        col = (l * 6 + j) * BATCH
                        mm = pe.matmul(g.ps[:, 0, col:col + BATCH], wmod[:, l, j * DIM:(j + 1) * DIM],
                                       silu_c[:, l, :], start=True, stop=True)
                mm.then_inc(mod_mm, 1)
                pe.wait_ge(wide, 1)
                for l in range(2):
                    for n, j in enumerate((2, 5)):
                        for b in range(BATCH):
                            mm = pe.matmul(g.ps[:, 1 + l * 2 + n, b * DIM:(b + 1) * DIM], silu_wide[:, l, b, :],
                                           wmod[:, l, j * DIM:(j + 1) * DIM], start=True, stop=True)
                mm.then_inc(mod_mm, 1)
                pe.wait_ge(mirrored_in, 16)
                for n in range(FLIPS):
                    if n >= 2:
                        pe.wait_ge(flip_out, n - 1)
                    pe.matmul(g.ps[:, 5 + n % 2, :], flip[:], mirrored[:, 2 * n:2 * n + 2, :].rearrange("p h j -> p (h j)"),
                              start=True, stop=True).then_inc(flip_mm, 1)

            @block.vector
            def _(dve):
                dve.wait_ge(silu_done, 1)
                dve.tensor_copy(silu_wide[:], silu_c[:].unsqueeze(3).to_broadcast([P, 2, BATCH, P])).then_inc(wide, 1)
                dve.wait_ge(mod_mm, 1)
                dve.tensor_copy(bias_sb[:], g.ps[0:HEADS, 7, 0:384]).then_inc(bias_out, 1)
                dve.wait_ge(mod_mm, 2)
                dve.tensor_copy(g.mod_cols[:].rearrange("p l j b -> p (l j b)"), g.ps[:, 0, 0:48]).then_inc(step, 1)
                dve.wait_ge(step, 1)
                for l in range(2):
                    for j in (1, 4):
                        last = dve.tensor_scalar(g.mod_cols[:, l, j, :], g.mod_cols[:, l, j, :], 1.0, None, ALU.add)
                last.then_inc(step, 1)
                dve.wait_ge(mod_mm, 3)
                for l in range(2):
                    gate = g.ps[:, 1 + l * 2:3 + l * 2, :].rearrange("p n c -> p (n c)")
                    dve.tensor_copy(raw[:], gate).then_inc(step, 1)
                    dve.wait_ge(step, 3 + 4 * l)
                    dve.scalar_tensor_tensor(gabs[:], raw[:], -1.0, raw[:], ALU.mult, ALU.max)
                    dve.tensor_scalar(gsgn[:], raw[:], 0.0, 2.0, ALU.is_ge, ALU.mult).then_inc(step, 1)
                    dve.wait_ge(step, 4 + 4 * l)
                    dve.tensor_scalar(gabs[:], gabs[:], 0.25, None, ALU.max).then_inc(step, 1)
                    dve.wait_ge(step, 5 + 4 * l)
                    dve.scalar_tensor_tensor(g.gate_rows[:, l].rearrange("p n b d -> p (n b d)"), gsgn[:], -1.0,
                                             gabs[:], ALU.add, ALU.mult).then_inc(step, 1)
                    dve.wait_ge(step, 6 + 4 * l)
                dve.wait_ge(loaded, 144)
                dve.tensor_tensor(g.ga_bo[:], g.gate_rows[:, 0, 0], bo_row[:].unsqueeze(1).to_broadcast([P, BATCH, DIM]),
                                  ALU.mult).then_inc(step, 1)


def norm_modulate(nc, g, layer, which, add_ga_bo=False, shift=False):
    tag = f"n{layer}{which}_"
    stage_sems = []
    with ExitStack() as ctx:
        ctx.callback(give_back, nc, stage_sems)

        def sem(name):
            return kept(nc, stage_sems, tag + name)

        stats = ctx.enter_context(nc.sbuf_tensor(tag + "stats", [P, TILES, 6], F32))
        mv = ctx.enter_context(nc.sbuf_tensor(tag + "mv", [P, TILES, 2], F32))
        std = ctx.enter_context(nc.sbuf_tensor(tag + "std", [P, TILES], F32))
        rstd = ctx.enter_context(nc.sbuf_tensor(tag + "rstd", [P, TILES], F32))
        xn = ctx.enter_context(nc.sbuf_tensor(tag + "xn", [P, TB, DIM], F32))
        stats_done, var_done, std_done, rstd_done, xn_done, turned, evacuated = map(sem, (
            "stats", "var", "std", "rstd", "xn", "turned", "evacuated"))
        s_cols, c_cols = g.mod_cols[:, layer, 3 * which, :], g.mod_cols[:, layer, 3 * which + 1, :]
        with nc.Block() as block:
            @block.vector
            def _(dve):
                for t in range(TILES):
                    last = dve.bn_stats(stats[:, t, :], g.x[:, t, :])
                last.then_inc(stats_done, 1)
                dve.wait_ge(stats_done, 1)
                for t in range(TILES):
                    last = dve.bn_aggr(mv[:, t, :], stats[:, t, :])
                last.then_inc(var_done, 1)
                dve.wait_ge(var_done, 1)
                dve.tensor_scalar(std[:], mv[:, :, 1], EPS, None, ALU.add).then_inc(var_done, 1)
                dve.wait_ge(std_done, 1)
                dve.reciprocal(rstd[:], std[:]).then_inc(rstd_done, 1)
                dve.wait_ge(rstd_done, 1)
                with dve.Fori(0, BATCH) as b:
                    for half in range(2):
                        dve.wait_ge(turned, 2 * b + half + 1)
                        for t in range(4 * half, 4 * half + 4):
                            tile = b * TB + t
                            last = dve.tensor_scalar(xn[:, t, :], g.x[:, ds(tile, 1), :].rearrange("p a d -> p (a d)"),
                                                     mv[:, ds(tile, 1), 0:1].rearrange("p a c -> p (a c)"),
                                                     rstd[:, ds(tile, 1)], ALU.subtract, ALU.mult)
                        last.then_inc(xn_done, 1)
                    if add_ga_bo:
                        rows = g.x[:, ds(b * TB, TB), :]
                        dve.wait_ge(xn_done, 2 * b + 2)
                        dve.tensor_tensor(rows, rows, g.ga_bo[:, ds(b, 1), :].to_broadcast([P, TB, DIM]), ALU.add)

            @block.scalar
            def _(act):
                act.wait_ge(var_done, 2)
                act.activation(std[:], std[:], ACT.Sqrt).then_inc(std_done, 1)
                with act.Fori(0, BATCH) as b:
                    for half in range(2):
                        act.wait_ge(turned, 2 * b + half + 3)
                        for rows in (TOP, LOW) if shift else (slice(0, P),):
                            dst = shifted(g.zA, rows, b, half * BANK, BANK) if shift else \
                                g.hT[:, ds(b * SEQ + half * BANK, BANK)]
                            last = act.activation(dst, g.ps[rows, half, :], ACT.Identity, bias=s_cols[rows, ds(b, 1)],
                                                  scale=c_cols[rows, ds(b, 1)])
                        last.then_inc(evacuated, 1)

            @block.tensor
            def _(pe):
                pe.sem_inc(turned, 2)
                pe.sem_inc(evacuated, 2)
                with pe.Fori(0, BATCH) as b:
                    for half in range(2):
                        pe.wait_ge(xn_done, 2 * b + half + 1)
                        pe.wait_ge(evacuated, 2 * b + half + 1)
                        for t in range(4):
                            last = pe.transpose(g.ps[:, half, t * P:(t + 1) * P], xn[:, 4 * half + t, :], g.ident[:])
                        last.then_inc(turned, 1)


def split_project(nc, g):
    stage_sems = []
    with ExitStack() as ctx:
        ctx.callback(give_back, nc, stage_sems)

        def sb(name, shape, dt=F32):
            return ctx.enter_context(nc.sbuf_tensor(name, shape, dt))

        def sem(name):
            return kept(nc, stage_sems, name)

        w = sb("pj_w", [P, 3, DIM])
        parts = [sb(f"pj_part{n}", [P, 2, 2, BANK], BF16) for n in range(3)]
        rest = sb("pj_rest", [P, 2, BANK])
        w_in, scaled, q_mm, part_done, v_mm, v_out = map(sem, (
            "pj_w_in", "pj_scaled", "pj_q_mm", "pj_part_done", "pj_v_mm", "pj_v_out"))
        rest_done, mid_done = sem("pj_rest_done"), sem("pj_mid_done")
        written = [sem(f"pj_written{n}") for n in range(2)]
        CHUNKS = TOKENS // BANK
        with nc.Block() as block:
            @block.sync
            def _(sp):
                sp.dma_start(w[:], g.w0_qkv).then_inc(w_in, 16)
                for c in range(CHUNKS):
                    sp.wait_ge(part_done, c + 1)
                    for part in range(3):
                        sp.dma_start(g.qk_dram[part, :, :, c * BANK:(c + 1) * BANK].rearrange("a p n -> p a n"),
                                     parts[part][:, c % 2]).then_inc(written[c % 2], 16)
                for n in range(2):
                    sp.wait_ge(written[n], 48 * CHUNKS // 2)

            @block.tensor
            def _(pe):
                pe.wait_ge(w_in, 16)
                pe.wait_ge(scaled, 1)
                for c in range(CHUNKS):
                    if c >= 2:
                        pe.wait_ge(part_done, c - 1)
                    for a in range(2):
                        mm = pe.matmul(g.ps[:, 2 * (c % 2) + a, :], w[:, a, :], g.hT[:, c * BANK:(c + 1) * BANK],
                                       start=True, stop=True)
                    mm.then_inc(q_mm, 1)
                    if c >= 2:
                        pe.wait_ge(v_out, c - 1)
                    for t in range(4):
                        tok = c * BANK + t * P
                        mm = pe.matmul(g.ps[:, 4 + c % 2, t * P:(t + 1) * P], g.hT[:, tok:tok + P], w[:, 2, :],
                                       start=True, stop=True)
                    mm.then_inc(v_mm, 1)

            @block.vector
            def _(dve):
                dve.wait_ge(w_in, 16)
                dve.tensor_scalar(w[:, 0, :], w[:, 0, :], -float(np.float32(8 ** -0.5)), None, ALU.mult).then_inc(scaled, 1)
                for c in range(CHUNKS):
                    dve.wait_ge(q_mm, c + 1)
                    both = g.ps[:, 2 * (c % 2):2 * (c % 2) + 2, :]
                    if c >= 2:
                        dve.wait_ge(written[c % 2], 48 * (c // 2))
                    dve.tensor_copy(parts[0][:, c % 2], both).then_inc(mid_done, 1)
                    dve.wait_ge(mid_done, 2 * c + 1)
                    dve.tensor_tensor(rest[:], both, parts[0][:, c % 2], ALU.subtract).then_inc(rest_done, 1)
                    dve.wait_ge(rest_done, c + 1)
                    dve.tensor_copy(parts[1][:, c % 2], rest[:]).then_inc(mid_done, 1)
                    dve.wait_ge(mid_done, 2 * c + 2)
                    dve.tensor_tensor(parts[2][:, c % 2], rest[:], parts[1][:, c % 2], ALU.subtract).then_inc(part_done, 1)

            @block.scalar
            def _(act):
                for c in range(CHUNKS):
                    act.wait_ge(v_mm, c + 1)
                    act.activation(g.v_all[:, 4 * c:4 * c + 4, :], g.ps[:, 4 + c % 2, :].rearrange("p (t d) -> p t d", t=4),
                                   ACT.Copy).then_inc(v_out, 1)


class Plan:

    JOBS = 2 * PAIRS
    TILES_OF = ((0, 3, 4, 7), (1, 2, 5, 6))
    ORDER = (3, 2, 1, 0)

    def __init__(self, layer):
        self.layer = layer
        self.causal = layer == 0
        self.rows = 32 if layer == 0 else 64
        self.group = 2 if layer == 0 else 1
        self.GROUPS = 8 // self.group
        self.prep = 0 if layer == 0 else 6
        self.total = 0
        self.index = {}
        for n in range(self.prep):
            self.index["prep", 0, n] = self.total
            self.total += 1
        for J in range(self.JOBS + 2):
            for s in range(8):
                for kind, job, n in self.items(J, s):
                    self.index[kind, job, n] = self.total
                    self.total += 1

    def steps(self, J):
        return self.TILES_OF[J % 2][-1] + 1 if self.causal else 8

    def step(self, J):
        return J // 2 * (self.steps(0) + self.steps(1)) + (J % 2) * self.steps(0)

    def width(self, J, i):
        return (self.TILES_OF[J % 2][i] + 1) * P if self.causal else SEQ

    def plain(self, J, i):
        tile = self.TILES_OF[J % 2][i]
        return max(0, tile - 1) * P if self.causal else tile * P

    def plains(self, J, u=0):
        if J < 0:
            return 0
        per = [sum(self.plain(j, self.ORDER[s // 2]) > 0 for s in range(8)) for j in range(2)]
        return J // 2 * sum(per) + (J % 2) * per[0] + sum(self.plain(J, self.ORDER[s // 2]) > 0 for s in range(u))

    def first(self, J, kt):
        return sum(tile < kt for tile in self.TILES_OF[J % 2]) * P if self.causal else 0

    def groups(self, J):
        return -(-self.steps(J) // self.group)

    def kts(self, J, m):
        return range(self.group * m, min(self.group * (m + 1), self.steps(J)))

    def product(self, J, s):
        if s % self.group:
            return None, None
        if s:
            return J - 1, s // self.group - 1
        return J - 2, self.groups(J - 2) - 1

    def items(self, J, s):
        out = []
        if s == 1 and 0 <= J - 2 < self.JOBS:
            out.append(("y", J - 2, 0))
        if s == 2 and 0 <= J - 1 < self.JOBS:
            out.append(("r", J - 1, 0))
        if self.prep and s in (3, 5, 7) and J < self.JOBS - 2:
            out.append(("prep", J // 2 + 1, 3 * (J % 2) + (s - 3) // 2))
        return out


def at(it, jj, f):
    if isinstance(it, int):
        return f(4 * it + jj)
    per = f(4 * 3 + jj) - f(4 * 2 + jj)
    return it * per + (f(4 * 2 + jj) - 2 * per)


def wait(eng, sem, it, jj, f):
    v = at(it, jj, f)
    if not isinstance(v, int) or v > 0:
        eng.wait_ge(sem, v)


def settle(eng, sem):
    eng.sem_inc(sem, 1)


def turns(eng, plan, turn):
    last = plan.JOBS // 4 - 1
    for jj in range(4):
        turn(0, jj, jj)
    with eng.Fori(1, last) as it:
        for jj in range(4):
            turn(it, jj, 8 + jj)
    for jj in range(6):
        turn(last, jj, 4 * last + jj)


def batch_of(it, jj):
    return (4 * it + jj) // 16 if isinstance(it, int) else (it * 4 + jj) // 16


def attention(nc, g, layer):
    plan = Plan(layer)
    tag = f"a{layer}_"
    rows = plan.rows
    SLOTS = 8
    LOADS = 16 * (2 * SLOTS + 4)
    JOBS = plan.JOBS
    stage_sems = []
    with ExitStack() as ctx:
        ctx.callback(give_back, nc, stage_sems)

        def sb(name, shape, dt=F32):
            return ctx.enter_context(nc.sbuf_tensor(tag + name, shape, dt))

        def sem(name):
            return kept(nc, stage_sems, tag + name)

        if layer == 0:
            q_stack = [[sb(f"q_stack{n}", [P, 2, SEQ], BF16)] for n in range(2)]
            toeplitz = [sb(f"toeplitz{n}", [P, 2, 2 * P]) for n in range(2)]
        else:
            q_stack = [[sb(f"q_stack{n}", [P, 2, SEQ], F32R), sb(f"q_turned{n}", [P, 2, SEQ], F32R)] for n in range(2)]
            causal_rows = sb("causal_rows", [P, SEQ])
            h_pair = sb("h_pair", [P, SEQ])
            w_qk = sb("w_qk", [P, 2, 2 * 64])
            w_q = sb("w_q", [P, 2 * 64])
            w_v = sb("w_v", [P, 2 * 64])
        k_stack = [sb(f"k_stack{n}", [P, 2, SEQ], F32R if layer else BF16) for n in range(2)]
        v = [sb(f"v{n}", [P, TB, 2, rows]) for n in range(2)]
        w_out_raw = [sb(f"w_out_raw{n}", [P, DIM]) for n in range(2)]
        w_out = [sb(f"w_out{n}", [P, DIM]) for n in range(2)]
        probs = [sb(f"probs{n}", [P, 2, 4, SEQ]) for n in range(2)]
        BUFFERS = 2 * plan.group
        turned = [[sb(f"turned{h}{n}", [P, BANK]) for n in range(BUFFERS)] for h in range(2)]
        plain_min = sb("plain_min", [P, 16])
        row_min = sb("row_min", [P, 16])
        row_sum = sb("row_sum", [P, 2, 8])
        inv_sum = sb("inv_sum", [P, 8])
        inv_wide = sb("inv_wide", [P, 4, 2, 64])
        inv_rows = sb("inv_rows", [P, BANK])
        out_T = [sb(f"out_T{n}", [P, BANK]) for n in range(2)]

        scores_bank = lambda s: g.ps[:, 2 * (s % 2):2 * (s % 2) + 2, :].rearrange("p a n -> p (a n)")
        turn_bank = [g.ps[:, 4, :], g.ps[:, 5, :]]
        out_bank = g.ps[:, 6, :]
        shared = g.ps[:, 7, :]

        scores_done = sem("scores_done")
        plain_done = sem("plain_done")
        min_done = sem("min_done")
        probs_done = sem("probs_done")
        turn_done = [sem(f"turn_done{h}") for h in range(2)]
        turned_out = [sem(f"turned_out{h}") for h in range(2)]
        product_done = sem("product_done")
        inv_done = sem("inv_done")
        wide_done = sem("wide_done")
        out_done = sem("out_done")
        item_done = sem("item_done")
        item_out = sem("item_out")
        w_out_done = sem("w_out_done")
        if layer == 0:
            stack_in = [sem(f"stack_in{n}") for n in range(2)]
            v_done = sem("v_done")
            table_done = sem("table_done")
        else:
            weights_in = sem("weights_in")
            w_q_done = sem("w_q_done")
            hi_done = sem("hi_done")
            lo_done = sem("lo_done")
            turned_q = sem("turned_q")
            v_done = sem("v_done")
        cleared = sem("cleared")
        held = {e: sem("held_" + e) for e in ("dve", "pool", "sp")}

        def unit(u):
            return plan.ORDER[u // 2], u % 2

        with nc.Block() as block:
            @block.sync
            def _(sp):
                if layer == 0:
                    sp.wait_ge(cleared, 1)

                    def pair(it, n):
                        wait(sp, scores_done, it, 2 * n, lambda J: 8 * (J - 2))
                        settle(sp, held["sp"])
                        wait(sp, w_out_done, it, 2 * n, lambda J: J // 2 - 1)
                        settle(sp, held["sp"])
                        tok = (it // 4) * SEQ
                        head = (it % 4) * 4 + 2 * n
                        for slot in range(SLOTS):
                            for a, part, dst in ((0, slot // 3, q_stack[n][0]), (1, slot % 3, k_stack[n])):
                                src = g.qk_dram[part, a, ds(head * 8, 16), ds(tok, SEQ)]
                                sp.dma_start(dst[8 * slot:8 * slot + 8], src.rearrange("(h d) t -> d h t", d=8))\
                                    .then_inc(stack_in[n], 16)
                        for lane in range(4):
                            sp.dma_start(w_out_raw[n][32 * lane:32 * lane + 8, :],
                                         g.w0_out[ds((head + lane % 2) * 8, 8), :]).then_inc(stack_in[n], 16)

                    for n in range(2):
                        pair(0, n)
                    with sp.Fori(1, PAIRS // 2) as it:
                        for n in range(2):
                            pair(it, n)
                else:
                    def pair(it, n):
                        if not (isinstance(it, int) and 2 * it + n == 0):
                            wait(sp, item_done, it, 2 * n, lambda J: plan.index["prep", J // 2 - 1, 5] + 1)
                            settle(sp, held["sp"])
                            wait(sp, w_out_done, it, 2 * n, lambda J: J // 2)
                        settle(sp, held["sp"])
                        col = (it % 4) * 256 + 128 * n
                        sp.dma_start(h_pair[:], g.hT[:, ds((it // 4) * SEQ, SEQ)]).then_inc(weights_in, 16)
                        for a in range(2):
                            sp.dma_start(w_qk[:, a, :], g.w1_qk[a, :, ds(col, 128)]).then_inc(weights_in, 16)
                        sp.dma_start(w_v[:], g.w1_v[:, ds(col, 128)]).then_inc(weights_in, 16)
                        sp.dma_start(w_out_raw[0][:], g.w1_out[ds(col, 128), :]).then_inc(weights_in, 16)

                    pair(0, 0)
                    pair(0, 1)
                    with sp.Fori(1, PAIRS // 2) as it:
                        for n in range(2):
                            pair(it, n)

            @block.gpsimd
            def _(pool):
                if layer == 0:
                    zeroed = [q_stack[0][0], q_stack[1][0], k_stack[0], k_stack[1]]
                    for t in zeroed:
                        pool.memset(t[:], 0.0)
                    for t in w_out_raw:
                        pool.memset(t[:], 0.0)
                    for t in v:
                        last = pool.memset(t[:], 0.0)
                    last.then_inc(cleared, 1)
                    pool.wait_ge(cleared, 1)
                else:
                    pool.memset(causal_rows[:], 50.0).then_inc(cleared, 1)
                    pool.wait_ge(cleared, 1)
                    pool.affine_select(out=causal_rows[:], in_=causal_rows[:], compare_op=ALU.is_gt, fill=0.0,
                                       base=0, pattern=[[1, SEQ]], channel_multiplier=-1).then_inc(cleared, 1)

                def pair(it, n):
                    b = it // 4
                    if layer == 0:
                        head = (it % 4) * 4 + 2 * n
                        wait(pool, product_done, it, 2 * n, lambda J: plan.GROUPS * (J - 2))
                        pool.tensor_copy(v[n][:, :, :, 0:8], g.v_all[:, ds(b * TB, TB), ds(head * 8, 16)].rearrange(
                            "p t (h d) -> p t h d", h=2)).then_inc(v_done, 1)
                        wait(pool, min_done, it, 2 * n, lambda J: 8 * (J - 2))
                        pool.tensor_copy(toeplitz[n][:], g.toeplitz_all[:, ds(head, 2), :]).then_inc(table_done, 1)
                        pool.wait_ge(stack_in[n], it * LOADS + LOADS)
                        raw = w_out_raw[n]
                    else:
                        pool.wait_ge(weights_in, (it * 2 + n) * 80 + 80)
                        if not (isinstance(it, int) and 2 * it + n == 0):
                            wait(pool, item_done, it, 2 * n, lambda J: plan.index["prep", J // 2 - 1, 1] + 1)
                        settle(pool, held["pool"])
                        pool.tensor_scalar(w_q[:], w_qk[:, 0], -0.125, None, ALU.mult).then_inc(w_q_done, 1)
                        raw = w_out_raw[0]
                        for half in range(2):
                            wait(pool, lo_done, it, 2 * n, lambda J: 4 * (J // 2) + half + 1)
                            settle(pool, held["pool"])
                            cols = slice(half * BANK, (half + 1) * BANK)
                            for m, (dst, src) in enumerate(((slice(0, 64), slice(64, 128)), (slice(64, 128), slice(0, 64)))):
                                pool.tensor_copy(q_stack[n][1][dst, :, cols], q_stack[n][0][src, :, cols]).then_inc(turned_q, 1)
                                wait(pool, turned_q, it, 2 * n, lambda J: 4 * (J // 2) + 2 * half + m + 1)
                                settle(pool, held["pool"])
                    if not (isinstance(it, int) and it == 0):
                        wait(pool, item_done, it, 2 * n, lambda J: plan.index["y", J - 3, 0] + 1)
                    settle(pool, held["pool"])
                    pool.tensor_tensor(w_out[n][:], raw[:],
                                       g.gate_rows[:, layer, 0, ds(b, 1), :].rearrange("p a d -> p (a d)"),
                                       ALU.mult).then_inc(w_out_done, 1)

                for n in range(2):
                    pair(0, n)
                with pool.Fori(1, PAIRS // 2) as it:
                    for n in range(2):
                        pair(it, n)

            @block.tensor
            def _(pe):
                def prep(it, jj, J, key):
                    _, p, n = key
                    if n == 0:
                        wait(pe, weights_in, it, jj, lambda J: 80 * (J // 2 + 2)) if J is not None else pe.wait_ge(weights_in, 80)
                        wait(pe, w_q_done, it, jj, lambda J: J // 2 + 2) if J is not None else pe.wait_ge(w_q_done, 1)
                    if n < 4:
                        half = n % 2
                        return pe.matmul(shared, w_q[:] if n < 2 else w_qk[:, 1, :], h_pair[:, half * BANK:(half + 1) * BANK],
                                         start=True, stop=True)
                    for t in range(4):
                        tok = (4 * (n - 4) + t) * P
                        mm = pe.matmul(shared[:, t * P:(t + 1) * P], h_pair[:, tok:tok + P], w_v[:], start=True, stop=True)
                    return mm

                def item(it, jj, J, key):
                    index = lambda J2: plan.index[key[0], J2 + key[1] - J, key[2]]
                    if key[0] == "prep":
                        index = lambda J2: plan.index["prep", J2 // 2 + 1, key[2]]
                    wait(pe, item_out, it, jj, index)
                    if key[0] == "prep":
                        mm = prep(it, jj, J, key)
                    elif key[0] == "r":
                        wait(pe, wide_done, it, jj, lambda J2: J2)
                        for i in range(4):
                            mm = pe.transpose(shared[:, i * P:(i + 1) * P], inv_wide[:, i].rearrange("p h r -> p (h r)"),
                                              g.ident[:])
                    else:
                        lag = J - key[1]
                        wait(pe, out_done, it, jj, lambda J2: J2 - lag + 1)
                        wait(pe, w_out_done, it, jj, lambda J2: (J2 - lag) // 2 + 1)
                        for i in range(4):
                            mm = pe.matmul(shared[:, i * P:(i + 1) * P], out_T[key[1] % 2][:, i * P:(i + 1) * P],
                                           w_out[key[1] // 2 % 2][:], start=True, stop=True)
                    mm.then_inc(item_done, 1)

                def turn(it, jj, J):
                    n = J // 2 % 2
                    for s in range(8):
                        i, h = unit(s)
                        if J < JOBS:
                            if s == 0 and layer == 0:
                                pe.wait_ge(stack_in[n], it * LOADS + LOADS)
                            if s == 0 and layer == 1:
                                wait(pe, lo_done, it, jj, lambda J2: 4 * (J2 // 2 + 1))
                                wait(pe, turned_q, it, jj, lambda J2: 4 * (J2 // 2 + 1))
                            wait(pe, probs_done, it, jj, lambda J2: 8 * J2 + s - 1)
                            q0 = plan.TILES_OF[J % 2][i] * P
                            width = plan.width(J, i)
                            for k0 in range(0, width, BANK):
                                k1 = min(width, k0 + BANK)
                                for m, q in enumerate(q_stack[n]):
                                    mm = pe.matmul(scores_bank(s)[:, k0:k1], q[:, h, q0:q0 + P], k_stack[n][:, h, k0:k1],
                                                   start=(m == 0), stop=(m == len(q_stack[n]) - 1))
                            mm.then_inc(scores_done, 1)
                        if 0 <= J - 1 < JOBS and s < plan.steps(J - 1):
                            if s == 0:
                                wait(pe, probs_done, it, jj, lambda J2: 8 * J2)
                            for h in range(2):
                                wait(pe, turned_out[h], it, jj, lambda J2: plan.step(J2 - 1) + s)
                                for i in range(plan.first(J - 1, s) // P, 4):
                                    mm = pe.transpose(turn_bank[h][:, i * P:(i + 1) * P],
                                                      probs[(J - 1) % 2][:, h, i, s * P:(s + 1) * P], g.ident[:])
                                mm.then_inc(turn_done[h], 1)
                        job, m = plan.product(J, s)
                        if job is not None and 0 <= job < JOBS:
                            lag = J - job
                            kts = plan.kts(job, m)
                            if m == 0:
                                wait(pe, out_done, it, jj, lambda J2: J2 - lag)
                                wait(pe, v_done, it, jj, lambda J2: ((J2 - lag) // 2 + 1) * (1 if layer == 0 else 2))
                            for h in range(2):
                                wait(pe, turned_out[h], it, jj, lambda J2: plan.step(J2 - lag) + kts[-1] + 1)
                            for kt in kts:
                                off = plan.first(job, kt)
                                for h in range(2):
                                    row = rows * (kt % plan.group * 2 + h)
                                    mm = pe.matmul(out_bank[row:row + rows, off:], v[job // 2 % 2][:, kt, h, :],
                                                   turned[h][kt % BUFFERS][:, off:], start=(kt < plan.group),
                                                   stop=(kt + plan.group >= plan.steps(job)), tile_position=(0, row))
                            mm.then_inc(product_done, 1)
                        for key in plan.items(J, s):
                            item(it, jj, J, key)

                for n in range(plan.prep):
                    if n:
                        pe.wait_ge(item_out, n)
                    prep(0, 0, None, ("prep", 0, n)).then_inc(item_done, 1)
                turns(pe, plan, turn)

            @block.vector
            def _(dve):
                def split(it, jj, J, key):
                    _, p, n = key
                    cols = slice((n % 2) * BANK, (n % 2 + 1) * BANK)
                    stack = q_stack[p % 2][0] if n < 2 else k_stack[p % 2]
                    if J is None:
                        dve.wait_ge(hi_done, n + 1)
                    else:
                        wait(dve, hi_done, it, jj, lambda J2: 4 * (J2 // 2 + 1) + n + 1)
                    for h, (own, other) in enumerate(((slice(0, 64), slice(64, 128)), (slice(64, 128), slice(0, 64)))):
                        done = dve.tensor_tensor(stack[other, h, cols], shared[own], stack[own, h, cols].bitcast(F32),
                                                 ALU.subtract)
                    done.then_inc(lo_done, 1)
                    if J is None:
                        dve.wait_ge(lo_done, n + 1)
                    else:
                        wait(dve, lo_done, it, jj, lambda J2: 4 * (J2 // 2 + 1) + n + 1)
                    dve.sem_inc(item_out, 1)

                def turn(it, jj, J):
                    for s in range(8):
                        i, h = unit(s)
                        if J < JOBS:
                            n = J // 2 % 2
                            wait(dve, scores_done, it, jj, lambda J2: 8 * J2 + s + 1)
                            width, plain = plan.width(J, i), plan.plain(J, i)
                            sc = scores_bank(s)
                            slot = 8 * (J % 2) + s
                            floor = 3e38
                            if plain:
                                dve.tensor_reduce(plain_min[:, slot:slot + 1], sc[:, 0:plain], AX, ALU.min)\
                                   .then_inc(plain_done, 1)
                                wait(dve, plain_done, it, jj, lambda J2: plan.plains(J2, s + 1))
                                floor = plain_min[:, slot:slot + 1]
                            rest = width - plain
                            if layer == 0:
                                if s == 0:
                                    wait(dve, table_done, it, jj, lambda J2: J2 // 2 + 1)
                                add = toeplitz[n][:, h, 2 * P - rest:]
                            else:
                                if s == 0 and J == 0:
                                    dve.wait_ge(cleared, 2)
                                add = causal_rows[:, 0:rest]
                            settle(dve, held["dve"])
                            dve.tensor_tensor_reduce(out=sc[:, plain:width], in0=sc[:, plain:width], in1=add, scale=1.0,
                                                     scalar=floor, op0=ALU.add, op1=ALU.min,
                                                     accum_out=row_min[:, slot:slot + 1]).then_inc(min_done, 1)
                        if 0 <= J - 1 < JOBS and s < plan.steps(J - 1):
                            wait(dve, turn_done[0], it, jj, lambda J2: plan.step(J2 - 1) + s + 1)
                            wait(dve, product_done, it, jj, lambda J2: plan.GROUPS * (J2 - 1) + s // plan.group - 1)
                            off = plan.first(J - 1, s)
                            dve.tensor_copy(turned[0][s % BUFFERS][:, off:], turn_bank[0][:, off:]).then_inc(turned_out[0], 1)
                        if s == 1 and 0 <= J - 1 < JOBS:
                            wait(dve, probs_done, it, jj, lambda J2: 8 * J2)
                            dve.reciprocal(inv_sum[:], row_sum[:, (J - 1) % 2]).then_inc(inv_done, 1)
                            wait(dve, inv_done, it, jj, lambda J2: J2)
                            if not (isinstance(it, int) and J - 2 < 0):
                                wait(dve, item_done, it, jj, lambda J2: plan.index["r", J2 - 2, 0] + 1)
                            wide = inv_wide[:].rearrange("p i h r -> p i (h r)")
                            for n in range(plan.group):
                                done = dve.tensor_copy(wide[:, :, 2 * rows * n:2 * rows * (n + 1)].rearrange(
                                    "p i (h r) -> p i h r", h=2),
                                    inv_sum[:].rearrange("p (i h) -> p i h", h=2).unsqueeze(3).to_broadcast([P, 4, 2, rows]))
                            done.then_inc(wide_done, 1)
                        for key in plan.items(J, s - 1) if s else plan.items(J - 1, 7):
                            if key[0] == "prep" and key[2] < 4:
                                split(it, jj, J, key)
                        for key in plan.items(J, s):
                            if key[0] == "y":
                                lag = J - key[1]
                                wait(dve, item_done, it, jj, lambda J2: plan.index["y", J2 - lag, 0] + 1)
                                row = (it * 4 + (jj - lag)) // 16
                                fours = g.x[:, ds(row * TB, TB), :].rearrange("p (a t) d -> p a t d", a=2)
                                mine = fours[:, :, 0:4:3, :] if key[1] % 2 == 0 else fours[:, :, 1:3, :]
                                dve.tensor_tensor(mine, mine, shared.rearrange("p (a t d) -> p a t d", a=2, t=2), ALU.add)\
                                   .then_inc(item_out, 1)
                        job, m = plan.product(J, s)
                        if job is not None and 0 <= job < JOBS and m == plan.groups(job) - 1:
                            lag = J - job
                            wait(dve, product_done, it, jj, lambda J2: plan.GROUPS * (J2 - lag + 1))
                            wait(dve, item_out, it, jj, lambda J2: plan.index["r", J2 - lag, 0] + 1)
                            if job > 0:
                                wait(dve, item_done, it, jj, lambda J2: plan.index["y", J2 - lag - 1, 0] + 1)
                            off = plan.first(job, plan.group - 1)
                            if off:
                                dve.tensor_tensor(out_T[job % 2][0:2 * rows, 0:off], out_bank[0:2 * rows, 0:off],
                                                  inv_rows[0:2 * rows, 0:off], ALU.mult)
                            dve.tensor_tensor(out_T[job % 2][:, off:], out_bank[:, off:], inv_rows[:, off:],
                                              ALU.mult).then_inc(out_done, 1)

                if layer == 0:
                    dve.memset(out_T[0][:], 0.0)
                for n in range(min(4, plan.prep)):
                    split(0, 0, None, ("prep", 0, n))
                turns(dve, plan, turn)

            @block.scalar
            def _(act):
                def round_up(key):
                    _, p, n = key
                    cols = slice((n % 2) * BANK, (n % 2 + 1) * BANK)
                    stack = q_stack[p % 2][0] if n < 2 else k_stack[p % 2]
                    for h, own in enumerate((slice(0, 64), slice(64, 128))):
                        done = act.activation(stack[own, h, cols], shared[own], ACT.Copy)
                    done.then_inc(hi_done, 1)

                def copy_v(it, jj, J, key):
                    _, p, n = key
                    t0 = 4 * (n - 4)
                    act.activation(v[p % 2][:, t0:t0 + 4].rearrange("p t h d -> p t (h d)"),
                                   shared.rearrange("p (t c) -> p t c", t=4), ACT.Copy).then_inc(v_done, 1)
                    if J is None:
                        act.wait_ge(v_done, n - 3)
                    else:
                        wait(act, v_done, it, jj, lambda J2: 2 * (J2 // 2 + 1) + n - 3)
                    act.sem_inc(item_out, 1)

                def turn(it, jj, J):
                    for s in range(8):
                        i, h = unit(s)
                        if 0 <= J - 1 < JOBS and s < plan.steps(J - 1):
                            wait(act, turn_done[1], it, jj, lambda J2: plan.step(J2 - 1) + s + 1)
                            wait(act, product_done, it, jj, lambda J2: plan.GROUPS * (J2 - 1) + s // plan.group - 1)
                            off = plan.first(J - 1, s)
                            act.activation(turned[1][s % BUFFERS][:, off:], turn_bank[1][:, off:], ACT.Copy)\
                               .then_inc(turned_out[1], 1)
                        if J < JOBS:
                            wait(act, min_done, it, jj, lambda J2: 8 * J2 + s + 1)
                            if s == 0:
                                wait(act, turn_done[1], it, jj, lambda J2: plan.step(J2 - 1))
                                wait(act, inv_done, it, jj, lambda J2: J2 - 1)
                            slot = 8 * (J % 2) + s
                            width = plan.width(J, i)
                            act.activation(probs[J % 2][:, h, i, 0:width], scores_bank(s)[:, 0:width], ACT.Exp,
                                           bias=row_min[:, slot:slot + 1], scale=-1.0,
                                           accum_out=row_sum[:, J % 2, 2 * i + h:2 * i + h + 1]).then_inc(probs_done, 1)
                        for key in plan.items(J, s):
                            if key[0] == "prep":
                                wait(act, item_done, it, jj, lambda J2: plan.index["prep", J2 // 2 + 1, key[2]] + 1)
                                if key[2] < 4:
                                    round_up(key)
                                else:
                                    copy_v(it, jj, J, key)
                            if key[0] == "r":
                                wait(act, item_done, it, jj, lambda J2: plan.index["r", J2 - 1, 0] + 1)
                                wait(act, out_done, it, jj, lambda J2: J2 - 1)
                                act.activation(inv_rows[:], shared, ACT.Copy).then_inc(item_out, 1)

                for n in range(plan.prep):
                    act.wait_ge(item_done, n + 1)
                    if n < 4:
                        round_up(("prep", 0, n))
                    else:
                        copy_v(0, 0, None, ("prep", 0, n))
                turns(act, plan, turn)


def experts(nc, g):
    EM = EXPERTS * 2
    CHUNKS = TOKENS // BANK
    stage_sems = []
    with ExitStack() as ctx:
        ctx.callback(give_back, nc, stage_sems)

        def sb(name, shape, dt=F32):
            return ctx.enter_context(nc.sbuf_tensor("e_" + name, shape, dt))

        def sem(name):
            return kept(nc, stage_sems, "e_" + name)

        w1 = sb("w1", [P, EXPERTS, HIDDEN])
        w3 = sb("w3", [P, EXPERTS, HIDDEN])
        w2 = sb("w2", [P, EXPERTS, 2, DIM])
        b13 = sb("b13", [P, 2, EXPERTS, 2])
        b2 = sb("b2", [EXPERTS, DIM])
        w_gate = sb("w_gate", [P, EXPERTS])
        iota = sb("iota", [P, EXPERTS])
        logits = sb("logits", [P, TILES, EXPERTS])
        best = sb("best", [P, TILES, 8])
        best_at = sb("best_at", [P, TILES, 8], U32)
        index = sb("index", [P, TILES, 2])
        weight = sb("weight", [P, TILES, 2])
        gap = sb("gap", [P, TILES])
        total = sb("total", [P, TILES])
        second = sb("second", [P, TILES, EXPERTS])
        gates = sb("gates", [P, TILES, EXPERTS])
        gates_T = sb("gates_T", [EXPERTS, TOKENS])
        gates_chunk = sb("gates_chunk", [EXPERTS, BANK])
        h_parts = [sb(f"h_part{n}", [P, TOKENS], F32R) for n in range(2)]
        w_parts = [[sb(f"w{a}_part{n}", [P, EXPERTS, HIDDEN], F32R) for n in range(2)] for a in (1, 3)]
        early = ExitStack()

        def sb_early(name, shape):
            return early.enter_context(nc.sbuf_tensor("e_" + name, shape, F32))

        logits_T = sb_early("logits_T", [EXPERTS, TOKENS])
        lora_a = sb_early("lora_a", [RANK, 2, EXPERTS, DIM])
        lora_b = sb_early("lora_b", [RANK, 2, EXPERTS, HIDDEN])
        lora_a2 = sb_early("lora_a2", [RANK, EXPERTS, HIDDEN])
        lora_b2 = sb_early("lora_b2", [RANK, EXPERTS, DIM])
        loaded, low_done, merged = sem("loaded"), sem("low_done"), sem("merged")
        h_hi_done, w_hi_done, w_lo_done = sem("h_hi_done"), sem("w_hi_done"), sem("w_lo_done")
        logit_mm, logit_out, turn_done, route, exp_done, gate_turned, gate_out = map(sem, (
            "logit_mm", "logit_out", "turn_done", "route", "exp_done", "gate_turned", "gate_out"))
        merges = [("13", a, e) for a in range(2) for e in range(0, EXPERTS, 2)] + [("2", 0, e) for e in range(0, EXPERTS, 2)]
        with nc.Block() as block:
            @block.sync
            def _(sp):
                loads = ((lora_a, g.lora_a), (lora_b, g.lora_b), (w1, g.w1), (w3, g.w3), (lora_a2, g.lora_a2),
                         (lora_b2, g.lora_b2), (w2, g.w2), (w_gate, g.w_gate), (iota, g.iota), (b13, g.b13), (b2, g.b2))
                for dst, src in loads:
                    sp.dma_start(dst[:], src).then_inc(loaded, 16)

            @block.tensor
            def _(pe):
                pe.wait_ge(loaded, 176)
                for c in range(CHUNKS):
                    if c >= 2:
                        pe.wait_ge(logit_out, c - 1)
                    pe.matmul(g.ps[0:EXPERTS, 6 + c % 2, :], w_gate[:], g.hT[:, c * BANK:(c + 1) * BANK], start=True,
                              stop=True).then_inc(logit_mm, 1)
                pe.wait_ge(logit_out, CHUNKS)
                for t in range(TILES):
                    mm = pe.transpose(g.ps[:, 6, t * EXPERTS:(t + 1) * EXPERTS], logits_T[:, t * P:(t + 1) * P],
                                      g.ident[0:EXPERTS, 0:EXPERTS])
                mm.then_inc(turn_done, 1)
                for n, (kind, a, e) in enumerate(merges):
                    if n >= 4:
                        pe.wait_ge(merged, n - 3)
                    for j in range(2):
                        if kind == "13":
                            mm = pe.matmul(g.ps[:, n % 4, j * HIDDEN:(j + 1) * HIDDEN], lora_a[:, a, e + j],
                                           lora_b[:, a, e + j], start=True, stop=True)
                        else:
                            for m in range(2):
                                col = (2 * j + m) * DIM
                                mm = pe.matmul(g.ps[:, n % 4, col:col + DIM], lora_a2[:, e + j, m * P:(m + 1) * P],
                                               lora_b2[:, e + j], start=True, stop=True)
                    mm.then_inc(low_done, 1)
                pe.wait_ge(route, 7)
                for c in range(CHUNKS):
                    if c >= 2:
                        pe.wait_ge(gate_out, c - 1)
                    for t in range(4):
                        mm = pe.transpose(g.ps[0:EXPERTS, 4 + c % 2, t * P:(t + 1) * P], gates[:, 4 * c + t, :], g.ident[:])
                    mm.then_inc(gate_turned, 1)

            def pair_of(part, e):
                return part[:, e:e + 2].rearrange("p e n -> p (e n)")

            @block.gpsimd
            def _(pool):
                for n, (kind, a, e) in enumerate(merges[:EXPERTS]):
                    pool.wait_ge(w_hi_done, n + 1)
                    pool.tensor_tensor(pair_of(w_parts[a][1], e), pair_of((w1, w3)[a], e),
                                       pair_of(w_parts[a][0], e).bitcast(F32), ALU.subtract).then_inc(w_lo_done, 1)

            @block.scalar
            def _(act):
                for c in range(CHUNKS):
                    cols = slice(c * BANK, (c + 1) * BANK)
                    act.activation(h_parts[0][:, cols], g.hT[:, cols], ACT.Copy).then_inc(h_hi_done, 1)
                for c in range(CHUNKS):
                    act.wait_ge(logit_mm, c + 1)
                    act.activation(logits_T[:, c * BANK:(c + 1) * BANK], g.ps[0:EXPERTS, 6 + c % 2, :], ACT.Copy)\
                       .then_inc(logit_out, 1)
                act.wait_ge(route, 3)
                act.activation(weight[:, :, 1], gap[:], ACT.Exp).then_inc(exp_done, 1)
                for n, (kind, a, e) in enumerate(merges[:EXPERTS]):
                    act.wait_ge(merged, n + 1)
                    act.activation(pair_of(w_parts[a][0], e), pair_of((w1, w3)[a], e), ACT.Copy).then_inc(w_hi_done, 1)
                for c in range(CHUNKS):
                    act.wait_ge(gate_turned, c + 1)
                    act.activation(gates_T[:, c * BANK:(c + 1) * BANK], g.ps[0:EXPERTS, 4 + c % 2, :], ACT.Copy)\
                       .then_inc(gate_out, 1)

            @block.vector
            def _(dve):
                for c in range(CHUNKS):
                    cols = slice(c * BANK, (c + 1) * BANK)
                    dve.wait_ge(h_hi_done, c + 1)
                    dve.tensor_tensor(h_parts[1][:, cols], g.hT[:, cols], h_parts[0][:, cols].bitcast(F32), ALU.subtract)
                dve.wait_ge(turn_done, 1)
                dve.tensor_copy(logits[:].rearrange("p t e -> p (t e)"), g.ps[:, 6, 0:TILES * EXPERTS]).then_inc(route, 1)
                dve.wait_ge(route, 1)
                for t in range(TILES):
                    last = dve.max(best[:, t, :], logits[:, t, :])
                last.then_inc(route, 1)
                dve.wait_ge(route, 2)
                dve.tensor_tensor(gap[:], best[:, :, 1], best[:, :, 0], ALU.subtract).then_inc(route, 1)
                for t in range(TILES):
                    last = dve.max_index(best_at[:, t, :], best[:, t, :], logits[:, t, :])
                last.then_inc(route, 1)
                dve.wait_ge(exp_done, 1)
                dve.tensor_scalar(total[:], weight[:, :, 1], 1.0, None, ALU.add).then_inc(route, 1)
                dve.wait_ge(route, 5)
                dve.reciprocal(weight[:, :, 0], total[:])
                dve.tensor_copy(index[:], best_at[:, :, 0:2]).then_inc(route, 1)
                dve.wait_ge(route, 6)
                dve.tensor_tensor(weight[:, :, 1], weight[:, :, 1], weight[:, :, 0], ALU.mult)
                wide = [P, TILES, EXPERTS]
                for n, dst in ((0, gates), (1, second)):
                    last = dve.tensor_tensor(dst[:], iota[:].unsqueeze(1).to_broadcast(wide),
                                             index[:, :, n:n + 1].to_broadcast(wide), ALU.is_equal)
                last.then_inc(exp_done, 1)
                dve.wait_ge(exp_done, 2)
                for n, dst in ((0, gates), (1, second)):
                    last = dve.tensor_tensor(dst[:], dst[:], weight[:, :, n:n + 1].to_broadcast(wide), ALU.mult)
                last.then_inc(exp_done, 1)
                dve.wait_ge(exp_done, 3)
                dve.tensor_tensor(gates[:], gates[:], second[:], ALU.add).then_inc(route, 1)
                for n, (kind, a, e) in enumerate(merges):
                    dve.wait_ge(low_done, n + 1)
                    w = (w1, w3)[a][:, e:e + 2].rearrange("p e n -> p (e n)") if kind == "13" else \
                        w2[:, e:e + 2].rearrange("p e m d -> p (e m d)")
                    dve.tensor_tensor(w, w, g.ps[:, n % 4, :], ALU.add).then_inc(merged, 1)

        early.close()
        silu = [sb(f"silu{n}", [P, BANK]) for n in range(2)]
        hidden = [[sb(f"hidden{n}{m}", [P, BANK]) for m in range(2)] for n in range(2)]
        acc = sb("acc", [P, 4, DIM])
        gated = sb("gated", [P, 4, DIM])
        up_done, silu_done, hidden_done, down_done, acc_done, bias_in, bias_mm, bias_out, gated_done, x_done = map(sem, (
            "up_done", "silu_done", "hidden_done", "down_done", "acc_done", "bias_in", "bias_mm", "bias_out",
            "gated_done", "x_done"))
        with nc.Block() as block:
            @block.gpsimd
            def _(pool):
                with pool.Fori(0, CHUNKS) as c:
                    pool.wait_ge(bias_mm, c + 1)
                    pool.tensor_copy(gates_chunk[:], gates_T[:, ds(c * BANK, BANK)]).then_inc(bias_in, 1)

            @block.tensor
            def _(pe):
                pe.sem_inc(bias_mm, 1)
                pe.sem_inc(down_done, 2)

                def down(c, e):
                    pe.wait_ge(hidden_done, c * EM + 2 * e + 4)
                    pe.wait_ge(acc_done, c * EXPERTS + e + 1)
                    for t in range(4):
                        for m in range(2):
                            mm = pe.matmul(g.ps[:, 4 + e % 2, t * DIM:(t + 1) * DIM], hidden[e % 2][m][:, t * P:(t + 1) * P],
                                           w2[:, e, m, :], start=(m == 0), stop=(m == 1))
                    mm.then_inc(down_done, 1)

                with pe.Fori(0, CHUNKS) as c:
                    for e in range(EXPERTS):
                        for m in range(2):
                            i = 2 * e + m
                            pe.wait_ge(hidden_done, c * EM + i + 1)
                            for n in range(2):
                                for k, (of_w, of_h) in enumerate(((0, 0), (0, 1), (1, 0))):
                                    mm = pe.matmul(g.ps[:, 2 * n + i % 2, :], w_parts[n][of_w][:, e, m * P:(m + 1) * P],
                                                   h_parts[of_h][:, ds(c * BANK, BANK)], start=(k == 0), stop=(k == 2))
                            mm.then_inc(up_done, 1)
                        if e == 0:
                            pe.wait_ge(bias_in, c + 1)
                            pe.wait_ge(bias_out, c + 1)
                            for t in range(4):
                                mm = pe.matmul(g.ps[:, 6, t * DIM:(t + 1) * DIM], gates_chunk[:, t * P:(t + 1) * P], b2[:],
                                               start=True, stop=True)
                            mm.then_inc(bias_mm, 1)
                        else:
                            down(c, e - 1)
                    down(c, EXPERTS - 1)

            @block.scalar
            def _(act):
                act.sem_inc(bias_out, 1)
                with act.Fori(0, CHUNKS) as c:
                    for i in range(EM):
                        act.wait_ge(up_done, c * EM + i + 1)
                        act.activation(silu[i % 2][:], g.ps[:, i % 2, :], ACT.Silu, bias=b13[:, 0, i // 2, i % 2:i % 2 + 1])\
                           .then_inc(silu_done, 1)
                        if i == 1:
                            act.wait_ge(bias_mm, c + 2)
                            act.wait_ge(gated_done, c + 1)
                            act.activation(acc[:].rearrange("p t d -> p (t d)"), g.ps[:, 6, :], ACT.Copy).then_inc(bias_out, 1)

            @block.vector
            def _(dve):
                dve.sem_inc(hidden_done, 2)
                dve.sem_inc(acc_done, 2)
                dve.sem_inc(gated_done, 1)

                def accumulate(c, e):
                    dve.wait_ge(down_done, c * EXPERTS + e + 3)
                    if e == 0:
                        dve.wait_ge(bias_out, c + 2)
                    else:
                        dve.wait_ge(acc_done, c * EXPERTS + e + 2)
                    for t in range(4):
                        last = dve.scalar_tensor_tensor(
                            acc[:, t, :], g.ps[:, 4 + e % 2, t * DIM:(t + 1) * DIM],
                            gates[:, ds(c * 4 + t, 1), e:e + 1].rearrange("p a e -> p (a e)"), acc[:, t, :], ALU.mult, ALU.add)
                    last.then_inc(acc_done, 1)

                with dve.Fori(0, CHUNKS) as c:
                    for e in range(EXPERTS):
                        for m in range(2):
                            i = 2 * e + m
                            dve.wait_ge(silu_done, c * EM + i + 1)
                            dve.wait_ge(down_done, c * EXPERTS + e + 1)
                            dve.scalar_tensor_tensor(hidden[e % 2][m][:], g.ps[:, 2 + i % 2, :], b13[:, 1, e, m:m + 1],
                                                     silu[i % 2][:], ALU.add, ALU.mult).then_inc(hidden_done, 1)
                        if e:
                            accumulate(c, e - 1)
                    accumulate(c, EXPERTS - 1)
                    dve.wait_ge(acc_done, c * EXPERTS + EXPERTS + 2)
                    dve.tensor_tensor(gated[:], acc[:], g.gate_rows[:, 0, 1, ds(c // 2, 1), :].to_broadcast([P, 4, DIM]),
                                      ALU.mult).then_inc(gated_done, 1)
                    dve.wait_ge(gated_done, c + 2)
                    rowsx = g.x[:, ds(c * 4, 4), :]
                    dve.tensor_tensor(rowsx, rowsx, gated[:], ALU.add).then_inc(x_done, 1)


def shifted(z, rows, b, t0, n):
    lo = t0 + (1 if rows.start else 0)
    return z[rows, ds(b, 1), ds(lo, n)].rearrange("p a t -> p (a t)")


TOP, LOW = slice(0, 64), slice(64, 128)


def local_attention(nc, g, layer):
    stage_sems = []
    with ExitStack() as ctx:
        ctx.callback(give_back, nc, stage_sems)

        def sb(name, shape, dt=F32):
            return ctx.enter_context(nc.sbuf_tensor(f"t{layer}_{name}", shape, dt))

        def sem(name):
            return kept(nc, stage_sems, f"t{layer}_{name}")

        G = 4
        KEYS = P + LWIN
        w = sb("w", [P, 3 * INNER])
        wo = sb("wo", [P, 4, DIM])
        scale_rows = sb("scale_rows", [P, 2, LDH])
        rot = sb("rot", [P, TB, 2, 2, LDH])
        mask = sb("mask", [P, 2, KEYS])
        minus_half = sb("minus_half", [P, 16])
        h_tile = [sb(f"h_tile{n}", [P, P]) for n in range(2)]
        h_parts = [[sb(f"h_part{n}{k}", [P, P], F32R) for k in range(2)] for n in range(2)]
        w_parts = [sb(f"w_part{k}", [P, 3 * INNER], F32R) for k in range(2)]
        squares = sb("squares", [P, 2 * INNER])
        squared_norm = sb("squared_norm", [P, 16])
        inv_norm = sb("inv_norm", [P, 16])
        by_cos = sb("by_cos", [P, 16, LDH])
        by_sin = sb("by_sin", [P, 16, LDH])
        rotated = sb("rotated", [P, 16, LDH])
        q_T = [[sb(f"q_T{n}{odd}", [P, 4, P]) for odd in range(2)] for n in range(2)]
        k_ring = sb("k_ring", [P, 4, (TB + 1) * P])
        v_ring = sb("v_ring", [P, TB + 1, INNER])
        row_min = sb("row_min", [P, 2, G])
        row_sum = sb("row_sum", [P, 2, G])
        inv_sum = sb("inv_sum", [P, 2, G])
        probs = [sb(f"probs{n}", [P, G, 2 * P]) for n in range(2)]
        probs_T = [sb(f"probs_T{n}", [P, 2, BANK]) for n in range(2)]
        out_T = sb("out_T", [P, 4, P])

        h_done = sem("h_done")
        h_hi_done = sem("h_hi_done")
        h_lo_done = sem("h_lo_done")
        qkv_done = sem("qkv_done")
        square_done, v_done = sem("square_done"), sem("v_done")
        sum_done = sem("sum_done")
        floor_done = sem("floor_done")
        inv_done = sem("inv_done")
        rotate_done = sem("rotate_done")
        pool_step = sem("pool_step")
        rotated_done = sem("rotated_done")
        front_done = sem("front_done")
        q_out, k_out = sem("q_out"), sem("k_out")
        proj_done = sem("proj_done")
        z_done = sem("z_done")
        scores_done = sem("scores_done")
        min_done = sem("min_done")
        probs_done = sem("probs_done")
        inv_sum_done = sem("inv_sum_done")
        scaled_done = sem("scaled_done")
        turn_done = sem("turn_done")
        turned5, turned6 = sem("turned5"), sem("turned6")
        product_done = sem("product_done")
        out_done = sem("out_done")
        w_hi_done, w_lo_done = sem("w_hi_done"), sem("w_lo_done")
        loaded, ready, tables, held = sem("loaded"), sem("ready"), sem("tables"), sem("held")
        held_dve = sem("held_dve")
        heads_of = lambda ap: ap.rearrange("p (h d) -> p h d", d=LDH)
        flat = lambda ap: ap.rearrange("p j t -> p (j t)")

        def reach(eng, sem, count):
            if not isinstance(count, int) or count > 0:
                eng.wait_ge(sem, count)

        def batches(eng, turn):
            for t in range(TB):
                turn(0, t)
            with eng.Fori(1, BATCH) as b:
                for t in range(TB):
                    turn(b, t)

        def exists(b, t, n):
            return not isinstance(b, int) or t - n >= 0

        with nc.Block() as block:
            @block.sync
            def _(sp):
                for dst, src in ((w[:], g.wqkv[layer]), (wo[:], g.wo[layer]), (rot[:], g.rotary), (mask[:], g.band)):
                    sp.dma_start(dst, src).then_inc(loaded, 16)
                for n, src in enumerate((g.q_scale, g.k_scale)):
                    sp.dma_start(scale_rows[:, n, :], src[layer].partition_broadcast(P)).then_inc(loaded, 16)

            @block.gpsimd
            def _(pool):
                def take(b, t):
                    pool.tensor_copy(h_tile[t % 2][:], g.zA[:, ds(b, 1), ds(t * P, P)].rearrange("p a t -> p (a t)"))\
                        .then_inc(h_done, 1)

                def add_products(n):
                    reach(pool, rotate_done, n + 1)
                    settle(pool, held)
                    reach(pool, front_done, n)
                    settle(pool, held)
                    pool.tensor_tensor(rotated[:], by_cos[:], by_sin[:], ALU.add).then_inc(pool_step, 1)

                def over_norm(n):
                    reach(pool, floor_done, n + 1)
                    settle(pool, held)
                    reach(pool, rotated_done, n)
                    settle(pool, held)
                    pool.tensor_tensor(inv_norm[:], squared_norm[:], minus_half[:], ALU.pow).then_inc(inv_done, 1)
                    reach(pool, pool_step, n + 1)
                    settle(pool, held)
                    reach(pool, inv_done, n + 1)
                    settle(pool, held)
                    pool.tensor_tensor(rotated[:], rotated[:], inv_norm[:].unsqueeze(2).to_broadcast([P, 16, LDH]),
                                       ALU.mult).then_inc(rotated_done, 1)

                def scale(k, s):
                    reach(pool, inv_sum_done, k + 1)
                    settle(pool, held)
                    pool.tensor_tensor(probs[s][:, :, P - LWIN:], probs[s][:, :, P - LWIN:],
                                       inv_sum[:, s, :].unsqueeze(2).to_broadcast([P, G, KEYS]), ALU.mult)\
                        .then_inc(scaled_done, 1)

                take(0, 0)
                take(0, 1)
                pool.memset(minus_half[:], -0.5)
                for t in probs + [k_ring] + q_T[0] + q_T[1]:
                    pool.memset(t[:], 0.0)
                pool.memset(v_ring[:, 0, :], 0.0).then_inc(ready, 1)
                pool.wait_ge(ready, 1)
                add_products(0)
                over_norm(0)
                pool.wait_ge(h_lo_done, 1)
                take(0, 2)
                add_products(1)
                over_norm(1)

                def turn(b, t):
                    T = b * TB + t
                    reach(pool, h_lo_done, T + 2)
                    ahead = t + 3
                    take(b if ahead < TB else (b + 1) % BATCH, ahead % TB)
                    scale(2 * T, 0)
                    add_products(T + 2)
                    scale(2 * T + 1, 1)
                    over_norm(T + 2)

                batches(pool, turn)

            @block.tensor
            def _(pe):
                def qkv(n, t):
                    reach(pe, h_lo_done, n + 1)
                    reach(pe, rotate_done, n)
                    reach(pe, square_done, 2 * n)
                    for a in range(3):
                        if a == 2:
                            reach(pe, v_done, n)
                            reach(pe, z_done, n - 4)
                        for k, (of_h, of_w) in enumerate(((0, 0), (0, 1), (1, 0))):
                            mm = pe.matmul(g.ps[:, a, :], h_parts[t % 2][of_h][:], w_parts[of_w][:, a * INNER:(a + 1) * INNER],
                                           start=(k == 0), stop=(k == 2))
                    mm.then_inc(qkv_done, 1)

                def scores(b, t, s):
                    k = 2 * (b * TB + t) + s
                    if s == 0:
                        reach(pe, q_out, b * TB + t + 1)
                        reach(pe, k_out, b * TB + t + 1)
                    reach(pe, probs_done, k)
                    for j in range(G):
                        h = s * G + j
                        mm = pe.matmul(g.ps[:, 3 + j // 2, j % 2 * KEYS:(j % 2 + 1) * KEYS], q_T[t % 2][h % 2][:, h // 2, :],
                                       k_ring[:, h // 2, t * P + P - LWIN:(t + 2) * P], start=True, stop=True)
                    mm.then_inc(scores_done, 1)

                def turn_probs(k, s, fronts=None):
                    reach(pe, scaled_done, k + 1)
                    if s == 0:
                        reach(pe, q_out, fronts)
                        reach(pe, k_out, fronts)
                    else:
                        reach(pe, turned5, k)
                        reach(pe, turned6, k)
                    for j in range(G):
                        for own in range(2):
                            col = j % 2 * 2 * P + own * P
                            mm = pe.transpose(g.ps[:, 5 + j // 2, col:col + P], probs[s][:, j, own * P:(own + 1) * P], g.ident[:])
                    mm.then_inc(turn_done, 1)

                def product(k, t, s):
                    reach(pe, turned5, k + 1)
                    reach(pe, turned6, k + 1)
                    reach(pe, out_done, k)
                    for pair in range(2):
                        for own in range(2):
                            for odd in range(2):
                                h = s * G + 2 * pair + odd
                                col = odd * 2 * P + own * P
                                mm = pe.matmul(g.ps[64 * odd:64 * odd + 64, 7, h // 2 * P:(h // 2 + 1) * P],
                                               v_ring[:, t + own, h * LDH:(h + 1) * LDH], probs_T[s][:, pair, col:col + P],
                                               start=(own == 0), stop=(own == 1), tile_position=(0, 64 * odd))
                    mm.then_inc(product_done, 1)

                def project(n):
                    reach(pe, out_done, 2 * n + 2)
                    reach(pe, v_done, n + 5 if not isinstance(n, int) else min(n + 5, BATCH * TB + 2))
                    for j in range(4):
                        mm = pe.matmul(g.ps[:, 2, 0:P], wo[:, j, :], out_T[:, j, :], start=(j == 0), stop=(j == 3))
                    mm.then_inc(proj_done, 1)

                def front_turn(n):
                    reach(pe, rotated_done, n + 1)
                    reach(pe, turned5, 2 * n - 2)
                    reach(pe, turned6, 2 * n - 2)
                    for a in range(2):
                        for j in range(4):
                            mm = pe.transpose(g.ps[:, 5 + a, j * P:(j + 1) * P],
                                              rotated[:, 8 * a + 2 * j:8 * a + 2 * j + 2, :].rearrange("p h d -> p (h d)"),
                                              g.ident[:])
                    mm.then_inc(front_done, 1)

                def turn(b, t):
                    T = b * TB + t
                    qkv(T + 2, t + 2)
                    scores(b, t, 0)
                    if exists(b, t, 1):
                        turn_probs(2 * T - 1, 1)
                    if exists(b, t, 2):
                        project(T - 2)
                    if exists(b, t, 1):
                        product(2 * T - 2, (t - 1) % TB, 0)
                    scores(b, t, 1)
                    front_turn(T + 1)
                    if exists(b, t, 1):
                        product(2 * T - 1, (t - 1) % TB, 1)
                    turn_probs(2 * T, 0, fronts=T + 2)

                pe.wait_ge(loaded, 96)
                pe.wait_ge(ready, 1)
                pe.wait_ge(w_lo_done, 1)
                qkv(0, 0)
                front_turn(0)
                qkv(1, 1)
                batches(pe, turn)
                last = BATCH * TB - 1
                project(last - 1)
                turn_probs(2 * last + 1, 1)
                product(2 * last, TB - 1, 0)
                product(2 * last + 1, TB - 1, 1)
                pe.wait_ge(z_done, last)
                project(last)

            @block.scalar
            def _(act):
                def round_up(n, t):
                    reach(act, h_done, n + 1)
                    reach(act, qkv_done, n - 1)
                    act.activation(h_parts[t % 2][0][:], h_tile[t % 2][:], ACT.Copy).then_inc(h_hi_done, 1)

                def square(n):
                    reach(act, qkv_done, n + 1)
                    reach(act, sum_done, n)
                    for a in range(2):
                        act.activation(squares[:, a * INNER:(a + 1) * INNER], g.ps[:, a, :], ACT.Square).then_inc(square_done, 1)

                def take_v(n, t):
                    reach(act, qkv_done, n + 1)
                    act.activation(v_ring[:, t % TB + 1, :], g.ps[:, 2, :], ACT.Copy).then_inc(v_done, 1)

                def exps(k, s):
                    reach(act, min_done, k + 1)
                    reach(act, turn_done, k - 1)
                    reach(act, inv_sum_done, k - 1)
                    for j in range(G):
                        done = act.activation(probs[s][:, j, P - LWIN:], g.ps[:, 3 + j // 2, j % 2 * KEYS:(j % 2 + 1) * KEYS],
                                              ACT.Exp, bias=row_min[:, s, j:j + 1], scale=-1.0,
                                              accum_out=row_sum[:, s, j:j + 1])
                    done.then_inc(probs_done, 1)

                def evacuate(k, s):
                    reach(act, turn_done, k + 1)
                    reach(act, product_done, k - 1)
                    act.activation(probs_T[s][:, 1, :], g.ps[:, 6, :], ACT.Copy).then_inc(turned6, 1)

                def take_out(k, s):
                    reach(act, product_done, k + 1)
                    act.activation(flat(out_T[:, 2 * s:2 * s + 2, :]), g.ps[:, 7, 2 * s * P:2 * (s + 1) * P], ACT.Copy)\
                       .then_inc(out_done, 1)

                def take_qk(n, t):
                    reach(act, front_done, n + 1)
                    act.activation(flat(q_T[t % 2][1][LOW]), g.ps[LOW, 5, :], ACT.Copy)
                    t = t % TB + 1
                    act.activation(k_ring[:, :, t * P:(t + 1) * P], g.ps[:, 6, :].rearrange("p (j t) -> p j t", j=4), ACT.Copy)\
                       .then_inc(k_out, 1)

                def turn(b, t):
                    T = b * TB + t
                    square(T + 2)
                    take_v(T + 2, t + 2)
                    exps(2 * T, 0)
                    if exists(b, t, 1):
                        evacuate(2 * T - 1, 1)
                        take_out(2 * T - 2, 0)
                    round_up(T + 3, t + 3)
                    take_qk(T + 1, t + 1)
                    exps(2 * T + 1, 1)
                    if exists(b, t, 1):
                        take_out(2 * T - 1, 1)
                    evacuate(2 * T, 0)

                act.wait_ge(loaded, 96)
                act.activation(w_parts[0][:], w[:], ACT.Copy).then_inc(w_hi_done, 1)
                round_up(0, 0)
                round_up(1, 1)
                act.wait_ge(ready, 1)
                square(0)
                take_v(0, 0)
                take_qk(0, 0)
                square(1)
                take_v(1, 1)
                round_up(2, 2)
                batches(act, turn)
                last = BATCH * TB - 1
                evacuate(2 * last + 1, 1)
                take_out(2 * last, 0)
                take_out(2 * last + 1, 1)

            @block.vector
            def _(dve):
                def remainder(n, t):
                    reach(dve, h_hi_done, n + 1)
                    dve.tensor_tensor(h_parts[t % 2][1][:], h_tile[t % 2][:], h_parts[t % 2][0][:].bitcast(F32), ALU.subtract)\
                       .then_inc(h_lo_done, 1)

                def rotate(n, t, a):
                    reach(dve, square_done, 2 * n + 1 + a)
                    if a == 0:
                        reach(dve, pool_step, n)
                    wide = [P, 8, LDH]
                    qk = heads_of(g.ps[:, a, :])
                    dve.tensor_tensor(by_cos[:, 8 * a:8 * a + 8, :], qk, rot[:, t % TB, a, 0, :].unsqueeze(1).to_broadcast(wide), ALU.mult)
                    for h in range(2):
                        d, o = slice(32 * h, 32 * h + 32), slice(32 - 32 * h, 64 - 32 * h)
                        last = dve.tensor_tensor(by_sin[:, 8 * a:8 * a + 8, d], qk[:, :, o],
                                                 rot[:, t % TB, a, 1, d].unsqueeze(1).to_broadcast([P, 8, 32]), ALU.mult)
                    if a == 1:
                        last.then_inc(rotate_done, 1)

                def sum_squares(n):
                    reach(dve, square_done, 2 * n + 2)
                    reach(dve, inv_done, n)
                    dve.tensor_reduce(squared_norm[:], heads_of(squares[:]), AX, ALU.add).then_inc(sum_done, 1)

                def floor_norm(n):
                    reach(dve, sum_done, n + 1)
                    dve.tensor_scalar(squared_norm[:], squared_norm[:], 1e-24, None, ALU.max).then_inc(floor_done, 1)

                def mins(k, t, s):
                    reach(dve, scores_done, k + 1)
                    settle(dve, held_dve)
                    for j in range(G):
                        sc = g.ps[:, 3 + j // 2, j % 2 * KEYS:(j % 2 + 1) * KEYS]
                        last = dve.tensor_tensor_reduce(out=sc, in0=sc, in1=mask[:, min(t, 1), :], scale=1.0, scalar=3e38,
                                                        op0=ALU.add, op1=ALU.min, accum_out=row_min[:, s, j:j + 1])
                    last.then_inc(min_done, 1)

                def invert_sum(k, s):
                    reach(dve, probs_done, k + 1)
                    reach(dve, scaled_done, k - 1)
                    dve.reciprocal(inv_sum[:, s, :], row_sum[:, s, :]).then_inc(inv_sum_done, 1)

                def evacuate(k, s):
                    reach(dve, turn_done, k + 1)
                    reach(dve, product_done, k - 1)
                    dve.tensor_copy(probs_T[s][:, 0, :], g.ps[:, 5, :]).then_inc(turned5, 1)

                def take_q(n, t):
                    reach(dve, front_done, n + 1)
                    dve.tensor_copy(flat(q_T[t % 2][0][TOP]), g.ps[TOP, 5, :]).then_inc(q_out, 1)

                def add(n, b, t):
                    reach(dve, proj_done, n + 1)
                    for rows in (TOP, LOW):
                        last = dve.tensor_tensor(shifted(g.zB, rows, b, t * P, P), shifted(g.zA, rows, b, t * P, P),
                                                 g.ps[rows, 2, 0:P], ALU.add)
                    last.then_inc(z_done, 1)

                def turn(b, t):
                    T = b * TB + t
                    mins(2 * T, t, 0)
                    if exists(b, t, 1):
                        evacuate(2 * T - 1, 1)
                    rotate(T + 2, t + 2, 0)
                    if exists(b, t, 2):
                        add(T - 2, b if t >= 2 else b - 1, (t - 2) % TB)
                    invert_sum(2 * T, 0)
                    rotate(T + 2, t + 2, 1)
                    mins(2 * T + 1, t, 1)
                    take_q(T + 1, t + 1)
                    remainder(T + 3, t + 3)
                    sum_squares(T + 2)
                    floor_norm(T + 2)
                    invert_sum(2 * T + 1, 1)
                    evacuate(2 * T, 0)

                dve.wait_ge(loaded, 96)
                dve.wait_ge(w_hi_done, 1)
                dve.tensor_tensor(w_parts[1][:], w[:], w_parts[0][:].bitcast(F32), ALU.subtract).then_inc(w_lo_done, 1)
                remainder(0, 0)
                remainder(1, 1)
                dve.wait_ge(ready, 1)
                for a in range(2):
                    sc = scale_rows[:, a, :]
                    for h in range(2):
                        d, o = slice(32 * h, 32 * h + 32), slice(32 - 32 * h, 64 - 32 * h)
                        last = dve.tensor_tensor(rot[:, :, a, 1, d], rot[:, :, a, 1, d], sc[:, o].unsqueeze(1).to_broadcast([P, TB, 32]), ALU.mult)
                    last = dve.tensor_tensor(rot[:, :, a, 0, :], rot[:, :, a, 0, :], sc.unsqueeze(1).to_broadcast([P, TB, LDH]), ALU.mult)
                last.then_inc(tables, 1)
                dve.wait_ge(tables, 1)
                dve.tensor_scalar(rot[:, :, 0], rot[:, :, 0], -8.0, None, ALU.mult).then_inc(tables, 1)
                dve.wait_ge(tables, 2)
                rotate(0, 0, 0)
                rotate(0, 0, 1)
                sum_squares(0)
                floor_norm(0)
                take_q(0, 0)
                remainder(2, 2)
                rotate(1, 1, 0)
                rotate(1, 1, 1)
                sum_squares(1)
                floor_norm(1)
                batches(dve, turn)
                last = BATCH * TB - 1
                add(last - 1, BATCH - 1, TB - 2)
                evacuate(2 * last + 1, 1)
                add(last, BATCH - 1, TB - 1)


def mlp(nc, g, layer):
    stage_sems = []
    with ExitStack() as ctx:
        ctx.callback(give_back, nc, stage_sems)

        def sb(name, shape, dt=F32):
            return ctx.enter_context(nc.sbuf_tensor(f"m{layer}_{name}", shape, dt))

        def sem(name):
            return kept(nc, stage_sems, f"m{layer}_{name}")

        CHUNKS = TOKENS // BANK
        SIZES = (P, P, LHID - 2 * P)
        w1 = sb("w1", [P, 2 * LHID])
        w1_scaled = sb("w1_scaled", [P, 2 * LHID])
        w2 = sb("w2", [P, 3, DIM])
        b1 = sb("b1", [P, 2, 3])
        cols = sb("cols", [P, 3])
        mean_of = sb("mean_of", [P, P])
        centred = [sb(f"centred{n}", [P, BANK]) for n in range(2)]
        squares = sb("squares", [P, BANK])
        variance = sb("variance", [P, BANK])
        std = sb("std", [P, BANK])
        rstd = sb("rstd", [P, BANK])
        normed = [sb(f"normed{n}", [P, BANK]) for n in range(2)]
        gelu = [sb(f"gelu{n}", [P, BANK]) for n in range(2)]
        hidden = [sb(f"hidden{n}", [P, BANK]) for n in range(3)]
        loaded, ready, shift_mm, folded = sem("loaded"), sem("ready"), sem("shift_mm"), sem("folded")
        mean_done, centred_done, square_done, var_done, eps_done, std_done, rstd_done, normed_done = map(sem, (
            "mean_done", "centred_done", "square_done", "var_done", "eps_done", "std_done", "rstd_done", "normed_done"))
        up_done, gelu_done, hidden_done, down_done, z_done, held = map(sem, (
            "up_done", "gelu_done", "hidden_done", "down_done", "z_done", "held"))

        def unit_cols(k, j):
            start = k * LHID + j * P
            return slice(start, start + SIZES[j])

        def z_shifted(z, c):
            return z[:, ds(c // 2, 1), ds((c % 2) * BANK, BANK)].rearrange("p a t -> p (a t)")

        with nc.Block() as block:
            @block.sync
            def _(sp):
                for dst, src in ((w1[:], g.mw1[layer]), (w2[:], g.mw2[layer]), (b1[:], g.mb1[layer]), (cols[:], g.mcols[layer])):
                    sp.dma_start(dst, src).then_inc(loaded, 16)

            @block.gpsimd
            def _(pool):
                pool.memset(mean_of[:], 1.0 / DIM).then_inc(ready, 1)

                def norm(n, u):
                    pool.wait_ge(rstd_done, n + 1)
                    settle(pool, held)
                    if not isinstance(n, int):
                        pool.wait_ge(up_done, (n - 1) * 3)
                        settle(pool, held)
                    pool.tensor_tensor(normed[u][:], centred[u][:], rstd[:], ALU.mult).then_inc(normed_done, 1)

                norm(0, 0)
                with pool.Fori(0, CHUNKS // 2) as cc:
                    for u in range(2):
                        norm(cc * 2 + u + 1, 1 - u)

            @block.tensor
            def _(pe):
                def mean(n, c):
                    pe.wait_ge(centred_done, n + 1)
                    pe.matmul(g.ps[:, 0, :], mean_of[:], z_shifted(g.zB, c), start=True, stop=True).then_inc(mean_done, 1)

                def var(n):
                    pe.wait_ge(square_done, n + 1)
                    pe.wait_ge(eps_done, n + 1)
                    pe.matmul(g.ps[:, 1, :], mean_of[:], squares[:], start=True, stop=True).then_inc(var_done, 1)

                def up(c, u, j):
                    i = 3 * u + j
                    pe.wait_ge(normed_done, c + 1)
                    pe.wait_ge(hidden_done, c * 3 + j + 1)
                    for k in range(2):
                        mm = pe.matmul(g.ps[0:SIZES[j], 2 + 2 * k + i % 2, :], w1_scaled[:, unit_cols(k, j)], normed[u][:],
                                       start=True, stop=True)
                    mm.then_inc(up_done, 1)

                def down(c, u, j):
                    pe.wait_ge(hidden_done, c * 3 + j + 3)
                    if j == 0:
                        pe.wait_ge(z_done, c + 1)
                    pe.matmul(g.ps[:, 6 + u, :], w2[0:SIZES[j], j, :], hidden[j][0:SIZES[j], :], start=(j == 0),
                              stop=(j == 2)).then_inc(down_done, 1)

                pe.sem_inc(down_done, 3)
                pe.wait_ge(loaded, 64)
                pe.wait_ge(ready, 1)
                for k in range(2):
                    for j in range(3):
                        mm = pe.matmul(g.ps[0:SIZES[j], 7, 3 * k + j:3 * k + j + 1], w1[:, unit_cols(k, j)], cols[:, 1:2],
                                       start=True, stop=True)
                mm.then_inc(shift_mm, 1)
                pe.wait_ge(folded, 1)
                mean(0, 0)
                var(0)
                mean(1, 1)
                with pe.Fori(0, CHUNKS // 2) as cc:
                    for u in range(2):
                        c = cc * 2 + u
                        var(c + 1)
                        up(c, u, 0)
                        up(c, u, 1)
                        mean(c + 2, (c + 2) % CHUNKS)
                        down(c, u, 0)
                        up(c, u, 2)
                        down(c, u, 1)
                        down(c, u, 2)

            @block.scalar
            def _(act):
                def square(n, u):
                    act.wait_ge(centred_done, n + 2)
                    if not isinstance(n, int):
                        act.wait_ge(var_done, n)
                    act.activation(squares[:], centred[u][:], ACT.Square).then_inc(square_done, 1)

                def root(n):
                    act.wait_ge(eps_done, n + 2)
                    if not isinstance(n, int):
                        act.wait_ge(rstd_done, n)
                    act.activation(std[:], variance[:], ACT.Sqrt).then_inc(std_done, 1)

                def gate(c, u, j):
                    i = 3 * u + j
                    act.wait_ge(up_done, c * 3 + j + 1)
                    rows = slice(0, SIZES[j])
                    act.activation(gelu[i % 2][rows, :], g.ps[rows, 4 + i % 2, :], ACT.Gelu, bias=b1[rows, 1, j:j + 1])\
                       .then_inc(gelu_done, 1)

                square(0, 0)
                root(0)
                square(1, 1)
                with act.Fori(0, CHUNKS // 2) as cc:
                    for u in range(2):
                        c = cc * 2 + u
                        root(c + 1)
                        gate(c, u, 0)
                        gate(c, u, 1)
                        gate(c, u, 2)
                        square(c + 2, u)

            @block.vector
            def _(dve):
                dve.sem_inc(eps_done, 1)
                dve.sem_inc(hidden_done, 2)
                dve.sem_inc(z_done, 2)
                dve.wait_ge(loaded, 64)
                dve.tensor_scalar(w1_scaled[:], w1[:], cols[:, 0:1], None, ALU.mult)
                dve.wait_ge(shift_mm, 1)
                shifts = g.ps[:, 7, 0:6].rearrange("p (k j) -> p k j", k=2)
                last_rows = slice(0, SIZES[2])
                dve.tensor_tensor(b1[:, :, 0:2], b1[:, :, 0:2], shifts[:, :, 0:2], ALU.add)
                dve.tensor_tensor(b1[last_rows, :, 2:3], b1[last_rows, :, 2:3], shifts[last_rows, :, 2:3], ALU.add)\
                   .then_inc(folded, 1)
                dve.wait_ge(folded, 1)
                dve.sem_inc(centred_done, 1)

                def centre(n, c, u):
                    dve.wait_ge(mean_done, n + 1)
                    if not isinstance(n, int):
                        dve.wait_ge(normed_done, n - 1)
                    dve.tensor_tensor(centred[u][:], z_shifted(g.zB, c), g.ps[:, 0, :], ALU.subtract).then_inc(centred_done, 1)

                def add_eps(n):
                    dve.wait_ge(var_done, n + 1)
                    dve.tensor_scalar(variance[:], g.ps[:, 1, :], EPS, None, ALU.add).then_inc(eps_done, 1)

                def invert(n):
                    dve.wait_ge(std_done, n + 1)
                    if not isinstance(n, int):
                        dve.wait_ge(normed_done, n)
                    dve.reciprocal(rstd[:], std[:]).then_inc(rstd_done, 1)

                def multiply(c, u, j):
                    i = 3 * u + j
                    rows = slice(0, SIZES[j])
                    dve.wait_ge(gelu_done, c * 3 + j + 1)
                    dve.wait_ge(down_done, c * 3 + j + 1)
                    dve.scalar_tensor_tensor(hidden[j][rows, :], g.ps[rows, 2 + i % 2, :], b1[rows, 0, j:j + 1],
                                             gelu[i % 2][rows, :], ALU.add, ALU.mult).then_inc(hidden_done, 1)

                def add(c, u):
                    dve.wait_ge(down_done, c * 3 + 6)
                    for rows in (TOP, LOW):
                        t0 = (c % 2) * BANK
                        last = dve.scalar_tensor_tensor(shifted(g.zA, rows, c // 2, t0, BANK), g.ps[rows, 6 + u, :], cols[rows, 2:3],
                                                        shifted(g.zB, rows, c // 2, t0, BANK), ALU.add, ALU.add)
                    last.then_inc(z_done, 1)

                centre(0, 0, 0)
                add_eps(0)
                invert(0)
                centre(1, 1, 1)
                with dve.Fori(0, CHUNKS // 2) as cc:
                    for u in range(2):
                        c = cc * 2 + u
                        add_eps(c + 1)
                        multiply(c, u, 0)
                        multiply(c, u, 1)
                        centre(c + 2, (c + 2) % CHUNKS, u)
                        invert(c + 1)
                        multiply(c, u, 2)
                        add(c, u)


def clear_first_token(nc, g):
    with nc.Block() as block:
        @block.gpsimd
        def _(pool):
            for z in (g.zA, g.zB):
                pool.memset(z[LOW, :, 0:1], 0.0)


def finish(nc, g):
    stage_sems = []
    with ExitStack() as ctx:
        ctx.callback(give_back, nc, stage_sems)

        def sem(name):
            return kept(nc, stage_sems, "f_" + name)

        gated = [ctx.enter_context(nc.sbuf_tensor(f"f_gated{n}", [P, 4, DIM], F32)) for n in range(2)]
        turned, scaled, added, stored = map(sem, ("turned", "scaled", "added", "stored"))
        CHUNKS = TOKENS // BANK
        with nc.Block() as block:
            @block.tensor
            def _(pe):
                for c in range(CHUNKS):
                    if c >= 4:
                        pe.wait_ge(scaled, c - 3)
                    for t in range(4):
                        b, t0 = c // 2, (c % 2) * BANK + t * P
                        for n, (rows, lag) in enumerate(((TOP, 0), (LOW, 1))):
                            mm = pe.transpose(g.ps[:, 2 * (c % 4) + n, t * 64:t * 64 + 64],
                                              g.zA[rows, b, t0 + lag:t0 + lag + P], g.ident[rows, rows])
                    mm.then_inc(turned, 1)

            @block.vector
            def _(dve):
                for c in range(CHUNKS):
                    dve.wait_ge(turned, c + 1)
                    for n, feats in enumerate((TOP, LOW)):
                        last = dve.tensor_tensor(gated[c % 2][:, :, feats], g.ps[:, 2 * (c % 4) + n, 0:256].rearrange("p (t d) -> p t d", t=4),
                                                 g.gate_rows[:, 1, 1, c // 2:c // 2 + 1, feats].to_broadcast([P, 4, 64]), ALU.mult)
                    last.then_inc(scaled, 1)
                    dve.wait_ge(scaled, c + 1)
                    rowsx = g.x[:, 4 * c:4 * c + 4, :]
                    dve.tensor_tensor(rowsx, rowsx, gated[c % 2][:], ALU.add).then_inc(added, 1)

            @block.sync
            def _(sp):
                for c in range(CHUNKS):
                    sp.wait_ge(added, c + 1)
                    sp.dma_start(g.out[c // 2, :, 4 * (c % 2):4 * (c % 2) + 4, :], g.x[:, 4 * c:4 * c + 4, :]).then_inc(stored, 16)
                sp.wait_ge(stored, 16 * CHUNKS)


def program(nc, g, stages=("l0a", "l0f", "l1a", "l1f")):
    with ExitStack() as ctx:
        allocate(nc, ctx, g)
        g.qk_dram = nc.dram_tensor("qk_dram", [3, 2, P, TOKENS], BF16, kind="Internal").ap()
        g.bias_dram_t = nc.dram_tensor("bias_dram", [HEADS, 384], F32, kind="Internal")
        g.bias_dram = g.bias_dram_t.ap()

        g.toeplitz_src = bass.AP(g.bias_dram_t, 0, [[1, P], [384, HEADS], [1, 2 * P]])
        with ExitStack() as first:
            g.toeplitz_all = first.enter_context(nc.sbuf_tensor("toeplitz_all", [P, HEADS, 2 * P], F32))
            g.ga_bo = first.enter_context(nc.sbuf_tensor("ga_bo", [P, BATCH, DIM], F32))
            g.v_all = first.enter_context(nc.sbuf_tensor("v_all", [P, TILES, DIM], F32))
            setup(nc, g)
            if "l0a" in stages:
                norm_modulate(nc, g, 0, 0, add_ga_bo=True)
                split_project(nc, g)
                attention(nc, g, 0)
        if "l0f" in stages:
            norm_modulate(nc, g, 0, 1)
            experts(nc, g)
        if "l1a" in stages:
            norm_modulate(nc, g, 1, 0)
            attention(nc, g, 1)
        if "l1f" in stages:
            g.zA = ctx.enter_context(nc.sbuf_tensor("zA", [P, BATCH, SEQ + 1], F32))
            g.zB = ctx.enter_context(nc.sbuf_tensor("zB", [P, BATCH, SEQ + 1], F32))
            clear_first_token(nc, g)
            norm_modulate(nc, g, 1, 1, shift=True)
            for layer in range(LDEPTH):
                local_attention(nc, g, layer)
                mlp(nc, g, layer)
            finish(nc, g)
        else:
            store(nc, g)


def store(nc, g):
    stored = nc.alloc_semaphore("stored")
    with nc.Block() as block:
        @block.sync
        def _(sp):
            for b in range(BATCH):
                sp.dma_start(g.out[b], g.x[:, b * TB:(b + 1) * TB, :]).then_inc(stored, 16)
            sp.wait_ge(stored, 16 * BATCH)


def lay_out(inputs):
    f = {k: np.ascontiguousarray(v) for k, v in inputs.items()}
    a = {}
    a["x_in"] = f["L0_attn_x"].reshape(BATCH, TB, P, DIM).transpose(0, 2, 1, 3)
    a["cT"] = np.stack([f["L0_c"].T, f["L1_c"].T], 1)
    a["wmod"] = np.stack([f["L0_wmod"], f["L1_wmod"]], 1)
    a["bo"] = f["L0_attn_bo"]
    a["rel_emb"] = f["L0_attn_rel_emb"]
    a["ident_in"] = np.eye(P, dtype=np.float32)
    a["flip_in"] = np.eye(P, dtype=np.float32)[::-1]
    a["bias_sel"] = bias_selector()
    a["w0_qkv"] = np.stack([f["L0_attn_Wq"], f["L0_attn_Wk"], f["L0_attn_Wv"]], 1)
    a["w0_out"] = f["L0_attn_Wo"]
    a["w1_qk"] = np.stack([f["L1_attn_Wq"], f["L1_attn_Wk"]])
    def hidden_first(w):
        return w.transpose(2, 0, 1)

    a["w1"] = hidden_first(f["L0_ffn_W1"])
    a["w3"] = hidden_first(f["L0_ffn_W3"])
    a["w2"] = f["L0_ffn_W2"].transpose(2, 0, 1).reshape(2, P, EXPERTS, DIM).transpose(1, 2, 0, 3)
    a["lora_a"] = np.stack([f["L0_ffn_A1"], f["L0_ffn_A3"]]).transpose(2, 0, 1, 3)
    a["lora_b"] = np.stack([f["L0_ffn_B1"], f["L0_ffn_B3"]]).transpose(3, 0, 1, 2)
    a["lora_a2"] = f["L0_ffn_A2"].transpose(1, 0, 2)
    a["lora_b2"] = f["L0_ffn_B2"].transpose(2, 0, 1)
    a["w_gate"] = f["L0_ffn_Wg"].T
    a["iota"] = np.tile(np.arange(EXPERTS, dtype=np.float32), (P, 1))
    a["b13"] = np.stack([f["L0_ffn_b1"], f["L0_ffn_b3"]]).reshape(2, EXPERTS, 2, P).transpose(3, 0, 1, 2)
    a["b2"] = f["L0_ffn_b2"]
    a["wqkv"] = f["L1_ffn_wqkv"]
    a["wo"] = f["L1_ffn_wo"].reshape(LDEPTH, 4, P, DIM).transpose(0, 2, 1, 3)
    a["q_scale"], a["k_scale"] = f["L1_ffn_q_scale"], f["L1_ffn_k_scale"]
    a["rotary"] = rotary_tables().reshape(2, 2, TB, P, LDH).transpose(3, 2, 0, 1, 4)
    band = band_mask()[:, 64:]
    no_past = band.copy()
    no_past[:, :64] = BIG
    a["band"] = np.stack([no_past, band], 1)
    a["mw1"] = f["L1_ffn_w1"]
    def hidden_tiles(w):
        out = np.zeros((w.shape[0], 3 * P, w.shape[2]), w.dtype)
        out[:, :LHID] = w
        return out.reshape(w.shape[0], 3, P, w.shape[2]).transpose(0, 2, 1, 3)

    a["mw2"] = hidden_tiles(f["L1_ffn_w2"])
    a["mb1"] = hidden_tiles(f["L1_ffn_b1"].reshape(LDEPTH, 2, LHID).transpose(0, 2, 1)).transpose(0, 1, 3, 2)
    a["mcols"] = np.stack([f["L1_ffn_ln_g"], f["L1_ffn_ln_b"], f["L1_ffn_b2"]], -1)
    a["w1_v"] = f["L1_attn_Wv"]
    a["w1_out"] = f["L1_attn_Wr"]
    return {k: np.ascontiguousarray(v) for k, v in a.items()}


_OUT = (BATCH, P, TB, DIM)


def kernel(**inputs):
    import numpy as _np
    import concourse.bacc as _bacc
    from concourse import mybir as _mybir
    from concourse.bass_utils import run_bass_kernel_spmd as _run

    nc = _bacc.Bacc("TRN2", target_bir_lowering=False, num_devices=1)
    arrays = lay_out(inputs)
    chip = Chip()
    fed = {}
    for name, a in arrays.items():
        fed[f"in_{name}"] = a
        chip.__dict__[name] = nc.dram_tensor(f"in_{name}", a.shape, _mybir.dt.from_np(a.dtype), kind="ExternalInput").ap()
    chip.out = nc.dram_tensor("out_0_dram", _OUT, _mybir.dt.float32, kind="ExternalOutput").ap()
    program(nc, chip)
    r = _run(nc, [fed], core_ids=[0])
    got = r.results[0]["out_0_dram"]
    return _np.ascontiguousarray(got.reshape(_OUT).transpose(0, 2, 1, 3).reshape(BATCH, SEQ, DIM))
```
